# Optimizing a Trainium2 kernel written in Bass

```python
import numpy as np
import jax
import jax.numpy as jnp

def _softmax(x, axis=-1):
    return jax.nn.softmax(x, axis=axis)

def _gelu(x):
    return jax.nn.gelu(x, approximate=True)

def _silu(x):
    return jax.nn.silu(x)

def _sigmoid(x):
    return jax.nn.sigmoid(x)

def _layernorm(x, axis=-1, eps=1e-05):
    m = jnp.mean(x, axis=axis, keepdims=True)
    v = jnp.var(x, axis=axis, keepdims=True)
    return (x - m) / jnp.sqrt(v + eps)

def _scatter_add(tgt, idx, src, axis=0):
    return tgt.at[idx].add(src)

def _segment_sum(src, seg, n):
    return jax.ops.segment_sum(src, seg, n)
kernel_name = 'mk_perceiver_d1_seqx_r2_267219'

def setup_inputs(seed: int=0):
    np.random.seed(seed)
    _w = jnp.asarray

    def _rec_inputs():
        import jax
        import jax.numpy as jnp
        _rk = jax.random.key(seed)
        x = 7.22e-05 + 1 * jax.random.normal(jax.random.fold_in(_rk, 1), (2, 512, 512), jnp.float32)
        _lenS = 512 - jax.random.randint(jax.random.fold_in(_rk, 7), (2,), 0, max(1, 512 // 4) + 1, jnp.int32)
        _lenS2 = 8192 - jax.random.randint(jax.random.fold_in(_rk, 8), (2,), 0, max(1, 8192 // 4) + 1, jnp.int32)
        _ctx_1024P = jax.random.normal(jax.random.fold_in(_rk, 11), (2, 16, 512), jnp.float32)
        _ctx_1024c = jax.random.dirichlet(jax.random.fold_in(_rk, 511), 0.3 * jnp.ones((16,), jnp.float32), (2, 8192))
        _ctx_1024t = jnp.einsum('bsk,bkd->bsd', _ctx_1024c, _ctx_1024P)
        _ctx_1024t = _ctx_1024t * jax.lax.rsqrt(jnp.mean(jnp.square(_ctx_1024t)) + 1e-12) * 0.953939
        ctx_1024 = 4.13588e-05 + 0.999923 * (_ctx_1024t + 0.3 * jax.random.normal(jax.random.fold_in(_rk, 611), (2, 8192, 512), jnp.float32))
        return (x, ctx_1024)
    x, ctx_1024 = _rec_inputs()

    def _L0_xattn_setup():
        import jax, jax.numpy as jnp
        import numpy as np
        D_MODEL = 512
        NUM_HEADS = 16
        HEAD_DIM = D_MODEL // NUM_HEADS
        B, T = (4, 1024)
        key = jax.random.key(seed)
        ks = jax.random.split(key, 6)
        s = 1.0 / np.sqrt(D_MODEL)
        return {'x_q': jax.random.normal(ks[0], (B, T, D_MODEL), jnp.float32), 'x_kv': jax.random.normal(ks[1], (B, T, D_MODEL), jnp.float32), 'Wq': jax.random.uniform(ks[2], (D_MODEL, D_MODEL), jnp.float32, -s, s), 'Wk': jax.random.uniform(ks[3], (D_MODEL, D_MODEL), jnp.float32, -s, s), 'Wv': jax.random.uniform(ks[4], (D_MODEL, D_MODEL), jnp.float32, -s, s), 'Wo': jax.random.uniform(ks[5], (D_MODEL, D_MODEL), jnp.float32, -s, s)}
    _L0_xattn_all = _L0_xattn_setup()
    _L0_xattn_in = {k: v for k, v in _L0_xattn_all.items() if k in ('Wq', 'Wk', 'Wv', 'Wo')}
    del _L0_xattn_all

    def _L0_attn_setup():
        import jax, jax.numpy as jnp
        import numpy as np
        D_MODEL, D_INNER, D_STATE, D_CONV, DT_RANK, D_FF = (512, 1024, 16, 4, 64, 2048)
        EPS = 1e-06
        B, L = (1, 1024)

        def rmsnorm(x, w):
            return x * jax.lax.rsqrt(jnp.mean(x * x, axis=-1, keepdims=True) + EPS) * w

        def ste(x, q):
            return x + jax.lax.stop_gradient(q - x)

        def bitlinear(x, w, b):
            g = jnp.maximum(jnp.mean(jnp.abs(w)), 1e-05)
            wq = ste(w, jnp.clip(jnp.round(w / g), -1.0, 1.0) * g)
            s = 127.0 / jnp.maximum(jnp.max(jnp.abs(x), axis=-1, keepdims=True), 1e-05)
            xq = ste(x, jnp.clip(jnp.round(x * s), -128.0, 127.0) / s)
            return xq @ wq.T + b

        def mamba(x, w_in, conv_w, conv_b, w_xproj, w_dt, b_dt, A_log, Dp, w_out):
            b, l, _ = x.shape
            xz = x @ w_in.T
            u, z = (xz[..., :D_INNER], xz[..., D_INNER:])
            uc = jax.lax.conv_general_dilated(u.transpose(0, 2, 1), conv_w, (1,), [(D_CONV - 1, 0)], feature_group_count=D_INNER, dimension_numbers=('NCH', 'OIH', 'NCH'))
            u = jax.nn.silu((uc + conv_b[None, :, None]).transpose(0, 2, 1))
            dbl = u @ w_xproj.T
            dt = dbl[..., :DT_RANK]
            Bm = dbl[..., DT_RANK:DT_RANK + D_STATE]
            Cm = dbl[..., DT_RANK + D_STATE:]
            delta = jax.nn.softplus(dt @ w_dt.T + b_dt)
            A = -jnp.exp(A_log)
            dA = jnp.exp(jnp.einsum('bld,dn->bldn', delta, A))
            dBu = jnp.einsum('bld,bln->bldn', delta * u, Bm)

            def step(h, t):
                dA_t, dBu_t, C_t = t
                h = dA_t * h + dBu_t
                y = jnp.einsum('bdn,bn->bd', h, C_t)
                return (h, y)
            h0 = jnp.zeros((b, D_INNER, D_STATE), x.dtype)
            _, ys = jax.lax.scan(step, h0, (dA.transpose(1, 0, 2, 3), dBu.transpose(1, 0, 2, 3), Cm.transpose(1, 0, 2)))
            y = ys.transpose(1, 0, 2) + u * Dp
            y = y * jax.nn.silu(z)
            return y @ w_out.T
        key = jax.random.key(seed)
        ks = jax.random.split(key, 12)
        f = jnp.float32
        return {'x': jax.random.normal(ks[0], (B, L, D_MODEL), f), 'w_in': jax.random.normal(ks[1], (2 * D_INNER, D_MODEL), f) * 0.02, 'conv_w': jax.random.normal(ks[2], (D_INNER, 1, D_CONV), f) * 0.1, 'conv_b': jnp.zeros((D_INNER,), f), 'w_xproj': jax.random.normal(ks[3], (DT_RANK + 2 * D_STATE, D_INNER), f) * 0.02, 'w_dt': jax.random.normal(ks[4], (D_INNER, DT_RANK), f) * 0.02, 'b_dt': jax.random.uniform(ks[5], (D_INNER,), f, -4.0, -2.0), 'A_log': jnp.log(jnp.tile(jnp.arange(1, D_STATE + 1, dtype=f), (D_INNER, 1))), 'Dp': jnp.ones((D_INNER,), f), 'w_out': jax.random.normal(ks[6], (D_MODEL, D_INNER), f) * 0.02, 'norm1_w': jnp.ones((D_MODEL,), f), 'norm2_w': jnp.ones((D_MODEL,), f), 'ffn_w1': jax.random.normal(ks[7], (D_FF, D_MODEL), f) * 0.02, 'ffn_b1': jnp.zeros((D_FF,), f), 'ffn_w2': jax.random.normal(ks[8], (D_MODEL, D_FF), f) * 0.02, 'ffn_b2': jnp.zeros((D_MODEL,), f)}
    _L0_attn_all = _L0_attn_setup()
    _L0_attn_in = {k: v for k, v in _L0_attn_all.items() if k in ('w_in', 'conv_w', 'conv_b', 'w_xproj', 'w_dt', 'b_dt', 'A_log', 'Dp', 'w_out', 'norm1_w', 'norm2_w', 'ffn_w1', 'ffn_b1', 'ffn_w2', 'ffn_b2')}
    del _L0_attn_all

    def _L0_ffn_setup():
        import jax, jax.numpy as jnp
        import numpy as np
        E = 16
        K = 4
        NG = 4
        TG = 2
        SCALE = 2.5
        NORM_TOPK = True
        H = 512
        I = 256
        SH_I = I * 2
        B, S = (2, 1024)
        key = jax.random.key(seed)
        ks = jax.random.split(key, 9)

        def w(k, shape, fan_in):
            return jax.random.normal(k, shape, jnp.float32) * (1.0 / np.sqrt(fan_in))
        return {'hidden_states': jax.random.normal(ks[0], (B, S, H), jnp.float32), 'gate_w': w(ks[1], (E, H), H), 'gate_bias': jnp.zeros((E,), jnp.float32), 'Wg': w(ks[2], (E, I, H), H), 'Wu': w(ks[3], (E, I, H), H), 'Wd': w(ks[4], (E, H, I), I), 'Ws_g': w(ks[5], (SH_I, H), H), 'Ws_u': w(ks[6], (SH_I, H), H), 'Ws_d': w(ks[7], (H, SH_I), SH_I)}
    _L0_ffn_all = _L0_ffn_setup()
    _L0_ffn_in = {k: v for k, v in _L0_ffn_all.items() if k in ('gate_w', 'gate_bias', 'Wg', 'Wu', 'Wd', 'Ws_g', 'Ws_u', 'Ws_d')}
    del _L0_ffn_all
    return {'x': x, 'ctx_1024': ctx_1024, 'L0_xattn_Wq': _L0_xattn_in['Wq'], 'L0_xattn_Wk': _L0_xattn_in['Wk'], 'L0_xattn_Wv': _L0_xattn_in['Wv'], 'L0_xattn_Wo': _L0_xattn_in['Wo'], 'L0_attn_w_in': _L0_attn_in['w_in'], 'L0_attn_conv_w': _L0_attn_in['conv_w'], 'L0_attn_conv_b': _L0_attn_in['conv_b'], 'L0_attn_w_xproj': _L0_attn_in['w_xproj'], 'L0_attn_w_dt': _L0_attn_in['w_dt'], 'L0_attn_b_dt': _L0_attn_in['b_dt'], 'L0_attn_A_log': _L0_attn_in['A_log'], 'L0_attn_Dp': _L0_attn_in['Dp'], 'L0_attn_w_out': _L0_attn_in['w_out'], 'L0_attn_norm1_w': _L0_attn_in['norm1_w'], 'L0_attn_norm2_w': _L0_attn_in['norm2_w'], 'L0_attn_ffn_w1': _L0_attn_in['ffn_w1'], 'L0_attn_ffn_b1': _L0_attn_in['ffn_b1'], 'L0_attn_ffn_w2': _L0_attn_in['ffn_w2'], 'L0_attn_ffn_b2': _L0_attn_in['ffn_b2'], 'L0_ffn_gate_w': _L0_ffn_in['gate_w'], 'L0_ffn_gate_bias': _L0_ffn_in['gate_bias'], 'L0_ffn_Wg': _L0_ffn_in['Wg'], 'L0_ffn_Wu': _L0_ffn_in['Wu'], 'L0_ffn_Wd': _L0_ffn_in['Wd'], 'L0_ffn_Ws_g': _L0_ffn_in['Ws_g'], 'L0_ffn_Ws_u': _L0_ffn_in['Ws_u'], 'L0_ffn_Ws_d': _L0_ffn_in['Ws_d']}

def reference(x, ctx_1024, L0_xattn_Wq, L0_xattn_Wk, L0_xattn_Wv, L0_xattn_Wo, L0_attn_w_in, L0_attn_conv_w, L0_attn_conv_b, L0_attn_w_xproj, L0_attn_w_dt, L0_attn_b_dt, L0_attn_A_log, L0_attn_Dp, L0_attn_w_out, L0_attn_norm1_w, L0_attn_norm2_w, L0_attn_ffn_w1, L0_attn_ffn_b1, L0_attn_ffn_w2, L0_attn_ffn_b2, L0_ffn_gate_w, L0_ffn_gate_bias, L0_ffn_Wg, L0_ffn_Wu, L0_ffn_Wd, L0_ffn_Ws_g, L0_ffn_Ws_u, L0_ffn_Ws_d):
    import jax
    import jax.numpy as jnp

    def _L0_xattn_ref(x_q, x_kv, Wq, Wk, Wv, Wo):
        import jax, jax.numpy as jnp
        import numpy as np
        D_MODEL = 512
        NUM_HEADS = 16
        HEAD_DIM = D_MODEL // NUM_HEADS
        B, T = (4, 1024)
        Bq, Tq, C = x_q.shape
        Tk = x_kv.shape[1]
        q = (x_q @ Wq.T).reshape(Bq, Tq, NUM_HEADS, HEAD_DIM).transpose(0, 2, 1, 3)
        k = (x_kv @ Wk.T).reshape(Bq, Tk, NUM_HEADS, HEAD_DIM).transpose(0, 2, 1, 3)
        v = (x_kv @ Wv.T).reshape(Bq, Tk, NUM_HEADS, HEAD_DIM).transpose(0, 2, 1, 3)
        scores = jnp.einsum('bhqd,bhkd->bhqk', q, k) / jnp.sqrt(jnp.asarray(HEAD_DIM, x_q.dtype))
        causal = jnp.triu(jnp.ones((Tq, Tk), bool), k=1)
        scores = jnp.where(causal, -jnp.inf, scores)
        attn = jax.nn.softmax(scores, axis=-1)
        out = jnp.einsum('bhqk,bhkd->bhqd', attn, v)
        out = out.transpose(0, 2, 1, 3).reshape(Bq, Tq, C)
        return out @ Wo.T

    def _L0_attn_ref(x, w_in, conv_w, conv_b, w_xproj, w_dt, b_dt, A_log, Dp, w_out, norm1_w, norm2_w, ffn_w1, ffn_b1, ffn_w2, ffn_b2):
        import jax, jax.numpy as jnp
        import numpy as np
        D_MODEL, D_INNER, D_STATE, D_CONV, DT_RANK, D_FF = (512, 1024, 16, 4, 64, 2048)
        EPS = 1e-06
        B, L = (1, 1024)

        def rmsnorm(x, w):
            return x * jax.lax.rsqrt(jnp.mean(x * x, axis=-1, keepdims=True) + EPS) * w

        def ste(x, q):
            return x + jax.lax.stop_gradient(q - x)

        def bitlinear(x, w, b):
            g = jnp.maximum(jnp.mean(jnp.abs(w)), 1e-05)
            wq = ste(w, jnp.clip(jnp.round(w / g), -1.0, 1.0) * g)
            s = 127.0 / jnp.maximum(jnp.max(jnp.abs(x), axis=-1, keepdims=True), 1e-05)
            xq = ste(x, jnp.clip(jnp.round(x * s), -128.0, 127.0) / s)
            return xq @ wq.T + b

        def mamba(x, w_in, conv_w, conv_b, w_xproj, w_dt, b_dt, A_log, Dp, w_out):
            b, l, _ = x.shape
            xz = x @ w_in.T
            u, z = (xz[..., :D_INNER], xz[..., D_INNER:])
            uc = jax.lax.conv_general_dilated(u.transpose(0, 2, 1), conv_w, (1,), [(D_CONV - 1, 0)], feature_group_count=D_INNER, dimension_numbers=('NCH', 'OIH', 'NCH'))
            u = jax.nn.silu((uc + conv_b[None, :, None]).transpose(0, 2, 1))
            dbl = u @ w_xproj.T
            dt = dbl[..., :DT_RANK]
            Bm = dbl[..., DT_RANK:DT_RANK + D_STATE]
            Cm = dbl[..., DT_RANK + D_STATE:]
            delta = jax.nn.softplus(dt @ w_dt.T + b_dt)
            A = -jnp.exp(A_log)
            dA = jnp.exp(jnp.einsum('bld,dn->bldn', delta, A))
            dBu = jnp.einsum('bld,bln->bldn', delta * u, Bm)

            def step(h, t):
                dA_t, dBu_t, C_t = t
                h = dA_t * h + dBu_t
                y = jnp.einsum('bdn,bn->bd', h, C_t)
                return (h, y)
            h0 = jnp.zeros((b, D_INNER, D_STATE), x.dtype)
            _, ys = jax.lax.scan(step, h0, (dA.transpose(1, 0, 2, 3), dBu.transpose(1, 0, 2, 3), Cm.transpose(1, 0, 2)))
            y = ys.transpose(1, 0, 2) + u * Dp
            y = y * jax.nn.silu(z)
            return y @ w_out.T
        h = mamba(x, w_in, conv_w, conv_b, w_xproj, w_dt, b_dt, A_log, Dp, w_out)
        x1 = rmsnorm(x + h, norm1_w)
        f = bitlinear(x1, ffn_w1, ffn_b1)
        f = jax.nn.gelu(f)
        f = bitlinear(f, ffn_w2, ffn_b2)
        return rmsnorm(x1 + f, norm2_w)

    def _L0_ffn_ref(hidden_states, gate_w, gate_bias, Wg, Wu, Wd, Ws_g, Ws_u, Ws_d):
        import jax, jax.numpy as jnp
        import numpy as np
        E = 16
        K = 4
        NG = 4
        TG = 2
        SCALE = 2.5
        NORM_TOPK = True
        H = 512
        I = 256
        SH_I = I * 2
        B, S = (2, 1024)
        x = hidden_states
        b, s, h = x.shape
        n = b * s
        xf = x.reshape(n, h)
        logits = xf @ gate_w.T
        scores = jax.nn.sigmoid(logits)
        sfc = scores + gate_bias
        epg = E // NG
        grp = sfc.reshape(n, NG, epg)
        g_scores = jax.lax.top_k(grp, 2)[0].sum(-1)
        _, gidx = jax.lax.top_k(g_scores, TG)
        gmask = jax.nn.one_hot(gidx, NG, dtype=sfc.dtype).sum(1)
        emask = jnp.repeat(gmask, epg, axis=1)
        masked = jnp.where(emask > 0, sfc, -jnp.inf)
        _, topk_idx = jax.lax.top_k(masked, K)
        topk_w = jnp.take_along_axis(scores, topk_idx, axis=1)
        if K > 1 and NORM_TOPK:
            topk_w = topk_w / (topk_w.sum(-1, keepdims=True) + 1e-20)
        topk_w = topk_w * SCALE
        cw = (jax.nn.one_hot(topk_idx, E, dtype=topk_w.dtype) * topk_w[..., None]).sum(1)
        hg = jnp.einsum('nh,eih->nei', xf, Wg)
        hu = jnp.einsum('nh,eih->nei', xf, Wu)
        act = jax.nn.silu(hg) * hu
        y = jnp.einsum('nei,ne,ehi->nh', act, cw, Wd)
        shared = jax.nn.silu(xf @ Ws_g.T) * (xf @ Ws_u.T) @ Ws_d.T
        y = y + shared
        return (x + y.reshape(b, s, h)).astype(hidden_states.dtype)
    x = x + _L0_xattn_ref(_layernorm(x, axis=-1), ctx_1024, L0_xattn_Wq, L0_xattn_Wk, L0_xattn_Wv, L0_xattn_Wo)
    x = x + _L0_attn_ref(_layernorm(x, axis=-1), L0_attn_w_in, L0_attn_conv_w, L0_attn_conv_b, L0_attn_w_xproj, L0_attn_w_dt, L0_attn_b_dt, L0_attn_A_log, L0_attn_Dp, L0_attn_w_out, L0_attn_norm1_w, L0_attn_norm2_w, L0_attn_ffn_w1, L0_attn_ffn_b1, L0_attn_ffn_w2, L0_attn_ffn_b2)
    x = x + _L0_ffn_ref(_layernorm(x, axis=-1), L0_ffn_gate_w, L0_ffn_gate_bias, L0_ffn_Wg, L0_ffn_Wu, L0_ffn_Wd, L0_ffn_Ws_g, L0_ffn_Ws_u, L0_ffn_Ws_d)
    return x

_drawn_inputs = setup_inputs


def setup_inputs(seed=0):
    import zlib

    import numpy as np

    out = dict(_drawn_inputs(seed))
    spreads = {'L0_attn_conv_b': (0.0, 0.437),
     'L0_attn_Dp': (1.0, 0.6),
     'L0_attn_norm1_w': (1.0, 0.2),
     'L0_attn_norm2_w': (1.0, 0.2),
     'L0_attn_ffn_b1': (0.0, 0.1),
     'L0_attn_ffn_b2': (0.0, 0.1),
     'L0_ffn_gate_bias': (0.0, 0.1)}
    factors = {'L0_attn_w_in': 3.324,
     'L0_attn_conv_w': 3.384,
     'L0_attn_w_xproj': 8.0,
     'L0_attn_w_dt': 8.0,
     'L0_attn_b_dt': 8.0,
     'L0_attn_A_log': 8.0,
     'L0_attn_w_out': 3.206}
    for name, (base, spread) in spreads.items():
        noise = np.random.default_rng([zlib.crc32(name.encode()), seed]).standard_normal(out[name].shape)
        drawn = base * np.exp(spread * noise) if base else spread * noise
        out[name] = jnp.asarray(drawn.astype(out[name].dtype))
    for name, factor in factors.items():
        out[name] = (out[name] * factor).astype(out[name].dtype)
    return out
```

```python
import concourse.bass as bass
from concourse import mybir
from contextlib import ExitStack

F32 = mybir.dt.float32
F32R = mybir.dt.float32r
BF16 = mybir.dt.bfloat16
ALU = mybir.AluOpType
ACT = mybir.ActivationFunctionType
AX = mybir.AxisListType

P = 128
BATCH, SEQ, D = 2, 512, 512
TT = SEQ // P
NT = BATCH * TT
KD = D // P
HEADS, HD = 16, 32
HG = HEADS // 4
DI, NS, DR = 1024, 16, 64
GI = DI // P
FF = 2048
E, EI = 16, 256
EALL = E + 2
LN_EPS, RMS_EPS = 1e-5, 1e-6
ROUND = 12582912.0
BIG = 1e30


def mm3(pe, out, lhs_hi, lhs_lo, rhs_hi, rhs_lo, start, stop):
    pe.matmul(out, lhs_hi, rhs_hi, start=start, stop=False)
    pe.matmul(out, lhs_hi, rhs_lo, start=False, stop=False)
    return pe.matmul(out, lhs_lo, rhs_hi, start=False, stop=stop)


def bc_free(ap, n):
    return ap.unsqueeze(2).to_broadcast([ap.shape[0], ap.shape[1], n])


def bc_mid(ap, n):
    return ap.unsqueeze(1).to_broadcast([ap.shape[0], n, ap.shape[1]])


def hold(eng, sem, value, passed):
    eng.wait_ge(sem, value)
    eng.sem_inc(passed, 1)


def constants(nc, sb, sem, c):
    c["ident"] = sb("ident", [P, P], F32)
    c["ident_r"] = sb("ident_r", [P, P], F32R)
    c["ident_b"] = sb("ident_b", [P, P], BF16)
    c["mask"] = sb("mask", [P, P], F32)
    c["minus_half"] = sb("minus_half", [P, 8], F32)
    c["ones"] = sb("ones", [P, P], F32)
    set_done = sem("constants_set")
    made = sem("constants_made")
    with nc.Block() as block:
        @block.gpsimd
        def _(pool):
            pool.memset(c["ident"][:], 0.0).then_inc(set_done, 1)
            pool.memset(c["mask"][:], 0.0).then_inc(set_done, 1)
            pool.memset(c["minus_half"][:], -0.5).then_inc(made, 1)
            pool.memset(c["ones"][:], 1.0).then_inc(made, 1)
            pool.wait_ge(set_done, 2)
            pool.affine_select(out=c["ident"][:], in_=c["ident"][:], compare_op=ALU.not_equal, fill=1.0,
                               base=0, pattern=[[-1, P]], channel_multiplier=1).then_inc(set_done, 1)
            pool.affine_select(out=c["mask"][:], in_=c["mask"][:], compare_op=ALU.is_ge, fill=-BIG,
                               base=0, pattern=[[-1, P]], channel_multiplier=1).then_inc(made, 1)
            pool.wait_ge(set_done, 3)
            pool.tensor_copy(c["ident_r"][:], c["ident"][:]).then_inc(made, 1)
            pool.tensor_copy(c["ident_b"][:], c["ident"][:]).then_inc(made, 1)
            pool.wait_ge(made, 5)


def attention(nc, sem, c, xres, banks, a, load_x):
    scale = float(HD) ** -0.5
    U = TT * HEADS
    STEPS = U + 8
    ctx = ExitStack()
    with ctx:
        def sb(name, shape, dt):
            return ctx.enter_context(nc.sbuf_tensor(name, shape, dt))
        stage = sb("a_stage", [P, 2, KD, D], F32)
        w_hi = sb("w_hi", [P, 4, KD, D], F32R)
        w_lo = sb("w_lo", [P, 4, KD, D], F32R)
        c_hi = sb("c_hi", [P, KD, SEQ], F32R)
        c_lo = sb("c_lo", [P, KD, SEQ], F32R)
        stats = sb("stats", [P, TT, 6], F32)
        mv = sb("mv", [P, TT, 2], F32)
        rstd = sb("rstd", [P, TT], F32)
        rows = sb("rows", [P, TT, D], F32)
        xT_hi = sb("xT_hi", [P, KD, SEQ], F32R)
        xT_lo = sb("xT_lo", [P, KD, SEQ], F32R)
        q_pad = sb("q_pad", [P, HEADS, SEQ], F32)
        kT = sb("kT", [P, KD, SEQ], F32)
        v = sb("v", [P, TT, D], F32)
        probs = sb("probs", [P, 4, SEQ], F32)
        probsT = sb("probsT", [P, 2, TT, P], F32)
        mask = sb("a_mask", [P, SEQ], F32)
        neg_max = sb("neg_max", [P, 4], F32)
        row_sum = sb("row_sum", [P, 4], F32)
        inv_sum = sb("inv_sum", [P, 4], F32)
        oT_hi = sb("oT_hi", [P, KD, P], F32R)
        oT_lo = sb("oT_lo", [P, KD, P], F32R)

        passed = sem("passed")
        x_loaded = sem("x_loaded")
        staged = [sem("staged0"), sem("staged1")]
        hi_done = sem("a_hi_done")
        cut = sem("a_cut")
        mask_done = sem("a_mask_done")
        zeroed = sem("q_zeroed")
        stats_done = sem("a_stats")
        mv_done = sem("a_mv")
        rstd_done = sem("a_rstd")
        xn_done = sem("a_xn")
        xT_psum = sem("a_xT_psum")
        xT_hi_done = sem("a_xT_hi")
        xT_lo_done = sem("a_xT_lo")
        proj_psum = sem("proj_psum")
        proj_act = sem("proj_act")
        proj_dve = sem("proj_dve")
        scores = sem("scores")
        max_done = sem("max_done")
        exp_done = sem("exp_done")
        inv_done = sem("inv_done")
        norm_done = sem("norm_done")
        pT_psum = sem("pT_psum")
        pT_act = sem("pT_act")
        pT_dve = sem("pT_dve")
        pv_done = sem("pv_done")
        oT_hi_done = sem("oT_hi_done")
        oT_lo_done = sem("oT_lo_done")
        y_psum = sem("y_psum")
        y_added = sem("y_added")

        ITEMS = ("wq", "ctx0", "wk", "wv", "wo", "ctx1")
        WEIGHTS = {"wq": 0, "wk": 1, "wv": 2, "wo": 3}
        PIECES = KD * 2 + 4

        def width(u):
            return (u // HEADS + 1) * P

        def on_act(u):
            return u % 5 in (1, 3)

        def taken(u):
            mine = [x for x in range(U) if on_act(x) == on_act(u)]
            return (pT_act if on_act(u) else pT_dve), len(mine), mine.index(u) + 1

        def take_pT(eng, copy, u, b):
            sem_, per, _ = taken(u)
            eng.wait_ge(pT_psum, b * U + u + 1)
            if u >= 2:
                eng.wait_ge(pv_done, b * U + u - 1)
            n = width(u)
            copy(probsT[:, u % 2].rearrange("p k n -> p (k n)")[:, 0:n], banks[3 + u % 2][:, 0:n]).then_inc(sem_, 1)

        with nc.Block() as block:
            @block.sync
            def _(sp):
                if load_x:
                    sp.dma_start(xres[:, 0:TT], a["x"][0].rearrange("(t p) d -> p t d", p=P)).then_inc(x_loaded, 16)
                for i, name in enumerate(ITEMS):
                    if i == 3 and load_x:
                        sp.wait_ge(x_loaded, 16)
                        sp.dma_start(xres[:, TT:NT], a["x"][1].rearrange("(t p) d -> p t d", p=P)).then_inc(x_loaded, 16)
                    if i >= 2:
                        sp.wait_ge(cut, i - 1)
                    src = a[name] if name in WEIGHTS else a["ctxT"][int(name[3:])]
                    sp.dma_start(stage[:, i % 2], src.rearrange("(k p) n -> p k n", p=P)).then_inc(staged[i % 2], 16)

            @block.gpsimd
            def _(pool):
                pool.memset(mask[:, 0:SEQ - P], 0.0).then_inc(mask_done, 1)
                pool.tensor_copy(mask[:, SEQ - P:SEQ], c["mask"][:]).then_inc(mask_done, 1)

                def rms(b):
                    pool.wait_ge(mv_done, (b + 1) * TT)
                    pool.tensor_scalar(rstd[:], mv[:, :, 1], LN_EPS, None, ALU.add).then_inc(rstd_done, 1)
                    pool.wait_ge(rstd_done, b * 2 + 1)
                    pool.tensor_tensor(rstd[:], rstd[:], c["minus_half"][:, 0:TT], ALU.pow).then_inc(rstd_done, 1)

                def cut_item(i):
                    name = ITEMS[i]
                    hi, lo = (w_hi[:, WEIGHTS[name]], w_lo[:, WEIGHTS[name]]) if name in WEIGHTS else (c_hi[:], c_lo[:])
                    pool.wait_ge(staged[i % 2], 16 * (i // 2 + 1))
                    if name == "ctx1":
                        pool.wait_ge(proj_psum, 12)
                    pool.tensor_copy(hi, stage[:, i % 2]).then_inc(hi_done, 1)
                    pool.wait_ge(hi_done, i + 1)
                    pool.tensor_tensor(lo, stage[:, i % 2], hi.bitcast(F32), ALU.subtract).then_inc(cut, 1)
                rms(0)
                cut_item(0)
                cut_item(1)
                for i in range(2, 6):
                    cut_item(i)
                for b in range(1, BATCH):
                    rms(b)

            @block.scalar
            def _(act):
                with act.Fori(0, BATCH) as b:
                    for t in range(TT):
                        act.wait_ge(xT_psum, b * TT + t + 1)
                        act.copy(xT_hi[:, :, t * P:(t + 1) * P],
                                 banks[4 + t % 2][:].rearrange("p (k n) -> p k n", k=KD)).then_inc(xT_hi_done, 1)
                    act.wait_ge(zeroed, 1)
                    for j in range(12):
                        what, n = divmod(j, 4)
                        if what == 0 or j % 2 == 0:
                            act.wait_ge(proj_psum, b * 12 + j + 1)
                        if what == 0:
                            for h in range(2):
                                r = slice(HD * h, HD * (h + 1))
                                act.copy(q_pad[r, 4 * n + h], banks[j % 4][r, :]).then_inc(proj_act, 1)
                        elif j % 2 == 0:
                            act.copy((kT, v)[what - 1][:, n], banks[j % 4][:]).then_inc(proj_act, 1)
                    for i in range(STEPS):
                        if i < U:
                            act.wait_ge(max_done, b * U + i + 1)
                            if i >= 4:
                                act.wait_ge(pT_psum, b * U + i - 3)
                            act.activation(probs[:, i % 4, 0:width(i)], rows[:, i % 4, 0:width(i)], ACT.Exp,
                                           bias=neg_max[:, i % 4:i % 4 + 1], scale=-1.0,
                                           accum_out=row_sum[:, i % 4:i % 4 + 1]).then_inc(exp_done, 1)
                        u = i - 3
                        if 0 <= u < U and on_act(u):
                            take_pT(act, act.copy, u, b)
                        if i >= 20 and (i - 20) % HEADS == 0:
                            qt = (i - 20) // HEADS
                            act.wait_ge(pv_done, b * U + (qt + 1) * HEADS)
                            if qt > 0:
                                act.wait_ge(y_psum, b * TT + qt)
                            act.copy(oT_hi[:], banks[5 + qt % 2][:].rearrange("p (k n) -> p k n", k=KD)).then_inc(oT_hi_done, 1)

            @block.vector
            def _(dve):
                dve.memset(q_pad[:], 0.0).then_inc(zeroed, 1)
                dve.wait_ge(mask_done, 2)
                with dve.Fori(0, BATCH) as b:
                    if load_x:
                        hold(dve, x_loaded, b * 16 + 16, passed)
                    for t in range(TT):
                        dve.bn_stats(stats[:, t, :], xres[:, b * TT + t, :]).then_inc(stats_done, 1)
                    for t in range(TT):
                        hold(dve, stats_done, b * TT + t + 1, passed)
                        dve.bn_aggr(mv[:, t, :], stats[:, t, :]).then_inc(mv_done, 1)
                    dve.wait_ge(rstd_done, b * 2 + 2)
                    for t in range(TT):
                        dve.tensor_scalar(rows[:, t, :], xres[:, b * TT + t, :], mv[:, t, 0:1], rstd[:, t:t + 1],
                                          ALU.subtract, ALU.mult).then_inc(xn_done, 1)
                    for t in range(TT):
                        dve.wait_ge(xT_hi_done, b * TT + t + 1)
                        s = slice(t * P, (t + 1) * P)
                        dve.tensor_tensor(xT_lo[:, :, s], banks[4 + t % 2][:].rearrange("p (k n) -> p k n", k=KD),
                                          xT_hi[:, :, s].bitcast(F32), ALU.subtract).then_inc(xT_lo_done, 1)
                    dve.wait_ge(zeroed, 1)
                    for j in range(12):
                        what, n = divmod(j, 4)
                        if what == 0 or j % 2:
                            dve.wait_ge(proj_psum, b * 12 + j + 1)
                        if what == 0:
                            for h in range(2, 4):
                                r = slice(HD * h, HD * (h + 1))
                                dve.tensor_copy(q_pad[r, 4 * n + h], banks[j % 4][r, :]).then_inc(proj_dve, 1)
                        elif j % 2:
                            dve.tensor_copy((kT, v)[what - 1][:, n], banks[j % 4][:]).then_inc(proj_dve, 1)
                    for i in range(STEPS):
                        if 0 <= i - 2 < U:
                            u = i - 2
                            dve.wait_ge(exp_done, b * U + u + 1)
                            dve.reciprocal(inv_sum[:, u % 4:u % 4 + 1], row_sum[:, u % 4:u % 4 + 1]).then_inc(inv_done, 1)
                        if i < U:
                            hold(dve, scores, b * U + i + 1, passed)
                            dve.tensor_tensor_reduce(out=rows[:, i % 4, 0:width(i)], in0=banks[i % 3][:, 0:width(i)],
                                                     in1=mask[:, SEQ - width(i):SEQ], scale=-scale, scalar=3e38,
                                                     op0=ALU.add, op1=ALU.min,
                                                     accum_out=neg_max[:, i % 4:i % 4 + 1]).then_inc(max_done, 1)
                        if 0 <= i - 2 < U:
                            u = i - 2
                            dve.wait_ge(inv_done, b * U + u + 1)
                            dve.tensor_scalar(probs[:, u % 4, 0:width(u)], probs[:, u % 4, 0:width(u)],
                                              inv_sum[:, u % 4:u % 4 + 1], None, ALU.mult).then_inc(norm_done, 1)
                        u = i - 3
                        if 0 <= u < U and not on_act(u):
                            take_pT(dve, dve.tensor_copy, u, b)
                        if i >= 20 and (i - 20) % HEADS == 0:
                            qt = (i - 20) // HEADS
                            dve.wait_ge(oT_hi_done, b * TT + qt + 1)
                            dve.tensor_tensor(oT_lo[:], banks[5 + qt % 2][:].rearrange("p (k n) -> p k n", k=KD),
                                              oT_hi[:].bitcast(F32), ALU.subtract).then_inc(oT_lo_done, 1)
                        if i >= 23 and (i - 23) % HEADS == 0:
                            qt = (i - 23) // HEADS
                            dve.wait_ge(y_psum, b * TT + qt + 1)
                            dve.tensor_tensor(xres[:, b * TT + qt, :], xres[:, b * TT + qt, :], banks[7][:],
                                              ALU.add).then_inc(y_added, 1)

            @block.tensor
            def _(pe):
                with pe.Fori(0, BATCH) as b:
                    for t in range(TT):
                        pe.wait_ge(xn_done, b * TT + t + 1)
                        if t >= 2:
                            pe.wait_ge(xT_lo_done, b * TT + t - 1)
                        for k in range(KD):
                            last = pe.transpose(banks[4 + t % 2][:, k * P:(k + 1) * P], rows[:, t, k * P:(k + 1) * P],
                                                c["ident"][:])
                        last.then_inc(xT_psum, 1)
                    for j in range(12):
                        what, n = divmod(j, 4)
                        if 4 <= j < 8:
                            pe.wait_ge(proj_dve, b * PIECES + 2 * (j - 3))
                            pe.wait_ge(proj_act, b * PIECES + 2 * (j - 3))
                        if j >= 8:
                            pe.wait_ge(proj_dve if j % 2 else proj_act, b * PIECES + 8 + (j - 8) // 2 + 1)
                        if j == 0:
                            pe.wait_ge(cut, 1)
                            pe.wait_ge(xT_lo_done, b * TT + TT)
                        if j == 4:
                            pe.wait_ge(cut, b * 3 + 3)
                        if j == 8:
                            pe.wait_ge(cut, b * 2 + 4)
                        s = slice(n * P, (n + 1) * P)
                        for k in range(KD):
                            if what == 0:
                                ops = (w_hi[:, 0, k, s], w_lo[:, 0, k, s], xT_hi[:, k], xT_lo[:, k])
                            elif what == 1:
                                ops = (w_hi[:, 1, k, s], w_lo[:, 1, k, s], c_hi[:, k], c_lo[:, k])
                            else:
                                ops = (c_hi[:, k, s], c_lo[:, k, s], w_hi[:, 2, k], w_lo[:, 2, k])
                            last = mm3(pe, banks[j % 4][:], *ops, k == 0, k == KD - 1)
                        last.then_inc(proj_psum, 1)
                    pe.wait_ge(proj_act, b * PIECES + PIECES)
                    pe.wait_ge(proj_dve, b * PIECES + PIECES)

                    for i in range(STEPS):
                        if i < U:
                            qt, head = divmod(i, HEADS)
                            if i >= 3:
                                pe.wait_ge(max_done, b * U + i - 2)
                            pe.matmul(banks[i % 3][:, 0:width(i)], q_pad[:, head, qt * P:(qt + 1) * P],
                                      kT[:, head // 4, 0:width(i)], start=True, stop=True).then_inc(scores, 1)
                        if 0 <= i - 3 < U:
                            u = i - 3
                            pe.wait_ge(norm_done, b * U + u + 1)
                            if u >= 2:
                                sem_, per, n = taken(u - 2)
                                pe.wait_ge(sem_, b * per + n)
                            for kt in range(u // HEADS + 1):
                                last = pe.transpose(banks[3 + u % 2][:, kt * P:(kt + 1) * P],
                                                    probs[:, u % 4, kt * P:(kt + 1) * P], c["ident"][:])
                            last.then_inc(pT_psum, 1)
                        if 0 <= i - 4 < U:
                            u = i - 4
                            qt, head = divmod(u, HEADS)
                            sem_, per, n = taken(u)
                            pe.wait_ge(sem_, b * per + n)
                            if head == 0 and qt >= 2:
                                pe.wait_ge(oT_lo_done, b * TT + qt - 1)
                            r = slice(HD * (head % 4), HD * (head % 4 + 1))
                            q = slice((head // 4) * P, (head // 4 + 1) * P)
                            for kt in range(qt + 1):
                                last = pe.matmul(banks[5 + qt % 2][r, q], v[:, kt, head * HD:(head + 1) * HD],
                                                 probsT[:, u % 2, kt], start=(kt == 0), stop=(kt == qt))
                            last.then_inc(pv_done, 1)
                        if i >= 22 and (i - 22) % HEADS == 0:
                            qt = (i - 22) // HEADS
                            pe.wait_ge(oT_lo_done, b * TT + qt + 1)
                            pe.wait_ge(cut, 5)
                            if qt > 0:
                                pe.wait_ge(y_added, b * TT + qt)
                            for k in range(KD):
                                last = mm3(pe, banks[7][:], oT_hi[:, k], oT_lo[:, k], w_hi[:, 3, k], w_lo[:, 3, k],
                                           k == 0, k == KD - 1)
                            last.then_inc(y_psum, 1)
                    pe.wait_ge(y_added, b * TT + TT)


def mamba_scan(nc, sem, c, xres, banks, a, ln_mv, ln_rstd, yT):
    UP = 2
    UNITS = NS // UP
    WR = 4
    ON_POOL = (1, 3, 5)
    HALF = GI // 2
    NIN = 2 * GI
    RB = DR + 2 * NS
    outer = ExitStack()
    with outer:
        def sb(name, shape, dt, ctx=outer):
            return ctx.enter_context(nc.sbuf_tensor(name, shape, dt))
        conv_w = sb("conv_w", [P, GI, 4], F32)
        conv_b = sb("conv_b", [P, GI], F32)
        w_xproj = sb("w_xproj", [P, GI, RB], F32)
        w_dt = sb("w_dt", [DR, DI], F32)
        b_dt = sb("b_dt", [P, GI], F32)
        A = sb("A", [P, GI, NS], F32)
        Dp = sb("Dp", [P, GI], F32)
        stats = sb("m_stats", [P, TT, 6], F32)
        mv = sb("m_mv", [P, TT, 2], F32)
        rstd = sb("m_rstd", [P, TT], F32)
        gate = sb("gate", [P, GI, SEQ], F32)
        delta = sb("delta", [P, GI, SEQ], F32)
        du = sb("du", [P, GI, SEQ], F32)
        dA = sb("dA", [P, 2, UP, SEQ], F32)
        hs = sb("hs", [P, WR, UP, SEQ], F32)
        dbl = sb("dbl", [RB, SEQ], F32)
        dbl_hi = sb("dbl_hi", [RB, SEQ], F32R)
        dbl_lo = sb("dbl_lo", [RB, SEQ], F32R)
        early = ExitStack()
        with early:
            xm = sb("xm", [P, TT, D], F32, early)
            xT_hi = sb("m_xT_hi", [P, KD, SEQ], F32R, early)
            xT_lo = sb("m_xT_lo", [P, KD, SEQ], F32R, early)
            w_stage = sb("w_in_stage", [P, 2, KD, P], F32, early)
            w_hi = sb("w_in_hi", [P, 2, KD, P], F32R, early)
            w_lo = sb("w_in_lo", [P, 2, KD, P], F32R, early)
            raw = sb("raw", [P, 3, SEQ + 3], F32, early)
            pre = sb("pre", [P, 3, SEQ], F32, early)
            th = sb("th", [P, 3, SEQ], F32, early)
            e_t = sb("e_t", [P, HALF, SEQ], F32, early)
            w_t = sb("w_t", [P, HALF, SEQ], F32, early)
        Bs = sb("Bs", [P, NS, SEQ], F32)
        Cs = sb("Cs", [P, NS, SEQ], F32)

        passed = sem("m_passed")
        par_loaded = sem("par_loaded")
        par_act = sem("par_act")
        par_done = sem("par_done")
        pads = sem("pads")
        kept = sem("kept")
        win_loaded = [sem("win_loaded0"), sem("win_loaded1")]
        win_hi = sem("win_hi")
        win_lo = sem("win_lo")
        stats_done = sem("m_stats_done")
        mv_done = sem("m_mv_done")
        rstd_done = sem("m_rstd_done")
        xm_done = sem("xm_done")
        xT_psum = sem("m_xT_psum")
        xT_hi_done = sem("m_xT_hi_done")
        xT_lo_done = sem("m_xT_lo_done")
        in_psum = sem("in_psum")
        raw_done = sem("raw_done")
        pre_done = sem("pre_done")
        tap_done = sem("tap_done")
        tanh_done = sem("tanh_done")
        silu_done = sem("silu_done")
        dbl_psum = sem("dbl_psum")
        dbl_act = sem("dbl_act")
        dbl_lo_done = sem("dbl_lo_done")
        dt_psum = sem("dt_psum")
        absx_done = sem("absx_done")
        relu_done = sem("relu_done")
        expx_done = sem("expx_done")
        onep_done = sem("onep_done")
        fix_done = sem("fix_done")
        ln_done = sem("ln_done")
        delta_done = sem("delta_done")
        skip_done = sem("skip_done")
        du_done = sem("du_done")
        bc_psum = sem("bc_psum")
        bc_act = sem("bc_act")
        bc_dve = sem("bc_dve")
        dA_done = sem("dA_done")
        dBu_done = sem("dBu_done")
        scan_done = sem("scan_done")
        hC_dve = sem("hC_dve")
        hC_pool = sem("hC_pool")
        unit_summed = sem("unit_summed")
        y_skip = sem("y_skip")
        y_gated = sem("y_gated")

        with nc.Block() as block:
            @block.sync
            def _(sp):
                for dst, name in ((conv_w, "conv_w"), (conv_b, "conv_b"), (w_xproj, "w_xproj"), (w_dt, "w_dt"),
                                  (b_dt, "b_dt"), (A, "A_log"), (Dp, "Dp")):
                    sp.dma_start(dst[:], a[name]).then_inc(par_loaded, 16)
                with sp.Fori(0, BATCH) as b:
                    hold(sp, y_gated, b * GI + 1, passed)
                    sp.wait_ge(win_lo, b * NIN + 1)
                    for n in range(NIN):
                        if n >= 2:
                            sp.wait_ge(win_lo, b * NIN + n)
                        sp.dma_start(w_stage[:, n % 2], a["w_in"][n]).then_inc(win_loaded[n % 2], 16)

            @block.gpsimd
            def _(pool):
                pool.sem_inc(win_lo, 1)
                for r in range(2):
                    pool.memset(dA[:, r, :, 0:1], 0.0).then_inc(scan_done, 1)
                for r in range(WR):
                    pool.memset(hs[:, r], 0.0).then_inc(unit_summed, 1)
                with pool.Fori(0, BATCH) as b:
                    hold(pool, y_gated, b * GI + 1, passed)
                    pool.memset(raw[:, :, 0:3], 0.0).then_inc(pads, 1)
                    hold(pool, mv_done, (b + 1) * TT, passed)
                    r = rstd[:]
                    pool.tensor_scalar(r, mv[:, :, 1], LN_EPS, None, ALU.add).then_inc(rstd_done, 1)
                    pool.wait_ge(rstd_done, b * 2 + 1)
                    pool.tensor_tensor(r, r, c["minus_half"][:, 0:TT], ALU.pow).then_inc(rstd_done, 1)
                    def cut(n):
                        pool.wait_ge(win_hi, b * NIN + n + 1)
                        pool.tensor_tensor(w_lo[:, n % 2], w_stage[:, n % 2], w_hi[:, n % 2].bitcast(F32),
                                           ALU.subtract).then_inc(win_lo, 1)

                    def drive_all(hf):
                        pool.wait_ge(delta_done, (b * 2 + hf) * 2 + 2)
                        pool.wait_ge(skip_done, b * GI + (hf + 1) * HALF)
                        pool.wait_ge(dbl_psum, b + 1)
                        s = slice(hf * HALF, (hf + 1) * HALF)
                        pool.tensor_tensor(du[:, s], du[:, s], delta[:, s], ALU.mult).then_inc(du_done, 1)
                    for n in range(GI + 4):
                        cut(n)
                    drive_all(0)
                    for n in range(GI + 4, NIN):
                        cut(n)
                    drive_all(1)
                    hold(pool, du_done, b * 2 + 2, passed)
                    hold(pool, bc_act, b * NS + NS, passed)
                    hold(pool, bc_dve, b * NS + NS, passed)
                    with pool.Fori(0, GI) as g:
                        base = b * (GI * UNITS) + g * UNITS

                        def drive(u):
                            hold(pool, unit_summed, base + u + 1, passed)
                            pool.tensor_tensor(hs[:, u % WR], bc_mid(du[:, g], UP), Bs[:, UP * u:UP * (u + 1)],
                                               ALU.mult).then_inc(dBu_done, 1)

                        def read_out(u):
                            pool.wait_ge(scan_done, base + u + 3)
                            pool.tensor_tensor(hs[:, u % WR], hs[:, u % WR], Cs[:, UP * u:UP * (u + 1)],
                                               ALU.mult).then_inc(hC_pool, 1)
                        drive(0)
                        for u in range(1, UNITS):
                            drive(u)
                            if u - 1 in ON_POOL:
                                read_out(u - 1)

            @block.scalar
            def _(act):
                act.wait_ge(par_loaded, 7 * 16)
                act.activation(A[:], A[:], ACT.Exp).then_inc(par_act, 1)
                with act.Fori(0, BATCH) as b:
                    act.wait_ge(y_gated, b * GI + 1)
                    for t in range(TT):
                        act.wait_ge(xT_psum, b * TT + t + 1)
                        act.copy(xT_hi[:, :, t * P:(t + 1) * P],
                                 banks[4 + t % 2][:].rearrange("p (k n) -> p k n", k=KD)).then_inc(xT_hi_done, 1)

                    def cut(n):
                        act.wait_ge(win_loaded[n % 2], (b * (NIN // 2) + n // 2 + 1) * 16)
                        act.wait_ge(in_psum, b * NIN + max(n - 1, 0) + 1)
                        act.copy(w_hi[:, n % 2], w_stage[:, n % 2]).then_inc(win_hi, 1)

                    def take(n):
                        act.wait_ge(in_psum, b * NIN + n + 2)
                        act.wait_ge(silu_done, b * NIN + max(n - 2, 0) + 1)
                        if n == 0:
                            act.wait_ge(par_done, 3)
                            act.wait_ge(pads, b + 1)
                        if n < GI:
                            act.copy(raw[:, n % 3, 3:SEQ + 3], banks[n % 4][:]).then_inc(raw_done, 1)
                            act.activation(pre[:, n % 3], banks[n % 4][:], ACT.Identity, bias=conv_b[:, n:n + 1],
                                           scale=conv_w[:, n, 3:4]).then_inc(pre_done, 1)
                        else:
                            act.activation(pre[:, n % 3], banks[n % 4][:], ACT.Identity, scale=0.5).then_inc(pre_done, 1)

                    def tanh(n):
                        if n < GI:
                            act.wait_ge(tap_done, b * GI * 3 + 3 * (n + 1))
                        else:
                            act.wait_ge(pre_done, b * NIN + n + 1)
                        act.activation(th[:, n % 3], pre[:, n % 3], ACT.Tanh).then_inc(tanh_done, 1)
                    def softplus(hf):
                        act.wait_ge(absx_done, b * GI + (hf + 1) * HALF)
                        act.activation(e_t[:], e_t[:], ACT.Exp, scale=-1.0).then_inc(expx_done, 1)

                    def logarithm(hf):
                        act.wait_ge(fix_done, b * 2 + hf + 1)
                        act.activation(w_t[:], w_t[:], ACT.Ln).then_inc(ln_done, 1)

                    def abs_x(g):
                        act.wait_ge(dt_psum, b * GI + g + 1)
                        if g >= HALF:
                            act.wait_ge(delta_done, b * 4 + 2)
                        act.activation(e_t[:, g % HALF], banks[5 + g % 2][:], ACT.Abs,
                                       bias=b_dt[:, g:g + 1]).then_inc(absx_done, 1)
                    cut(0)
                    cut(1)
                    for n in range(GI):
                        take(n)
                        cut(n + 2)
                        if n >= 1:
                            tanh(n - 1)
                    tanh(GI - 1)
                    act.wait_ge(dbl_psum, b + 1)
                    act.copy(dbl[:], banks[4][0:RB, :]).then_inc(dbl_act, 1)
                    act.copy(dbl_hi[:], banks[4][0:RB, :]).then_inc(dbl_act, 1)
                    for g in range(HALF):
                        abs_x(g)
                    softplus(0)
                    take(GI)
                    cut(GI + 2)
                    logarithm(0)
                    for g in range(HALF, GI):
                        abs_x(g)
                    softplus(1)
                    take(GI + 1)
                    cut(GI + 3)
                    tanh(GI)
                    logarithm(1)
                    for n in range(GI + 2, NIN):
                        take(n)
                        if n + 2 < NIN:
                            cut(n + 2)
                        tanh(n - 1)
                    tanh(NIN - 1)
                    act.wait_ge(delta_done, b * 4 + 4)
                    act.wait_ge(silu_done, b * NIN + NIN + 1)
                    for i in range(0, 2 * NS, 2):
                        act.wait_ge(bc_psum, b * 2 * NS + i + 1)
                        act.copy((Bs if i < NS else Cs)[:, i % NS], banks[i % 4][:]).then_inc(bc_act, 1)
                    with act.Fori(0, GI) as g:
                        base = b * (GI * UNITS) + g * UNITS
                        for u in range(UNITS):
                            act.wait_ge(scan_done, base + u + 1)
                            for n in range(UP):
                                act.activation(dA[:, u % 2, n, 1:SEQ], delta[:, g, 1:SEQ], ACT.Exp,
                                               scale=A[:, g, UP * u + n:UP * u + n + 1]).then_inc(dA_done, 1)

            @block.vector
            def _(dve):
                dve.sem_inc(y_gated, 1)
                dve.sem_inc(silu_done, 1)
                dve.sem_inc(y_skip, 1)
                dve.wait_ge(par_act, 1)
                dve.tensor_scalar(A[:], A[:], -1.0, None, ALU.mult).then_inc(par_done, 1)
                dve.tensor_scalar(conv_w[:], conv_w[:], 0.5, None, ALU.mult).then_inc(par_done, 1)
                dve.tensor_scalar(conv_b[:], conv_b[:], 0.5, None, ALU.mult).then_inc(par_done, 1)
                dve.wait_ge(par_done, 3)
                with dve.Fori(0, BATCH) as b:
                    for t in range(TT):
                        dve.bn_stats(stats[:, t, :], xres[:, b * TT + t, :]).then_inc(stats_done, 1)
                    for t in range(TT):
                        hold(dve, stats_done, b * TT + t + 1, passed)
                        dve.bn_aggr(mv[:, t, :], stats[:, t, :]).then_inc(mv_done, 1)
                    dve.wait_ge(rstd_done, b * 2 + 2)
                    dve.tensor_copy(ln_mv[:, bass.ds(b * TT, TT), :], mv[:]).then_inc(kept, 1)
                    dve.tensor_copy(ln_rstd[:, bass.ds(b * TT, TT)], rstd[:]).then_inc(kept, 1)
                    for t in range(TT):
                        dve.tensor_scalar(xm[:, t, :], xres[:, b * TT + t, :], mv[:, t, 0:1],
                                          rstd[:, t:t + 1], ALU.subtract, ALU.mult).then_inc(xm_done, 1)
                    for t in range(TT):
                        dve.wait_ge(xT_hi_done, b * TT + t + 1)
                        s = slice(t * P, (t + 1) * P)
                        dve.tensor_tensor(xT_lo[:, :, s], banks[4 + t % 2][:].rearrange("p (k n) -> p k n", k=KD),
                                          xT_hi[:, :, s].bitcast(F32), ALU.subtract).then_inc(xT_lo_done, 1)

                    def taps(n):
                        dve.wait_ge(raw_done, b * GI + n + 1)
                        for j in range(3):
                            if j == 0:
                                dve.wait_ge(pre_done, b * NIN + n + 1)
                            else:
                                dve.wait_ge(tap_done, b * GI * 3 + 3 * n + j)
                            dve.scalar_tensor_tensor(pre[:, n % 3], raw[:, n % 3, j:j + SEQ], conv_w[:, n, j:j + 1],
                                                     pre[:, n % 3], ALU.mult, ALU.add).then_inc(tap_done, 1)

                    def silu(n):
                        dve.wait_ge(tanh_done, b * NIN + n + 1)
                        dst = du[:, n] if n < GI else gate[:, n - GI]
                        dve.scalar_tensor_tensor(dst, th[:, n % 3], 1.0, pre[:, n % 3], ALU.add,
                                                 ALU.mult).then_inc(silu_done, 1)
                    for n in range(GI):
                        taps(n)
                        if n >= 1:
                            silu(n - 1)
                    silu(GI - 1)
                    dve.wait_ge(dbl_act, b * 2 + 2)
                    dve.tensor_tensor(dbl_lo[:], banks[4][0:RB, :], dbl_hi[:].bitcast(F32), ALU.subtract).then_inc(dbl_lo_done, 1)
                    for hf in range(2):
                        s = slice(hf * HALF, (hf + 1) * HALF)
                        for g in range(hf * HALF, (hf + 1) * HALF):
                            dve.wait_ge(absx_done, b * GI + g + 1)
                            dve.tensor_scalar(delta[:, g], banks[5 + g % 2][:], b_dt[:, g:g + 1], 0.0,
                                              ALU.add, ALU.max).then_inc(relu_done, 1)
                        for g in range(hf * HALF, (hf + 1) * HALF):
                            dve.tensor_scalar(yT[:, g, bass.ds(b * SEQ, SEQ)], du[:, g], Dp[:, g:g + 1], None,
                                              ALU.mult).then_inc(skip_done, 1)
                        dve.wait_ge(expx_done, b * 2 + hf + 1)
                        dve.tensor_scalar(w_t[:], e_t[:], 1.0, None, ALU.add).then_inc(onep_done, 1)
                        dve.wait_ge(onep_done, b * 2 + hf + 1)
                        dve.scalar_tensor_tensor(e_t[:].rearrange("p g s -> p (g s)"), w_t[:].rearrange("p g s -> p (g s)"),
                                                 -1.0, e_t[:].rearrange("p g s -> p (g s)"), ALU.add,
                                                 ALU.subtract).then_inc(fix_done, 1)
                        dve.wait_ge(relu_done, b * GI + (hf + 1) * HALF)
                        dve.wait_ge(fix_done, b * 2 + hf + 1)
                        dve.tensor_tensor(delta[:, s], delta[:, s], e_t[:], ALU.subtract).then_inc(delta_done, 1)
                        dve.wait_ge(ln_done, b * 2 + hf + 1)
                        dve.wait_ge(delta_done, b * 4 + 2 * hf + 1)
                        dve.tensor_tensor(delta[:, s], delta[:, s], w_t[:], ALU.add).then_inc(delta_done, 1)
                    for n in range(GI, NIN):
                        silu(n)
                    dve.wait_ge(delta_done, b * 4 + 4)
                    for i in range(1, 2 * NS, 2):
                        dve.wait_ge(bc_psum, b * 2 * NS + i + 1)
                        dve.tensor_copy((Bs if i < NS else Cs)[:, i % NS], banks[i % 4][:]).then_inc(bc_dve, 1)
                    hold(dve, skip_done, b * GI + GI, passed)
                    dve.wait_ge(bc_act, b * NS + NS)
                    dve.wait_ge(bc_dve, b * NS + NS)

                    def unit_loop(g, first):
                        base = b * (GI * UNITS) + g * UNITS

                        def scan(u):
                            dve.wait_ge(dA_done, (base + u + 1) * UP)
                            dve.wait_ge(dBu_done, base + u + 1)
                            w = hs[:, u % WR].rearrange("p n s -> p (n s)")
                            dve.tensor_tensor_scan(w, dA[:, u % 2].rearrange("p n s -> p (n s)"), w, 0.0,
                                                   ALU.mult, ALU.add).then_inc(scan_done, 1)

                        def read_out(u):
                            if u not in ON_POOL:
                                dve.wait_ge(scan_done, base + u + 3)
                                dve.tensor_tensor(hs[:, u % WR], hs[:, u % WR], Cs[:, UP * u:UP * (u + 1)],
                                                  ALU.mult).then_inc(hC_dve, 1)
                        scan(0)
                        scan(1)
                        if not first:
                            skip(g - 1)
                        read_out(0)
                        if not first:
                            gated(g - 1)
                        for u in range(2, UNITS):
                            scan(u)
                            read_out(u - 1)
                        read_out(UNITS - 1)

                    def skip(g):
                        dve.wait_ge(unit_summed, b * (GI * UNITS) + (g + 1) * UNITS + WR)
                        y = yT[:, g, bass.ds(b * SEQ, SEQ)]
                        dve.tensor_tensor(y, y, banks[7][:], ALU.add).then_inc(y_skip, 1)

                    def gated(g):
                        dve.wait_ge(y_skip, b * GI + g + 2)
                        y = yT[:, g, bass.ds(b * SEQ, SEQ)]
                        dve.tensor_tensor(y, y, gate[:, g], ALU.mult).then_inc(y_gated, 1)
                    unit_loop(0, True)
                    with dve.Fori(1, GI) as g:
                        unit_loop(g, False)
                    skip(GI - 1)
                    gated(GI - 1)
                    dve.wait_ge(y_gated, b * GI + GI + 1)

            @block.tensor
            def _(pe):
                pe.sem_inc(in_psum, 1)
                with pe.Fori(0, BATCH) as b:
                    for t in range(TT):
                        pe.wait_ge(xm_done, b * TT + t + 1)
                        if t >= 2:
                            pe.wait_ge(xT_lo_done, b * TT + t - 1)
                        for k in range(KD):
                            last = pe.transpose(banks[4 + t % 2][:, k * P:(k + 1) * P], xm[:, t, k * P:(k + 1) * P],
                                                c["ident"][:])
                        last.then_inc(xT_psum, 1)
                    pe.wait_ge(xT_lo_done, b * TT + TT)
                    def project_in(n):
                        pe.wait_ge(win_lo, b * NIN + n + 2)
                        if n >= 4:
                            pe.wait_ge(pre_done, b * NIN + n - 3)
                        for k in range(KD):
                            last = mm3(pe, banks[n % 4][:], w_hi[:, n % 2, k], w_lo[:, n % 2, k], xT_hi[:, k], xT_lo[:, k],
                                       k == 0, k == KD - 1)
                        last.then_inc(in_psum, 1)
                    def project_u(k):
                        pe.wait_ge(silu_done, b * NIN + k + 2)
                        last = pe.matmul(banks[4][0:RB, :], w_xproj[:, k], du[:, k], start=(k == 0), stop=(k == GI - 1))
                        if k == GI - 1:
                            last.then_inc(dbl_psum, 1)
                    for n in range(GI):
                        project_in(n)
                        if n >= 3:
                            project_u(n - 3)
                    for k in range(GI - 3, GI):
                        project_u(k)
                    pe.wait_ge(dbl_act, b * 2 + 1)
                    for g in range(GI):
                        if g >= 2:
                            pe.wait_ge(relu_done, b * GI + g - 1)
                        pe.matmul(banks[5 + g % 2][:], w_dt[:, g * P:(g + 1) * P], dbl[0:DR, :],
                                  start=True, stop=True).then_inc(dt_psum, 1)
                        if g == HALF + 1:
                            project_in(GI)
                    for n in range(GI + 1, NIN):
                        project_in(n)
                    pe.wait_ge(dbl_lo_done, b + 1)
                    for i in range(2 * NS):
                        if i == 0:
                            pe.wait_ge(pre_done, b * NIN + NIN)
                        if i >= 4:
                            pe.wait_ge(bc_dve if i % 2 else bc_act, b * NS + (i - 4) // 2 + 1)
                        pick = c["ident_r"][0:RB, DR + i:DR + i + 1].to_broadcast([RB, P])
                        pe.matmul(banks[i % 4][:], pick, dbl_hi[:], start=True, stop=False)
                        pe.matmul(banks[i % 4][:], pick, dbl_lo[:], start=False, stop=True).then_inc(bc_psum, 1)
                    hold(pe, bc_act, b * NS + NS, passed)
                    hold(pe, bc_dve, b * NS + NS, passed)
                    with pe.Fori(0, GI) as g:
                        nd = UNITS - len(ON_POOL)
                        for u in range(UNITS):
                            if u in ON_POOL:
                                pe.wait_ge(hC_pool, b * (GI * len(ON_POOL)) + g * len(ON_POOL) + ON_POOL.index(u) + 1)
                            else:
                                k = len([x for x in range(u) if x not in ON_POOL])
                                pe.wait_ge(hC_dve, b * (GI * nd) + g * nd + k + 1)
                            if u == 0:
                                pe.wait_ge(y_skip, b * GI + g + 1)
                            for n in range(UP):
                                last = pe.matmul(banks[7][:], c["ident"][:], hs[:, u % WR, n], start=(u == 0 and n == 0),
                                                 stop=(u == UNITS - 1 and n == UP - 1))
                            last.then_inc(unit_summed, 1)


def feed_forward(nc, sem, c, xres, banks, a, ln_mv, ln_rstd, yT):
    KF = FF // P
    outer = ExitStack()
    with outer:
        def sb(name, shape, dt, ctx=outer):
            return ctx.enter_context(nc.sbuf_tensor(name, shape, dt))
        wo_hi = sb("wo_hi", [P, GI, D], F32R)
        wo_lo = sb("wo_lo", [P, GI, D], F32R)
        w1q = sb("w1q", [P, KD, FF], BF16)
        w2q = sb("w2q", [P, KF, D], BF16)
        n1 = sb("n1", [P, D], F32)
        n2 = sb("n2", [P, D], F32)
        b1 = sb("b1", [P, FF], F32)
        b2 = sb("b2", [P, D], F32)
        part = sb("part", [P, 2], F32)
        g = sb("g", [P, 2], F32)
        g_inv = sb("g_inv", [P, 2], F32)
        g_127 = sb("g_127", [P, 2], F32)

        stage = ExitStack()
        with stage:
            w1 = sb("w1_stage", [P, KD, FF], F32, stage)
            w2 = sb("w2_stage", [P, KF, D], F32, stage)
            wo = sb("wo_stage", [P, GI // 2, D], F32, stage)
            w1_loaded, w2_loaded, wo_loaded, rows_loaded = sem("w1_loaded"), sem("w2_loaded"), sem("wo_loaded"), sem("rows_loaded")
            part_done, total_psum, g_done, wo_cut = sem("part_done"), sem("total_psum"), sem("g_done"), sem("wo_cut")
            q1, q2 = sem("q1"), sem("q2")
            with nc.Block() as block:
                @block.sync
                def _(sp):
                    sp.dma_start(w1[:], a["w1"]).then_inc(w1_loaded, 16)
                    sp.dma_start(w2[:], a["w2"]).then_inc(w2_loaded, 16)
                    sp.dma_start(wo[:], a["w_out"][:, 0:GI // 2]).then_inc(wo_loaded, 16)
                    for dst, name in ((n1, "n1"), (n2, "n2"), (b1, "b1"), (b2, "b2")):
                        sp.dma_start(dst[:], a[name].to_broadcast([P, a[name].shape[1]])).then_inc(rows_loaded, 16)
                    sp.wait_ge(wo_cut, 2)
                    sp.dma_start(wo[:], a["w_out"][:, GI // 2:GI]).then_inc(wo_loaded, 16)
                    sp.wait_ge(rows_loaded, 64)

                @block.scalar
                def _(act):
                    for hf in range(2):
                        act.wait_ge(wo_loaded, 16 * (hf + 1))
                        act.copy(wo_hi[:, hf * (GI // 2):(hf + 1) * (GI // 2)], wo[:]).then_inc(wo_cut, 1)

                @block.vector
                def _(dve):
                    dve.wait_ge(w1_loaded, 16)
                    dve.tensor_reduce(part[:, 0:1], w1[:], AX.XY, ALU.add, apply_absolute_value=True).then_inc(part_done, 1)
                    dve.wait_ge(w2_loaded, 16)
                    dve.tensor_reduce(part[:, 1:2], w2[:], AX.XY, ALU.add, apply_absolute_value=True).then_inc(part_done, 1)
                    dve.wait_ge(total_psum, 1)
                    dve.tensor_scalar(g[:], banks[0][:, 0:2], 1.0 / (FF * D), 1e-5, ALU.mult, ALU.max).then_inc(g_done, 1)
                    dve.wait_ge(g_done, 1)
                    dve.reciprocal(g_inv[:], g[:]).then_inc(g_done, 1)
                    dve.tensor_scalar(g_127[:], g[:], 1.0 / 127.0, None, ALU.mult).then_inc(g_done, 1)
                    dve.wait_ge(g_done, 3)
                    dve.tensor_scalar(w1[:], w1[:], g_inv[:, 0:1], 1.0, ALU.mult, ALU.min).then_inc(q1, 1)
                    dve.wait_ge(q1, 1)
                    dve.tensor_scalar(w1[:], w1[:], -1.0, ROUND, ALU.max, ALU.add).then_inc(q1, 1)
                    dve.wait_ge(q1, 2)
                    dve.tensor_scalar(w1q[:], w1[:], -ROUND, None, ALU.add).then_inc(q1, 1)

                @block.gpsimd
                def _(pool):
                    for hf in range(2):
                        s = slice(hf * (GI // 2), (hf + 1) * (GI // 2))
                        pool.wait_ge(wo_cut, 2 * hf + 1)
                        pool.tensor_tensor(wo_lo[:, s], wo[:], wo_hi[:, s].bitcast(F32), ALU.subtract).then_inc(wo_cut, 1)
                    pool.wait_ge(g_done, 3)
                    pool.tensor_scalar(w2[:], w2[:], g_inv[:, 1:2], 1.0, ALU.mult, ALU.min).then_inc(q2, 1)
                    pool.wait_ge(q2, 1)
                    pool.tensor_scalar(w2[:], w2[:], -1.0, ROUND, ALU.max, ALU.add).then_inc(q2, 1)
                    pool.wait_ge(q2, 2)
                    pool.tensor_scalar(w2q[:], w2[:], -ROUND, None, ALU.add).then_inc(q2, 1)

                @block.tensor
                def _(pe):
                    pe.wait_ge(part_done, 2)
                    pe.matmul(banks[0][:, 0:2], c["ones"][:], part[:], start=True, stop=True).then_inc(total_psum, 1)

        y_hi = sb("y_hi", [P, GI, P], F32R)
        y_lo = sb("y_lo", [P, GI, P], F32R)
        xm = sb("p_xm", [P, D], F32)
        xr = sb("xr", [P, D], F32)
        sq = sb("sq", [P, D], F32)
        x1 = sb("x1", [P, NT, D], F32)
        qt = sb("qt", [P, D], F32)
        qx = sb("qx", [P, D], BF16)
        qxT = sb("qxT", [P, KD, P], BF16)
        f1 = sb("f1", [P, FF], F32)
        fq = sb("fq", [P, FF], BF16)
        fqT = sb("fqT", [P, KF, P], BF16)
        f2 = sb("f2", [P, D], F32)
        sq2 = sb("sq2", [P, D], F32)
        o2 = sb("o2", [P, D], F32)
        ss = sb("ss", [P, 2], F32)
        rs = sb("rs", [P, 2], F32)
        am = sb("am", [P, 2], F32)
        quant = sb("quant", [P, 2], F32)
        unscale = sb("unscale", [P, NT, 2], F32)

        passed = sem("p_passed")
        y_hi_done, y_lo_done, out_psum = sem("y_hi_done"), sem("y_lo_done"), sem("out_psum")
        xm_done, xr_done, ss1, rs1, x1_done = sem("p_xm_done"), sem("xr_done"), sem("ss1"), sem("rs1"), sem("x1_done")
        am1, qt1, qx_done, qxT_psum, qxT_done = sem("am1"), sem("qt1"), sem("qx_done"), sem("qxT_psum"), sem("qxT_done")
        ff1_psum, f1_done, gelu_done, am2, fq_tmp, fq_done = (sem("ff1_psum"), sem("f1_done"), sem("gelu_done"), sem("am2"),
                                                              sem("fq_tmp"), sem("fq_done"))
        fqT_psum, fqT_done, ff2_psum, f2_done, ss2, rs2, o2_done, res_done = (
            sem("fqT_psum"), sem("fqT_done"), sem("ff2_psum"), sem("f2_done"), sem("ss2"), sem("rs2"), sem("o2_done"), sem("res_done"))
        tq = banks[1][:, 0:KD * P // 2].bitcast(BF16)
        tf = banks[6][:].bitcast(BF16)

        with nc.Block() as block:
            @block.gpsimd
            def _(pool):
                def rms(i, k, sums, done):
                    hold(pool, sums, i + 1, passed)
                    pool.tensor_scalar(rs[:, k:k + 1], ss[:, k:k + 1], 1.0 / D, RMS_EPS, ALU.mult, ALU.add).then_inc(done, 1)
                    pool.wait_ge(done, 2 * i + 1)
                    pool.tensor_tensor(rs[:, k:k + 1], rs[:, k:k + 1], c["minus_half"][:, 0:1], ALU.pow).then_inc(done, 1)

                def cut_y(i):
                    hold(pool, y_hi_done, i + 1, passed)
                    pool.tensor_tensor(y_lo[:], yT[:, :, bass.ds(i * P, P)], y_hi[:].bitcast(F32), ALU.subtract).then_inc(y_lo_done, 1)
                cut_y(0)
                rms(0, 0, ss1, rs1)
                with pool.Fori(1, NT) as i:
                    cut_y(i)
                    rms(i, 0, ss1, rs1)
                    rms(i - 1, 1, ss2, rs2)
                rms(NT - 1, 1, ss2, rs2)

            @block.scalar
            def _(act):
                act.sem_inc(qxT_done, 1)
                act.sem_inc(fqT_done, 1)
                def cut_y(i):
                    act.wait_ge(out_psum, i + 1)
                    act.copy(y_hi[:], yT[:, :, bass.ds(i * P, P)]).then_inc(y_hi_done, 1)

                def square1(i):
                    act.wait_ge(xr_done, i + 2)
                    act.activation(sq[:], xr[:], ACT.Square, accum_out=ss[:, 0:1]).then_inc(ss1, 1)

                def take_qxT(i):
                    act.wait_ge(qxT_psum, i + 1)
                    act.copy(qxT[:].rearrange("p k n -> p (k n)"), tq).then_inc(qxT_done, 1)

                def gelu(i):
                    act.wait_ge(f1_done, 4 * i + 5)
                    act.activation(f1[:], f1[:], ACT.Gelu_apprx_tanh).then_inc(gelu_done, 1)

                def take_fqT(i):
                    for hf in range(2):
                        act.wait_ge(fqT_psum, 2 * i + hf + 1)
                        act.copy(fqT[:, hf * (KF // 2):(hf + 1) * (KF // 2)].rearrange("p k n -> p (k n)"), tf).then_inc(fqT_done, 1)

                def square2(i):
                    act.wait_ge(f2_done, 2 * i + 3)
                    act.activation(sq2[:], f2[:], ACT.Square, accum_out=ss[:, 1:2]).then_inc(ss2, 1)
                cut_y(0)
                square1(0)
                take_qxT(0)
                with act.Fori(1, NT) as i:
                    cut_y(i)
                    square1(i)
                    gelu(i - 1)
                    take_qxT(i)
                    take_fqT(i - 1)
                    square2(i - 1)
                gelu(NT - 1)
                take_fqT(NT - 1)
                square2(NT - 1)

            @block.vector
            def _(dve):
                dve.sem_inc(xr_done, 1)
                dve.sem_inc(f1_done, 1)
                dve.sem_inc(f2_done, 1)
                def front1(i):
                    dve.tensor_scalar(xm[:], xres[:, i, :], ln_mv[:, i, 0:1], ln_rstd[:, bass.ds(i, 1)], ALU.subtract,
                                      ALU.mult).then_inc(xm_done, 1)
                    dve.wait_ge(xm_done, i + 1)
                    dve.wait_ge(out_psum, i + 2)
                    dve.tensor_tensor(xr[:], xm[:], banks[0][:], ALU.add).then_inc(xr_done, 1)

                def front2(i):
                    dve.wait_ge(rs1, 2 * i + 2)
                    dve.scalar_tensor_tensor(x1[:, i, :], xr[:], rs[:, 0:1], n1[:], ALU.mult, ALU.mult).then_inc(x1_done, 1)
                    hold(dve, x1_done, i + 1, passed)
                    dve.tensor_reduce(am[:, 0:1], x1[:, i, :], AX.X, ALU.max, apply_absolute_value=True).then_inc(am1, 1)
                    dve.wait_ge(am1, 4 * i + 1)
                    dve.tensor_scalar(am[:, 0:1], am[:, 0:1], 1e-5, None, ALU.max).then_inc(am1, 1)
                    dve.wait_ge(am1, 4 * i + 2)
                    dve.reciprocal(quant[:, 0:1], am[:, 0:1]).then_inc(am1, 1)
                    dve.tensor_scalar(unscale[:, i, 0:1], am[:, 0:1], g_127[:, 0:1], None, ALU.mult).then_inc(am1, 1)
                    dve.wait_ge(am1, 4 * i + 4)
                    dve.tensor_scalar(quant[:, 0:1], quant[:, 0:1], 127.0, None, ALU.mult).then_inc(qt1, 1)
                    dve.wait_ge(qt1, 2 * i + 1)
                    dve.tensor_scalar(qt[:], x1[:, i, :], quant[:, 0:1], ROUND, ALU.mult, ALU.add).then_inc(qt1, 1)
                    dve.wait_ge(qt1, 2 * i + 2)
                    dve.tensor_scalar(qx[:], qt[:], -ROUND, None, ALU.add).then_inc(qx_done, 1)

                def back1(i):
                    for n in range(4):
                        dve.wait_ge(ff1_psum, 4 * i + n + 1)
                        s = slice(n * 512, (n + 1) * 512)
                        dve.scalar_tensor_tensor(f1[:, s], banks[2 + n][:], unscale[:, i, 0:1], b1[:, s], ALU.mult,
                                                 ALU.add).then_inc(f1_done, 1)

                def back2(i):
                    dve.wait_ge(gelu_done, i + 1)
                    dve.tensor_reduce(am[:, 1:2], f1[:], AX.X, ALU.max, apply_absolute_value=True).then_inc(am2, 1)
                    dve.wait_ge(am2, 4 * i + 1)
                    dve.tensor_scalar(am[:, 1:2], am[:, 1:2], 1e-5, None, ALU.max).then_inc(am2, 1)
                    dve.wait_ge(am2, 4 * i + 2)
                    dve.reciprocal(quant[:, 1:2], am[:, 1:2]).then_inc(am2, 1)
                    dve.tensor_scalar(unscale[:, i, 1:2], am[:, 1:2], g_127[:, 1:2], None, ALU.mult).then_inc(am2, 1)
                    dve.wait_ge(am2, 4 * i + 4)
                    dve.tensor_scalar(quant[:, 1:2], quant[:, 1:2], 127.0, None, ALU.mult).then_inc(fq_tmp, 1)
                    dve.wait_ge(fq_tmp, 2 * i + 1)
                    dve.tensor_scalar(f1[:], f1[:], quant[:, 1:2], ROUND, ALU.mult, ALU.add).then_inc(fq_tmp, 1)
                    dve.wait_ge(fq_tmp, 2 * i + 2)
                    dve.tensor_scalar(fq[:], f1[:], -ROUND, None, ALU.add).then_inc(fq_done, 1)

                def back3(i):
                    dve.wait_ge(ff2_psum, i + 1)
                    dve.scalar_tensor_tensor(f2[:], banks[7][:], unscale[:, i, 1:2], b2[:], ALU.mult, ALU.add).then_inc(f2_done, 1)
                    dve.wait_ge(f2_done, 2 * i + 2)
                    dve.tensor_tensor(f2[:], f2[:], x1[:, i, :], ALU.add).then_inc(f2_done, 1)

                def back4(i):
                    dve.wait_ge(rs2, 2 * i + 2)
                    dve.scalar_tensor_tensor(o2[:], f2[:], rs[:, 1:2], n2[:], ALU.mult, ALU.mult).then_inc(o2_done, 1)
                    dve.wait_ge(o2_done, i + 1)
                    dve.tensor_tensor(xres[:, i, :], xres[:, i, :], o2[:], ALU.add).then_inc(res_done, 1)
                front1(0)
                front2(0)
                with dve.Fori(1, NT) as i:
                    front1(i)
                    back1(i - 1)
                    front2(i)
                    back2(i - 1)
                    back3(i - 1)
                    back4(i - 1)
                back1(NT - 1)
                back2(NT - 1)
                back3(NT - 1)
                back4(NT - 1)

            @block.tensor
            def _(pe):
                pe.sem_inc(out_psum, 1)
                def out_product(i):
                    pe.wait_ge(y_lo_done, i + 1)
                    pe.wait_ge(xr_done, i + 1)
                    for k in range(GI):
                        last = mm3(pe, banks[0][:], y_hi[:, k], y_lo[:, k], wo_hi[:, k], wo_lo[:, k], k == 0, k == GI - 1)
                    last.then_inc(out_psum, 1)

                def turn_x(i):
                    pe.wait_ge(qx_done, i + 1)
                    pe.wait_ge(qxT_done, i + 1)
                    for k in range(KD):
                        last = pe.transpose(tq[:, k * P:(k + 1) * P], qx[:, k * P:(k + 1) * P], c["ident_b"][:])
                    last.then_inc(qxT_psum, 1)

                def ff1(i):
                    pe.wait_ge(qxT_done, i + 2)
                    for n in range(4):
                        pe.wait_ge(f1_done, 4 * i + 1)
                        for k in range(KD):
                            last = pe.matmul(banks[2 + n][:], qxT[:, k], w1q[:, k, n * 512:(n + 1) * 512],
                                             start=(k == 0), stop=(k == KD - 1))
                        last.then_inc(ff1_psum, 1)

                def turn_f(i):
                    pe.wait_ge(fq_done, i + 1)
                    for hf in range(2):
                        pe.wait_ge(fqT_done, 2 * i + hf + 1)
                        for k in range(KF // 2):
                            kk = hf * (KF // 2) + k
                            last = pe.transpose(tf[:, k * P:(k + 1) * P], fq[:, kk * P:(kk + 1) * P], c["ident_b"][:])
                        last.then_inc(fqT_psum, 1)

                def ff2(i):
                    pe.wait_ge(fqT_done, 2 * i + 3)
                    pe.wait_ge(f2_done, 2 * i + 1)
                    for k in range(KF):
                        last = pe.matmul(banks[7][:], fqT[:, k], w2q[:, k], start=(k == 0), stop=(k == KF - 1))
                    last.then_inc(ff2_psum, 1)
                out_product(0)
                turn_x(0)
                with pe.Fori(1, NT) as i:
                    out_product(i)
                    ff1(i - 1)
                    turn_x(i)
                    turn_f(i - 1)
                    ff2(i - 1)
                ff1(NT - 1)
                turn_f(NT - 1)
                ff2(NT - 1)


def experts(nc, sem, c, xres, banks, a, out):
    KI = EI // P
    PAIRS = E // 2
    outer = ExitStack()
    with outer:
        def sb(name, shape, dt):
            return outer.enter_context(nc.sbuf_tensor(name, shape, dt))
        gate_w = sb("gate_w", [P, KD, E], F32)
        gate_hi = sb("gate_hi", [P, KD, E], F32R)
        gate_lo = sb("gate_lo", [P, KD, E], F32R)
        gate_b = sb("gate_b", [P, E], F32)
        before4 = sb("before4", [P, 4, 4], F32)
        before16 = sb("before16", [P, E, E], F32)
        zero = sb("zero", [P, 512], BF16)
        stats = sb("e_stats", [P, TT, 6], F32)
        mv = sb("e_mv", [P, TT, 2], F32)
        rstd = sb("e_rstd", [P, TT], F32)
        xf = sb("xf", [P, TT, D], F32)
        xT_hi = sb("e_xT_hi", [P, KD, SEQ], F32R)
        xT_lo = sb("e_xT_lo", [P, KD, SEQ], F32R)
        up_stage = sb("up_stage", [P, 2, KD, 2 * EI], F32)
        up_hi = sb("up_hi", [P, 2, KD, 2 * EI], F32R)
        up_lo = sb("up_lo", [P, 2, KD, 2 * EI], F32R)
        dn_stage = sb("dn_stage", [P, 2, KI, D], F32)
        dn_hi = sb("dn_hi", [P, 2, KI, D], F32R)
        dn_lo = sb("dn_lo", [P, 2, KI, D], F32R)
        cwb = sb("cwb", [P, EALL, SEQ], F32)
        th = sb("e_th", [P, 2, SEQ], F32)
        ga = sb("ga", [P, 2, SEQ], F32)
        ub = sb("ub", [P, 2, SEQ], F32)
        ac = sb("ac", [P, 2, KI, SEQ], F32)
        ac_hi = sb("ac_hi", [P, 2, KI, SEQ], F32R)
        ac_lo = sb("ac_lo", [P, 2, KI, SEQ], F32R)
        prob = sb("prob", [P, TT, E], F32)
        sfc = sb("sfc", [P, TT, E], F32)
        pairs = sb("pairs", [P, 4, TT * 4], F32)
        grp = sb("grp", [P, TT, 4], F32)
        cmp = sb("cmp", [P, TT * E, E], F32)
        eqs = sb("eqs", [P, TT * E, E], F32)
        rank = sb("rank", [P, TT * E], F32)
        cw = sb("cw", [P, TT, E], F32)
        tot = sb("tot", [P, TT], F32)
        cwT_hi = sb("cwT_hi", [E, SEQ], F32R)
        cwT_lo = sb("cwT_lo", [E, SEQ], F32R)

        passed = sem("e_passed")
        gate_loaded, gate_cut, masks = sem("gate_loaded"), sem("gate_cut"), sem("masks")
        up_loaded = [sem("up_loaded0"), sem("up_loaded1")]
        dn_loaded = [sem("dn_loaded0"), sem("dn_loaded1")]
        up_hi_done, up_lo_done, dn_hi_done, dn_lo_done = sem("up_hi_done"), sem("up_lo_done"), sem("dn_hi_done"), sem("dn_lo_done")
        stats_done, mv_done, rstd_done, xf_done, xres_done = (sem("e_stats_done"), sem("e_mv_done"), sem("e_rstd_done"),
                                                              sem("xf_done"), sem("xres_done"))
        xT_psum, xT_hi_done, xT_lo_done = sem("e_xT_psum"), sem("e_xT_hi_done"), sem("e_xT_lo_done")
        logit_psum, elogit, route, cwT_psum, cwT_hi_done, cwT_lo_done = (
            sem("logit_psum"), sem("elogit"), sem("route"), sem("cwT_psum"), sem("cwT_hi_done"), sem("cwT_lo_done"))
        cwb_psum, cwb_act, cwb_dve = sem("cwb_psum"), sem("cwb_act"), sem("cwb_dve")
        up_psum, tanh_done, ga_done, gated = sem("up_psum"), sem("e_tanh_done"), sem("ga_done"), sem("gated")
        ub_done = sem("ub_done")
        ac_hi_done, ac_lo_done, dn_psum, y_psum, y_added, stored = (
            sem("ac_hi_done"), sem("ac_lo_done"), sem("dn_psum"), sem("e_y_psum"), sem("e_y_added"), sem("stored"))
        ROUTE = 28

        with nc.Block() as block:
            @block.sync
            def _(sp):
                sp.dma_start(gate_w[:], a["gate"]).then_inc(gate_loaded, 16)
                sp.dma_start(gate_b[:], a["gate_b"].to_broadcast([P, E])).then_inc(gate_loaded, 16)

                def load(b, e, r, free):
                    sp.wait_ge(up_lo_done, free + 1)
                    sp.dma_start(up_stage[:, r], a["up"][e]).then_inc(up_loaded[r], 16)
                    sp.wait_ge(dn_lo_done, free + 1)
                    sp.dma_start(dn_stage[:, r], a["down"][e]).then_inc(dn_loaded[r], 16)
                with sp.Fori(0, BATCH) as b:
                    for r in range(2):
                        load(b, r, r, b * EALL)
                    with sp.Fori(1, PAIRS + 1) as j:
                        for r in range(2):
                            load(b, 2 * j + r, r, b * EALL + 2 * j + r - 1)
                    sp.wait_ge(y_added, b * TT + TT + 1)
                    sp.dma_start(out[b].rearrange("(t p) d -> p t d", p=P), xres[:, bass.ds(b * TT, TT)]).then_inc(stored, 16)
                sp.wait_ge(stored, 16 * BATCH)

            @block.gpsimd
            def _(pool):
                pool.sem_inc(up_lo_done, 1)
                pool.sem_inc(dn_lo_done, 1)
                pool.memset(before4[:], 1.0).then_inc(masks, 1)
                pool.memset(before16[:], 1.0).then_inc(masks, 1)
                pool.wait_ge(masks, 2)
                pool.affine_select(out=before4[:], in_=before4[:], compare_op=ALU.is_gt, fill=0.0, base=0,
                                   pattern=[[1, 4], [-1, 4]], channel_multiplier=0).then_inc(masks, 1)
                pool.affine_select(out=before16[:], in_=before16[:], compare_op=ALU.is_gt, fill=0.0, base=0,
                                   pattern=[[1, E], [-1, E]], channel_multiplier=0).then_inc(masks, 1)
                pool.wait_ge(gate_cut, 1)
                pool.tensor_tensor(gate_lo[:], gate_w[:], gate_hi[:].bitcast(F32), ALU.subtract).then_inc(gate_cut, 1)
                with pool.Fori(0, BATCH) as b:
                    def cut(n, r):
                        pool.wait_ge(up_hi_done, n + 1)
                        pool.tensor_tensor(up_lo[:, r], up_stage[:, r], up_hi[:, r].bitcast(F32), ALU.subtract).then_inc(up_lo_done, 1)
                        pool.wait_ge(dn_hi_done, n + 1)
                        pool.tensor_tensor(dn_lo[:, r], dn_stage[:, r], dn_hi[:, r].bitcast(F32), ALU.subtract).then_inc(dn_lo_done, 1)

                    def cut_ac(n, r, i):
                        pool.wait_ge(ac_hi_done, n * KI + i + 1)
                        pool.tensor_tensor(ac_lo[:, r, i], ac[:, r, i], ac_hi[:, r, i].bitcast(F32), ALU.subtract).then_inc(ac_lo_done, 1)
                    hold(pool, mv_done, (b + 1) * TT, passed)
                    pool.tensor_scalar(rstd[:], mv[:, :, 1], LN_EPS, None, ALU.add).then_inc(rstd_done, 1)
                    pool.wait_ge(rstd_done, b * 2 + 1)
                    pool.tensor_tensor(rstd[:], rstd[:], c["minus_half"][:, 0:TT], ALU.pow).then_inc(rstd_done, 1)
                    n0 = b * EALL
                    cut(n0, 0)
                    cut(n0 + 1, 1)

                    def pair(j, more):
                        for r in range(2):
                            for i in range(KI):
                                cut_ac(n0 + 2 * j + r, r, i)
                        if more:
                            for r in range(2):
                                cut(n0 + 2 * j + r + 2, r)
                    with pool.Fori(0, PAIRS) as j:
                        pair(j, True)
                    pair(PAIRS, False)

            @block.scalar
            def _(act):
                act.wait_ge(gate_loaded, 32)
                act.copy(gate_hi[:], gate_w[:]).then_inc(gate_cut, 1)
                with act.Fori(0, BATCH) as b:
                    n0 = b * EALL

                    def cut_at(n, use, r, before):
                        act.wait_ge(up_loaded[r], (use + 1) * 16)
                        act.wait_ge(up_psum, before * KI + 1)
                        act.copy(up_hi[:, r], up_stage[:, r]).then_inc(up_hi_done, 1)
                        act.wait_ge(dn_loaded[r], (use + 1) * 16)
                        act.wait_ge(dn_psum, before + 1)
                        act.copy(dn_hi[:, r], dn_stage[:, r]).then_inc(dn_hi_done, 1)
                    for r in range(2):
                        cut_at(n0 + r, b * (EALL // 2), r, n0)
                    for t in range(TT):
                        act.wait_ge(xT_psum, b * TT + t + 1)
                        act.copy(xT_hi[:, :, t * P:(t + 1) * P],
                                 banks[t % 2][:].rearrange("p (k n) -> p k n", k=KD)).then_inc(xT_hi_done, 1)
                    act.wait_ge(logit_psum, b + 1)
                    act.activation(prob[:].rearrange("p t e -> p (t e)"), banks[2][:, 0:TT * E], ACT.Exp, scale=-1.0).then_inc(elogit, 1)
                    act.wait_ge(cwT_psum, b + 1)
                    act.copy(cwT_hi[:], banks[3][0:E, :]).then_inc(cwT_hi_done, 1)
                    for e in range(0, E, 2):
                        act.wait_ge(cwb_psum, b * E + e + 1)
                        act.copy(cwb[:, e], banks[e % 4][:]).then_inc(cwb_act, 1)

                    def tanh(n, i):
                        act.wait_ge(up_psum, n * KI + i + 2)
                        act.activation(th[:, i], banks[2 * i][:], ACT.Tanh, scale=0.5).then_inc(tanh_done, 1)

                    def cut_ac(n, r, i):
                        act.wait_ge(gated, n * KI + i + 1)
                        act.copy(ac_hi[:, r, i], ac[:, r, i]).then_inc(ac_hi_done, 1)

                    def pair(j, more):
                        for r in range(2):
                            n = n0 + 2 * j + r
                            for i in range(KI):
                                tanh(n, i)
                            for i in range(KI):
                                cut_ac(n, r, i)
                        if more:
                            for r in range(2):
                                n = n0 + 2 * j + r
                                cut_at(n + 2, b * (EALL // 2) + j + 1, r, n + 1)
                    with act.Fori(0, PAIRS) as j:
                        pair(j, True)
                    pair(PAIRS, False)

            @block.vector
            def _(dve):
                dve.sem_inc(y_added, 1)
                dve.memset(zero[:], 0.0).then_inc(ub_done, 1)
                dve.memset(cwb[:, E:EALL], 0.5).then_inc(ub_done, 1)
                dve.wait_ge(gate_loaded, 32)
                dve.wait_ge(masks, 4)
                with dve.Fori(0, BATCH) as b:
                    n0 = b * EALL
                    for t in range(TT):
                        dve.bn_stats(stats[:, t, :], xres[:, b * TT + t, :]).then_inc(stats_done, 1)
                    for t in range(TT):
                        hold(dve, stats_done, b * TT + t + 1, passed)
                        dve.bn_aggr(mv[:, t, :], stats[:, t, :]).then_inc(mv_done, 1)
                    dve.wait_ge(rstd_done, b * 2 + 2)
                    for t in range(TT):
                        dve.tensor_scalar(xf[:, t, :], xres[:, b * TT + t, :], mv[:, t, 0:1], rstd[:, t:t + 1],
                                          ALU.subtract, ALU.mult).then_inc(xf_done, 1)
                    for t in range(TT):
                        dve.wait_ge(xT_hi_done, b * TT + t + 1)
                        s = slice(t * P, (t + 1) * P)
                        dve.tensor_tensor(xT_lo[:, :, s], banks[t % 2][:].rearrange("p (k n) -> p k n", k=KD),
                                          xT_hi[:, :, s].bitcast(F32), ALU.subtract).then_inc(xT_lo_done, 1)
                    for t in range(TT):
                        dve.wait_ge(xf_done, b * TT + t + 1)
                        dve.tensor_tensor(xres[:, b * TT + t, :], xres[:, b * TT + t, :], xf[:, t, :], ALU.add).then_inc(xres_done, 1)

                    steps = [0]

                    def step(instruction):
                        steps[0] += 1
                        instruction.then_inc(route, 1)
                        dve.wait_ge(route, b * ROUTE + steps[0])
                    dve.wait_ge(elogit, b + 1)
                    step(dve.tensor_scalar(prob[:], prob[:], 1.0, None, ALU.add))
                    step(dve.reciprocal(prob[:], prob[:]))
                    step(dve.tensor_tensor(sfc[:], prob[:], bc_mid(gate_b[:], TT), ALU.add))
                    f = sfc[:].rearrange("p t (g e) -> p (t g) e", e=4)
                    step(dve.tensor_tensor(pairs[:, 0], f[:, :, 0], f[:, :, 1], ALU.max))
                    step(dve.tensor_tensor(pairs[:, 1], f[:, :, 2], f[:, :, 3], ALU.max))
                    step(dve.tensor_tensor(pairs[:, 2], f[:, :, 0], f[:, :, 1], ALU.add))
                    step(dve.tensor_tensor(pairs[:, 3], f[:, :, 2], f[:, :, 3], ALU.add))
                    step(dve.tensor_tensor(pairs[:, 0], pairs[:, 0], pairs[:, 1], ALU.add))
                    step(dve.tensor_tensor(pairs[:, 2], pairs[:, 2], pairs[:, 3], ALU.max))
                    step(dve.tensor_tensor(grp[:].rearrange("p t g -> p (t g)"), pairs[:, 0], pairs[:, 2], ALU.max))

                    def ranks(v, n, before):
                        full = [P, TT, n, n]
                        other = v.unsqueeze(2).to_broadcast(full)
                        own = v.unsqueeze(3).to_broadcast(full)
                        gt = cmp[:, 0:TT * n, 0:n].rearrange("p (t x) y -> p t x y", t=TT)
                        eq = eqs[:, 0:TT * n, 0:n].rearrange("p (t x) y -> p t x y", t=TT)
                        step(dve.tensor_tensor(gt, other, own, ALU.is_gt))
                        step(dve.tensor_tensor(eq, other, own, ALU.is_equal))
                        step(dve.tensor_tensor(eq, eq, before.unsqueeze(1).to_broadcast(full), ALU.mult))
                        step(dve.tensor_tensor(gt, gt, eq, ALU.add))
                        step(dve.tensor_reduce(rank[:, 0:TT * n], cmp[:, 0:TT * n, 0:n], AX.X, ALU.add))
                    ranks(grp[:], 4, before4[:])
                    step(dve.tensor_scalar(rank[:, 0:TT * 4], rank[:, 0:TT * 4], 2.0, BIG, ALU.is_lt, ALU.mult))
                    step(dve.tensor_scalar(rank[:, 0:TT * 4], rank[:, 0:TT * 4], -BIG, None, ALU.add))
                    step(dve.tensor_tensor(f, f, bc_free(rank[:, 0:TT * 4], 4), ALU.add))
                    ranks(sfc[:], E, before16[:])
                    r = rank[:].rearrange("p (t e) -> p t e", t=TT)
                    step(dve.scalar_tensor_tensor(cw[:], r, 4.0, prob[:], ALU.is_lt, ALU.mult))
                    step(dve.reduce_sum(tot[:], cw[:], AX.X))
                    step(dve.tensor_scalar(tot[:], tot[:], 1e-20, None, ALU.add))
                    step(dve.reciprocal(tot[:], tot[:]))
                    step(dve.scalar_tensor_tensor(cw[:], cw[:], 1.25, bc_free(tot[:], E), ALU.mult, ALU.mult))
                    assert steps[0] == ROUTE, steps[0]
                    dve.wait_ge(cwT_hi_done, b + 1)
                    dve.tensor_tensor(cwT_lo[:], banks[3][0:E, :], cwT_hi[:].bitcast(F32), ALU.subtract).then_inc(cwT_lo_done, 1)
                    for e in range(1, E, 2):
                        dve.wait_ge(cwb_psum, b * E + e + 1)
                        dve.tensor_copy(cwb[:, e], banks[e % 4][:]).then_inc(cwb_dve, 1)
                    hold(dve, cwb_act, b * (E // 2) + E // 2, passed)
                    hold(dve, cwb_dve, b * (E // 2) + E // 2, passed)

                    def pair(j):
                        for r in range(2):
                            n = n0 + 2 * j + r
                            for i in range(KI):
                                m = n * KI + i
                                dve.wait_ge(tanh_done, m + 1)
                                dve.scalar_tensor_tensor(ga[:, i], th[:, i], 1.0, banks[2 * i][:], ALU.add,
                                                         ALU.mult).then_inc(ga_done, 1)
                                dve.tensor_tensor(ub[:, i], banks[2 * i + 1][:], cwb[:, 2 * j + r], ALU.mult).then_inc(ub_done, 1)
                                dve.wait_ge(ga_done, m + 1)
                                dve.wait_ge(ub_done, m + 3)
                                dve.tensor_tensor(ac[:, r, i], ga[:, i], ub[:, i], ALU.mult).then_inc(gated, 1)
                    with dve.Fori(0, PAIRS) as j:
                        pair(j)
                    pair(PAIRS)
                    dve.wait_ge(y_psum, b + 1)
                    for t in range(TT):
                        dve.tensor_tensor(xres[:, b * TT + t, :], xres[:, b * TT + t, :], banks[4 + t][:], ALU.add).then_inc(y_added, 1)

            @block.tensor
            def _(pe):
                pe.sem_inc(up_psum, 1)
                pe.sem_inc(dn_psum, 1)
                pe.wait_ge(ub_done, 2)
                with pe.Fori(0, BATCH) as b:
                    n0 = b * EALL
                    for t in range(TT):
                        pe.wait_ge(xf_done, b * TT + t + 1)
                        if t >= 2:
                            pe.wait_ge(xT_lo_done, b * TT + t - 1)
                        for k in range(KD):
                            last = pe.transpose(banks[t % 2][:, k * P:(k + 1) * P], xf[:, t, k * P:(k + 1) * P], c["ident"][:])
                        last.then_inc(xT_psum, 1)
                    pe.wait_ge(xT_lo_done, b * TT + TT)
                    pe.wait_ge(gate_cut, 2)
                    for t in range(TT):
                        s = slice(t * P, (t + 1) * P)
                        for k in range(KD):
                            last = mm3(pe, banks[2][:, t * E:(t + 1) * E], xT_hi[:, k, s], xT_lo[:, k, s], gate_hi[:, k],
                                       gate_lo[:, k], k == 0, k == KD - 1)
                    last.then_inc(logit_psum, 1)
                    pe.wait_ge(route, b * ROUTE + ROUTE)
                    for t in range(TT):
                        last = pe.transpose(banks[3][0:E, t * P:(t + 1) * P], cw[:, t, :], c["ident"][:])
                    last.then_inc(cwT_psum, 1)
                    pe.wait_ge(cwT_lo_done, b + 1)
                    for e in range(E):
                        if e >= 4:
                            pe.wait_ge(cwb_dve if e % 2 else cwb_act, b * (E // 2) + (e - 4) // 2 + 1)
                        pick = c["ident_r"][0:E, e:e + 1].to_broadcast([E, P])
                        pe.matmul(banks[e % 4][:], pick, cwT_hi[:], start=True, stop=False)
                        pe.matmul(banks[e % 4][:], pick, cwT_lo[:], start=False, stop=True).then_inc(cwb_psum, 1)
                    pe.wait_ge(cwb_act, b * (E // 2) + E // 2)
                    pe.wait_ge(cwb_dve, b * (E // 2) + E // 2)
                    pe.wait_ge(y_added, b * TT + 1)
                    for t in range(TT):
                        pe.matmul(banks[4 + t][:], zero[:, 0:P], zero[:], start=True, stop=False)

                    def up(n, r):
                        pe.wait_ge(up_lo_done, n + 2)
                        for i in range(KI):
                            pe.wait_ge(ub_done, n * KI + i + 1)
                            for half in range(2):
                                s = slice(half * EI + i * P, half * EI + (i + 1) * P)
                                for k in range(KD):
                                    last = mm3(pe, banks[2 * i + half][:], up_hi[:, r, k, s], up_lo[:, r, k, s], xT_hi[:, k],
                                               xT_lo[:, k], k == 0, k == KD - 1)
                            last.then_inc(up_psum, 1)

                    def down(n, r):
                        pe.wait_ge(ac_lo_done, (n + 1) * KI)
                        pe.wait_ge(dn_lo_done, n + 2)
                        for t in range(TT):
                            s = slice(t * P, (t + 1) * P)
                            for i in range(KI):
                                last = mm3(pe, banks[4 + t][:], ac_hi[:, r, i, s], ac_lo[:, r, i, s], dn_hi[:, r, i],
                                           dn_lo[:, r, i], False, False)
                        last.then_inc(dn_psum, 1)

                    def pair(j):
                        up(n0 + 2 * j, 0)
                        up(n0 + 2 * j + 1, 1)
                        down(n0 + 2 * j, 0)
                        down(n0 + 2 * j + 1, 1)
                    with pe.Fori(0, PAIRS) as j:
                        pair(j)
                    pair(PAIRS)
                    for t in range(TT):
                        last = pe.matmul(banks[4 + t][:], zero[:, 0:P], zero[:], start=False, stop=True)
                    last.then_inc(y_psum, 1)


def store(nc, sem, xres, out):
    stored = sem("stored")
    with nc.Block() as block:
        @block.sync
        def _(sp):
            sp.dma_start(out.rearrange("b (t p) d -> p (b t) d", p=P), xres[:]).then_inc(stored, 16)
            sp.wait_ge(stored, 16)


def load_only(nc, sem, xres, a):
    loaded = sem("x_only")
    with nc.Block() as block:
        @block.sync
        def _(sp):
            sp.dma_start(xres[:], a["x"].rearrange("b (t p) d -> p (b t) d", p=P)).then_inc(loaded, 16)
            sp.wait_ge(loaded, 16)


def dump(nc, sem, yT, out):
    d = nc.dram_tensor("dump", (P, GI, BATCH * SEQ), F32, kind="ExternalOutput").ap()
    dumped = sem("dumped")
    with nc.Block() as block:
        @block.sync
        def _(sp):
            sp.dma_start(d, yT[:]).then_inc(dumped, 16)
            sp.wait_ge(dumped, 16)


def stage_semaphores(nc, stage):
    taken = []

    def sem(name):
        taken.append(nc.alloc_semaphore(name=name))
        return taken[-1]
    stage(sem)
    nc.clear_and_free_semaphores(taken)
    nc.all_engine_barrier()


def build(nc, a, out, stages=("attention", "mamba", "moe")):
    ctx = ExitStack()
    with ctx:
        def sb(name, shape, dt):
            return ctx.enter_context(nc.sbuf_tensor(name, shape, dt))
        xres = sb("xres", [P, NT, D], F32)
        banks = [ctx.enter_context(nc.psum_tensor(f"bank{i}", [P, 512], F32)) for i in range(8)]
        c = {}
        stage_semaphores(nc, lambda sem: constants(nc, sb, sem, c))
        if "attention" in stages:
            stage_semaphores(nc, lambda sem: attention(nc, sem, c, xres, banks, a, True))
        else:
            stage_semaphores(nc, lambda sem: load_only(nc, sem, xres, a))
        if "mamba" in stages:
            with ExitStack() as mid:
                ln_mv = mid.enter_context(nc.sbuf_tensor("ln_mv", [P, NT, 2], F32))
                ln_rstd = mid.enter_context(nc.sbuf_tensor("ln_rstd", [P, NT], F32))
                yT = mid.enter_context(nc.sbuf_tensor("yT", [P, GI, BATCH * SEQ], F32))
                stage_semaphores(nc, lambda sem: mamba_scan(nc, sem, c, xres, banks, a, ln_mv, ln_rstd, yT))
                stage_semaphores(nc, lambda sem: feed_forward(nc, sem, c, xres, banks, a, ln_mv, ln_rstd, yT))
        if "moe" in stages:
            stage_semaphores(nc, lambda sem: experts(nc, sem, c, xres, banks, a, out))
        else:
            stage_semaphores(nc, lambda sem: store(nc, sem, xres, out))


def layout(np, i):
    T = np.transpose
    wg = np.concatenate([i["L0_ffn_Wg"], np.reshape(i["L0_ffn_Ws_g"], (2, EI, D))])
    wu = np.concatenate([i["L0_ffn_Wu"], np.reshape(i["L0_ffn_Ws_u"], (2, EI, D))])
    wd = np.concatenate([T(i["L0_ffn_Wd"], (0, 2, 1)), np.reshape(T(i["L0_ffn_Ws_d"]), (2, EI, D))])
    up = np.concatenate([wg, wu], axis=1)
    return {
        "x": i["x"],
        "ctxT": T(i["ctx_1024"][:, :SEQ], (0, 2, 1)),
        "wq": T(i["L0_xattn_Wq"]), "wk": T(i["L0_xattn_Wk"]), "wv": T(i["L0_xattn_Wv"]), "wo": T(i["L0_xattn_Wo"]),
        "w_in": T(np.reshape(i["L0_attn_w_in"], (2 * GI, P, KD, P)), (0, 3, 2, 1)),
        "conv_w": T(np.reshape(i["L0_attn_conv_w"], (GI, P, 4)), (1, 0, 2)),
        "conv_b": T(np.reshape(i["L0_attn_conv_b"], (GI, P))),
        "w_xproj": T(np.reshape(i["L0_attn_w_xproj"], (DR + 2 * NS, GI, P)), (2, 1, 0)),
        "w_dt": T(i["L0_attn_w_dt"]),
        "b_dt": T(np.reshape(i["L0_attn_b_dt"], (GI, P))),
        "A_log": T(np.reshape(i["L0_attn_A_log"], (GI, P, NS)), (1, 0, 2)),
        "Dp": T(np.reshape(i["L0_attn_Dp"], (GI, P))),
        "w_out": T(np.reshape(i["L0_attn_w_out"], (D, GI, P)), (2, 1, 0)),
        "n1": np.reshape(i["L0_attn_norm1_w"], (1, D)), "n2": np.reshape(i["L0_attn_norm2_w"], (1, D)),
        "w1": T(np.reshape(i["L0_attn_ffn_w1"], (FF, KD, P)), (2, 1, 0)),
        "b1": np.reshape(i["L0_attn_ffn_b1"], (1, FF)),
        "w2": T(np.reshape(i["L0_attn_ffn_w2"], (D, FF // P, P)), (2, 1, 0)),
        "b2": np.reshape(i["L0_attn_ffn_b2"], (1, D)),
        "gate": T(np.reshape(i["L0_ffn_gate_w"], (E, KD, P)), (2, 1, 0)),
        "gate_b": np.reshape(i["L0_ffn_gate_bias"], (1, E)),
        "up": T(np.reshape(up, (EALL, 2 * EI, KD, P)), (0, 3, 2, 1)),
        "down": T(np.reshape(wd, (EALL, EI // P, P, D)), (0, 2, 1, 3)),
    }


def kernel(**inputs):
    import numpy as np
    import concourse.bacc as bacc
    from concourse.bass_utils import run_bass_kernel_spmd

    nc = bacc.Bacc("TRN2", target_bir_lowering=False, num_devices=1)
    arrays, aps = {}, {}
    for name, array in layout(np, inputs).items():
        array = np.ascontiguousarray(array)
        arrays[f"in_{name}"] = array
        aps[name] = nc.dram_tensor(f"in_{name}", array.shape, F32, kind="ExternalInput").ap()
    out = nc.dram_tensor("out_x", (BATCH, SEQ, D), F32, kind="ExternalOutput").ap()
    build(nc, aps, out)
    result = run_bass_kernel_spmd(nc, [arrays], core_ids=[0])
    return result.results[0]["out_x"]
```

```python
import concourse.bass as bass
from concourse import mybir
from contextlib import ExitStack

F32 = mybir.dt.float32
F32R = mybir.dt.float32r
BF16 = mybir.dt.bfloat16
ALU = mybir.AluOpType
ACT = mybir.ActivationFunctionType
AX = mybir.AxisListType

P = 128
BATCH, SEQ, D = 2, 512, 512
TT = SEQ // P
NT = BATCH * TT
KD = D // P
HEADS, HD = 16, 32
HG = HEADS // 4
DI, NS, DR = 1024, 16, 64
GI = DI // P
FF = 2048
E, EI = 16, 256
EALL = E + 2
LN_EPS, RMS_EPS = 1e-5, 1e-6
ROUND = 12582912.0
BIG = 1e30


def mm3(pe, out, lhs_hi, lhs_lo, rhs_hi, rhs_lo, start, stop):
    pe.matmul(out, lhs_hi, rhs_hi, start=start, stop=False)
    pe.matmul(out, lhs_hi, rhs_lo, start=False, stop=False)
    return pe.matmul(out, lhs_lo, rhs_hi, start=False, stop=stop)


def bc_free(ap, n):
    return ap.unsqueeze(2).to_broadcast([ap.shape[0], ap.shape[1], n])


def bc_mid(ap, n):
    return ap.unsqueeze(1).to_broadcast([ap.shape[0], n, ap.shape[1]])


def hold(eng, sem, value, passed):
    eng.wait_ge(sem, value)
    eng.sem_inc(passed, 1)


def constants(nc, sb, sem, c):
    c["ident"] = sb("ident", [P, P], F32)
    c["ident_r"] = sb("ident_r", [P, P], F32R)
    c["ident_b"] = sb("ident_b", [P, P], BF16)
    c["mask"] = sb("mask", [P, P], F32)
    c["minus_half"] = sb("minus_half", [P, 8], F32)
    c["ones"] = sb("ones", [P, P], F32)
    set_done = sem("constants_set")
    made = sem("constants_made")
    with nc.Block() as block:
        @block.gpsimd
        def _(pool):
            pool.memset(c["ident"][:], 0.0).then_inc(set_done, 1)
            pool.memset(c["mask"][:], 0.0).then_inc(set_done, 1)
            pool.memset(c["minus_half"][:], -0.5).then_inc(made, 1)
            pool.memset(c["ones"][:], 1.0).then_inc(made, 1)
            pool.wait_ge(set_done, 2)
            pool.affine_select(out=c["ident"][:], in_=c["ident"][:], compare_op=ALU.not_equal, fill=1.0,
                               base=0, pattern=[[-1, P]], channel_multiplier=1).then_inc(set_done, 1)
            pool.affine_select(out=c["mask"][:], in_=c["mask"][:], compare_op=ALU.is_ge, fill=-BIG,
                               base=0, pattern=[[-1, P]], channel_multiplier=1).then_inc(made, 1)
            pool.wait_ge(set_done, 3)
            pool.tensor_copy(c["ident_r"][:], c["ident"][:]).then_inc(made, 1)
            pool.tensor_copy(c["ident_b"][:], c["ident"][:]).then_inc(made, 1)
            pool.wait_ge(made, 5)


def attention(nc, sem, c, xres, banks, a, load_x):
    scale = float(HD) ** -0.5
    U = TT * HEADS
    STEPS = U + 8
    ctx = ExitStack()
    with ctx:
        def sb(name, shape, dt):
            return ctx.enter_context(nc.sbuf_tensor(name, shape, dt))
        stage = sb("a_stage", [P, 2, KD, D], F32)
        w_hi = sb("w_hi", [P, 4, KD, D], F32R)
        w_lo = sb("w_lo", [P, 4, KD, D], F32R)
        c_hi = sb("c_hi", [P, KD, SEQ], F32R)
        c_lo = sb("c_lo", [P, KD, SEQ], F32R)
        stats = sb("stats", [P, TT, 6], F32)
        mv = sb("mv", [P, TT, 2], F32)
        rstd = sb("rstd", [P, TT], F32)
        rows = sb("rows", [P, TT, D], F32)
        xT_hi = sb("xT_hi", [P, KD, SEQ], F32R)
        xT_lo = sb("xT_lo", [P, KD, SEQ], F32R)
        q_pad = sb("q_pad", [P, HEADS, SEQ], F32)
        kT = sb("kT", [P, KD, SEQ], F32)
        v = sb("v", [P, TT, D], F32)
        probs = sb("probs", [P, 4, SEQ], F32)
        probsT = sb("probsT", [P, 2, TT, P], F32)
        mask = sb("a_mask", [P, SEQ], F32)
        neg_max = sb("neg_max", [P, 4], F32)
        row_sum = sb("row_sum", [P, 4], F32)
        inv_sum = sb("inv_sum", [P, 4], F32)
        oT_hi = sb("oT_hi", [P, KD, P], F32R)
        oT_lo = sb("oT_lo", [P, KD, P], F32R)

        passed = sem("passed")
        x_loaded = sem("x_loaded")
        staged = [sem("staged0"), sem("staged1")]
        hi_done = sem("a_hi_done")
        cut = sem("a_cut")
        mask_done = sem("a_mask_done")
        zeroed = sem("q_zeroed")
        stats_done = sem("a_stats")
        mv_done = sem("a_mv")
        rstd_done = sem("a_rstd")
        xn_done = sem("a_xn")
        xT_psum = sem("a_xT_psum")
        xT_hi_done = sem("a_xT_hi")
        xT_lo_done = sem("a_xT_lo")
        proj_psum = sem("proj_psum")
        proj_act = sem("proj_act")
        proj_dve = sem("proj_dve")
        scores = sem("scores")
        max_done = sem("max_done")
        exp_done = sem("exp_done")
        inv_done = sem("inv_done")
        norm_done = sem("norm_done")
        pT_psum = sem("pT_psum")
        pT_act = sem("pT_act")
        pT_dve = sem("pT_dve")
        pv_done = sem("pv_done")
        oT_hi_done = sem("oT_hi_done")
        oT_lo_done = sem("oT_lo_done")
        y_psum = sem("y_psum")
        y_added = sem("y_added")

        ITEMS = ("ctx0", "wk", "wv", "wq", "wo", "ctx1")
        ON_ACT = 4
        WEIGHTS = {"wq": 0, "wk": 1, "wv": 2, "wo": 3}
        PIECES = KD * 2 + 4

        def width(u):
            return (u // HEADS + 1) * P

        def on_act(u):
            return u % 5 in (1, 3)

        def taken(u):
            mine = [x for x in range(U) if on_act(x) == on_act(u)]
            return (pT_act if on_act(u) else pT_dve), len(mine), mine.index(u) + 1

        def take_pT(eng, copy, u, b):
            sem_, per, _ = taken(u)
            eng.wait_ge(pT_psum, b * U + u + 1)
            if u >= 2:
                eng.wait_ge(pv_done, b * U + u - 1)
            n = width(u)
            copy(probsT[:, u % 2].rearrange("p k n -> p (k n)")[:, 0:n], banks[3 + u % 2][:, 0:n]).then_inc(sem_, 1)

        with nc.Block() as block:
            @block.sync
            def _(sp):
                if load_x:
                    sp.dma_start(xres[:, 0:TT], a["x"][0].rearrange("(t p) d -> p t d", p=P)).then_inc(x_loaded, 16)
                for i, name in enumerate(ITEMS):
                    if i == 3 and load_x:
                        sp.wait_ge(x_loaded, 16)
                        sp.dma_start(xres[:, TT:NT], a["x"][1].rearrange("(t p) d -> p t d", p=P)).then_inc(x_loaded, 16)
                    if i >= 2:
                        sp.wait_ge(cut, i - 1)
                    src = a[name] if name in WEIGHTS else a["ctxT"][int(name[3:])]
                    sp.dma_start(stage[:, i % 2], src.rearrange("(k p) n -> p k n", p=P)).then_inc(staged[i % 2], 16)

            @block.gpsimd
            def _(pool):
                pool.memset(mask[:, 0:SEQ - P], 0.0).then_inc(mask_done, 1)
                pool.tensor_copy(mask[:, SEQ - P:SEQ], c["mask"][:]).then_inc(mask_done, 1)

                def rms(b):
                    pool.wait_ge(mv_done, (b + 1) * TT)
                    pool.tensor_scalar(rstd[:], mv[:, :, 1], LN_EPS, None, ALU.add).then_inc(rstd_done, 1)
                    pool.wait_ge(rstd_done, b * 2 + 1)
                    pool.tensor_tensor(rstd[:], rstd[:], c["minus_half"][:, 0:TT], ALU.pow).then_inc(rstd_done, 1)

                def cut_item(i):
                    name = ITEMS[i]
                    hi, lo = (w_hi[:, WEIGHTS[name]], w_lo[:, WEIGHTS[name]]) if name in WEIGHTS else (c_hi[:], c_lo[:])
                    pool.wait_ge(staged[i % 2], 16 * (i // 2 + 1))
                    if name == "ctx1":
                        pool.wait_ge(proj_psum, 8)
                    if i >= ON_ACT:
                        pool.tensor_copy(hi, stage[:, i % 2]).then_inc(hi_done, 1)
                    pool.wait_ge(hi_done, i + 1)
                    pool.tensor_tensor(lo, stage[:, i % 2], hi.bitcast(F32), ALU.subtract).then_inc(cut, 1)
                cut_item(0)
                rms(0)
                for i in range(1, 6):
                    cut_item(i)
                for b in range(1, BATCH):
                    rms(b)

            @block.scalar
            def _(act):
                for i in range(ON_ACT):
                    hi = w_hi[:, WEIGHTS[ITEMS[i]]] if ITEMS[i] in WEIGHTS else c_hi[:]
                    act.wait_ge(staged[i % 2], 16 * (i // 2 + 1))
                    act.copy(hi, stage[:, i % 2]).then_inc(hi_done, 1)
                with act.Fori(0, BATCH) as b:
                    for j in range(12):
                        what, n = divmod(j, 4)
                        for t in range(TT if j == 8 else 0):
                            act.wait_ge(xT_psum, b * TT + t + 1)
                            act.copy(xT_hi[:, :, t * P:(t + 1) * P],
                                     banks[4 + t % 2][:].rearrange("p (k n) -> p k n", k=KD)).then_inc(xT_hi_done, 1)
                        if what == 2 or j % 2 == 0:
                            act.wait_ge(proj_psum, b * 12 + j + 1)
                        if what == 2:
                            if j == 8:
                                act.wait_ge(zeroed, 1)
                            for h in range(2):
                                r = slice(HD * h, HD * (h + 1))
                                act.copy(q_pad[r, 4 * n + h], banks[j % 4][r, :]).then_inc(proj_act, 1)
                        elif j % 2 == 0:
                            act.copy((kT, v)[what][:, n], banks[j % 4][:]).then_inc(proj_act, 1)
                    for i in range(STEPS):
                        if i < U:
                            act.wait_ge(max_done, b * U + i + 1)
                            if i >= 4:
                                act.wait_ge(pT_psum, b * U + i - 3)
                            act.activation(probs[:, i % 4, 0:width(i)], rows[:, i % 4, 0:width(i)], ACT.Exp,
                                           bias=neg_max[:, i % 4:i % 4 + 1], scale=-1.0,
                                           accum_out=row_sum[:, i % 4:i % 4 + 1]).then_inc(exp_done, 1)
                        u = i - 3
                        if 0 <= u < U and on_act(u):
                            take_pT(act, act.copy, u, b)
                        if i >= 20 and (i - 20) % HEADS == 0:
                            qt = (i - 20) // HEADS
                            act.wait_ge(pv_done, b * U + (qt + 1) * HEADS)
                            if qt > 0:
                                act.wait_ge(y_psum, b * TT + qt)
                            act.copy(oT_hi[:], banks[5 + qt % 2][:].rearrange("p (k n) -> p k n", k=KD)).then_inc(oT_hi_done, 1)

            @block.vector
            def _(dve):
                dve.memset(q_pad[:], 0.0).then_inc(zeroed, 1)
                dve.wait_ge(mask_done, 2)
                with dve.Fori(0, BATCH) as b:
                    if load_x:
                        hold(dve, x_loaded, b * 16 + 16, passed)
                    for t in range(TT):
                        dve.bn_stats(stats[:, t, :], xres[:, b * TT + t, :]).then_inc(stats_done, 1)
                    for t in range(TT):
                        hold(dve, stats_done, b * TT + t + 1, passed)
                        dve.bn_aggr(mv[:, t, :], stats[:, t, :]).then_inc(mv_done, 1)
                    dve.wait_ge(rstd_done, b * 2 + 2)
                    for t in range(TT):
                        dve.tensor_scalar(rows[:, t, :], xres[:, b * TT + t, :], mv[:, t, 0:1], rstd[:, t:t + 1],
                                          ALU.subtract, ALU.mult).then_inc(xn_done, 1)
                    dve.wait_ge(zeroed, 1)
                    for j in range(12):
                        what, n = divmod(j, 4)
                        for t in range(TT if j == 8 else 0):
                            dve.wait_ge(xT_hi_done, b * TT + t + 1)
                            s = slice(t * P, (t + 1) * P)
                            dve.tensor_tensor(xT_lo[:, :, s], banks[4 + t % 2][:].rearrange("p (k n) -> p k n", k=KD),
                                              xT_hi[:, :, s].bitcast(F32), ALU.subtract).then_inc(xT_lo_done, 1)
                        if what == 2 or j % 2:
                            dve.wait_ge(proj_psum, b * 12 + j + 1)
                        if what == 2:
                            for h in range(2, 4):
                                r = slice(HD * h, HD * (h + 1))
                                dve.tensor_copy(q_pad[r, 4 * n + h], banks[j % 4][r, :]).then_inc(proj_dve, 1)
                        elif j % 2:
                            dve.tensor_copy((kT, v)[what][:, n], banks[j % 4][:]).then_inc(proj_dve, 1)
                    for i in range(STEPS):
                        if 0 <= i - 2 < U:
                            u = i - 2
                            dve.wait_ge(exp_done, b * U + u + 1)
                            dve.reciprocal(inv_sum[:, u % 4:u % 4 + 1], row_sum[:, u % 4:u % 4 + 1]).then_inc(inv_done, 1)
                        if i < U:
                            hold(dve, scores, b * U + i + 1, passed)
                            dve.tensor_tensor_reduce(out=rows[:, i % 4, 0:width(i)], in0=banks[i % 3][:, 0:width(i)],
                                                     in1=mask[:, SEQ - width(i):SEQ], scale=-scale, scalar=3e38,
                                                     op0=ALU.add, op1=ALU.min,
                                                     accum_out=neg_max[:, i % 4:i % 4 + 1]).then_inc(max_done, 1)
                        if 0 <= i - 2 < U:
                            u = i - 2
                            dve.wait_ge(inv_done, b * U + u + 1)
                            dve.tensor_scalar(probs[:, u % 4, 0:width(u)], probs[:, u % 4, 0:width(u)],
                                              inv_sum[:, u % 4:u % 4 + 1], None, ALU.mult).then_inc(norm_done, 1)
                        u = i - 3
                        if 0 <= u < U and not on_act(u):
                            take_pT(dve, dve.tensor_copy, u, b)
                        if i >= 20 and (i - 20) % HEADS == 0:
                            qt = (i - 20) // HEADS
                            dve.wait_ge(oT_hi_done, b * TT + qt + 1)
                            dve.tensor_tensor(oT_lo[:], banks[5 + qt % 2][:].rearrange("p (k n) -> p k n", k=KD),
                                              oT_hi[:].bitcast(F32), ALU.subtract).then_inc(oT_lo_done, 1)
                        if i >= 23 and (i - 23) % HEADS == 0:
                            qt = (i - 23) // HEADS
                            dve.wait_ge(y_psum, b * TT + qt + 1)
                            dve.tensor_tensor(xres[:, b * TT + qt, :], xres[:, b * TT + qt, :], banks[7][:],
                                              ALU.add).then_inc(y_added, 1)

            @block.tensor
            def _(pe):
                with pe.Fori(0, BATCH) as b:
                    def turn_rows():
                        for t in range(TT):
                            pe.wait_ge(xn_done, b * TT + t + 1)
                            if t >= 2:
                                pe.wait_ge(xT_lo_done, b * TT + t - 1)
                            for k in range(KD):
                                last = pe.transpose(banks[4 + t % 2][:, k * P:(k + 1) * P], rows[:, t, k * P:(k + 1) * P],
                                                    c["ident"][:])
                            last.then_inc(xT_psum, 1)
                    for j in range(12):
                        what, n = divmod(j, 4)
                        if j >= 4:
                            pe.wait_ge(proj_dve if j % 2 else proj_act, b * PIECES + (j - 4) // 2 + 1)
                        if j == 0:
                            pe.wait_ge(cut, b * 4 + 2)
                        if j == 4:
                            pe.wait_ge(cut, 3)
                        if j == 8:
                            turn_rows()
                            pe.wait_ge(cut, 4)
                            pe.wait_ge(xT_lo_done, b * TT + TT)
                        s = slice(n * P, (n + 1) * P)
                        for k in range(KD):
                            if what == 2:
                                ops = (w_hi[:, 0, k, s], w_lo[:, 0, k, s], xT_hi[:, k], xT_lo[:, k])
                            elif what == 0:
                                ops = (w_hi[:, 1, k, s], w_lo[:, 1, k, s], c_hi[:, k], c_lo[:, k])
                            else:
                                ops = (c_hi[:, k, s], c_lo[:, k, s], w_hi[:, 2, k], w_lo[:, 2, k])
                            last = mm3(pe, banks[j % 4][:], *ops, k == 0, k == KD - 1)
                        last.then_inc(proj_psum, 1)
                    pe.wait_ge(proj_act, b * PIECES + PIECES)
                    pe.wait_ge(proj_dve, b * PIECES + PIECES)

                    for i in range(STEPS):
                        if i < U:
                            qt, head = divmod(i, HEADS)
                            if i >= 3:
                                pe.wait_ge(max_done, b * U + i - 2)
                            pe.matmul(banks[i % 3][:, 0:width(i)], q_pad[:, head, qt * P:(qt + 1) * P],
                                      kT[:, head // 4, 0:width(i)], start=True, stop=True).then_inc(scores, 1)
                        if 0 <= i - 3 < U:
                            u = i - 3
                            pe.wait_ge(norm_done, b * U + u + 1)
                            if u >= 2:
                                sem_, per, n = taken(u - 2)
                                pe.wait_ge(sem_, b * per + n)
                            for kt in range(u // HEADS + 1):
                                last = pe.transpose(banks[3 + u % 2][:, kt * P:(kt + 1) * P],
                                                    probs[:, u % 4, kt * P:(kt + 1) * P], c["ident"][:])
                            last.then_inc(pT_psum, 1)
                        if 0 <= i - 4 < U:
                            u = i - 4
                            qt, head = divmod(u, HEADS)
                            sem_, per, n = taken(u)
                            pe.wait_ge(sem_, b * per + n)
                            if head == 0 and qt >= 2:
                                pe.wait_ge(oT_lo_done, b * TT + qt - 1)
                            r = slice(HD * (head % 4), HD * (head % 4 + 1))
                            q = slice((head // 4) * P, (head // 4 + 1) * P)
                            for kt in range(qt + 1):
                                last = pe.matmul(banks[5 + qt % 2][r, q], v[:, kt, head * HD:(head + 1) * HD],
                                                 probsT[:, u % 2, kt], start=(kt == 0), stop=(kt == qt))
                            last.then_inc(pv_done, 1)
                        if i >= 22 and (i - 22) % HEADS == 0:
                            qt = (i - 22) // HEADS
                            pe.wait_ge(oT_lo_done, b * TT + qt + 1)
                            pe.wait_ge(cut, 5)
                            if qt > 0:
                                pe.wait_ge(y_added, b * TT + qt)
                            for k in range(KD):
                                last = mm3(pe, banks[7][:], oT_hi[:, k], oT_lo[:, k], w_hi[:, 3, k], w_lo[:, 3, k],
                                           k == 0, k == KD - 1)
                            last.then_inc(y_psum, 1)
                    pe.wait_ge(y_added, b * TT + TT)


def mamba_scan(nc, sem, c, xres, banks, a, ln_mv, ln_rstd, yT):
    UP = 2
    UNITS = NS // UP
    WR = 4
    ON_POOL = ()
    HALF = GI // 2
    NIN = 2 * GI
    RB = DR + 2 * NS
    outer = ExitStack()
    with outer:
        def sb(name, shape, dt, ctx=outer):
            return ctx.enter_context(nc.sbuf_tensor(name, shape, dt))
        conv_w = sb("conv_w", [P, GI, 4], F32)
        conv_b = sb("conv_b", [P, GI], F32)
        w_xproj = sb("w_xproj", [P, GI, RB], F32)
        w_dt = sb("w_dt", [DR, DI], F32)
        b_dt = sb("b_dt", [P, GI], F32)
        A = sb("A", [P, GI, NS], F32)
        Dp = sb("Dp", [P, GI], F32)
        stats = sb("m_stats", [P, TT, 6], F32)
        mv = sb("m_mv", [P, TT, 2], F32)
        rstd = sb("m_rstd", [P, TT], F32)
        gate = sb("gate", [P, GI, SEQ], F32)
        delta = sb("delta", [P, GI, SEQ], F32)
        du = sb("du", [P, GI, SEQ], F32)
        dA = sb("dA", [P, 2, UP, SEQ], F32)
        hs = sb("hs", [P, WR, UP, SEQ], F32)
        dbl = sb("dbl", [RB, SEQ], F32)
        dbl_hi = sb("dbl_hi", [RB, SEQ], F32R)
        dbl_lo = sb("dbl_lo", [RB, SEQ], F32R)
        early = ExitStack()
        with early:
            xm = sb("xm", [P, TT, D], F32, early)
            xT_hi = sb("m_xT_hi", [P, KD, SEQ], F32R, early)
            xT_lo = sb("m_xT_lo", [P, KD, SEQ], F32R, early)
            w_stage = sb("w_in_stage", [P, 2, KD, P], F32, early)
            w_hi = sb("w_in_hi", [P, 2, KD, P], F32R, early)
            w_lo = sb("w_in_lo", [P, 2, KD, P], F32R, early)
            raw = sb("raw", [P, 3, SEQ + 3], F32, early)
            pre = sb("pre", [P, 3, SEQ], F32, early)
            th = sb("th", [P, 3, SEQ], F32, early)
            e_t = sb("e_t", [P, HALF, SEQ], F32, early)
            w_t = sb("w_t", [P, HALF, SEQ], F32, early)
        Bs = sb("Bs", [P, NS, SEQ], F32)
        Cs = sb("Cs", [P, NS, SEQ], F32)

        passed = sem("m_passed")
        par_loaded = sem("par_loaded")
        par_act = sem("par_act")
        par_done = sem("par_done")
        pads = sem("pads")
        kept = sem("kept")
        win_loaded = [sem("win_loaded0"), sem("win_loaded1")]
        win_hi = sem("win_hi")
        win_lo = sem("win_lo")
        stats_done = sem("m_stats_done")
        mv_done = sem("m_mv_done")
        rstd_done = sem("m_rstd_done")
        xm_done = sem("xm_done")
        xT_psum = sem("m_xT_psum")
        xT_hi_done = sem("m_xT_hi_done")
        xT_lo_done = sem("m_xT_lo_done")
        in_psum = sem("in_psum")
        raw_done = sem("raw_done")
        pre_done = sem("pre_done")
        tap_done = sem("tap_done")
        tanh_done = sem("tanh_done")
        silu_done = sem("silu_done")
        dbl_psum = sem("dbl_psum")
        dbl_act = sem("dbl_act")
        dbl_lo_done = sem("dbl_lo_done")
        dt_psum = sem("dt_psum")
        absx_done = sem("absx_done")
        relu_done = sem("relu_done")
        expx_done = sem("expx_done")
        onep_done = sem("onep_done")
        fix_done = sem("fix_done")
        ln_done = sem("ln_done")
        delta_done = sem("delta_done")
        skip_done = sem("skip_done")
        du_done = sem("du_done")
        bc_psum = sem("bc_psum")
        bc_act = sem("bc_act")
        bc_dve = sem("bc_dve")
        dA_done = sem("dA_done")
        dBu_done = sem("dBu_done")
        scan_done = sem("scan_done")
        hC_dve = sem("hC_dve")
        hC_pool = sem("hC_pool")
        unit_summed = sem("unit_summed")
        y_gated = sem("y_gated")

        with nc.Block() as block:
            @block.sync
            def _(sp):
                for dst, name in ((conv_w, "conv_w"), (conv_b, "conv_b"), (w_xproj, "w_xproj"), (w_dt, "w_dt"),
                                  (b_dt, "b_dt"), (A, "A_log"), (Dp, "Dp")):
                    sp.dma_start(dst[:], a[name]).then_inc(par_loaded, 16)
                with sp.Fori(0, BATCH) as b:
                    hold(sp, y_gated, b * GI + 1, passed)
                    sp.wait_ge(win_lo, b * NIN + 1)
                    for n in range(NIN):
                        if n >= 2:
                            sp.wait_ge(win_lo, b * NIN + n)
                        sp.dma_start(w_stage[:, n % 2], a["w_in"][n]).then_inc(win_loaded[n % 2], 16)

            @block.gpsimd
            def _(pool):
                pool.sem_inc(win_lo, 1)
                for r in range(2):
                    pool.memset(dA[:, r, :, 0:1], 0.0).then_inc(scan_done, 1)
                for r in range(WR):
                    pool.memset(hs[:, r], 0.0).then_inc(unit_summed, 1)
                with pool.Fori(0, BATCH) as b:
                    hold(pool, y_gated, b * GI + 1, passed)
                    pool.memset(raw[:, :, 0:3], 0.0).then_inc(pads, 1)
                    hold(pool, mv_done, (b + 1) * TT, passed)
                    r = rstd[:]
                    pool.tensor_scalar(r, mv[:, :, 1], LN_EPS, None, ALU.add).then_inc(rstd_done, 1)
                    pool.wait_ge(rstd_done, b * 2 + 1)
                    pool.tensor_tensor(r, r, c["minus_half"][:, 0:TT], ALU.pow).then_inc(rstd_done, 1)
                    def cut(n):
                        pool.wait_ge(win_hi, b * NIN + n + 1)
                        pool.tensor_tensor(w_lo[:, n % 2], w_stage[:, n % 2], w_hi[:, n % 2].bitcast(F32),
                                           ALU.subtract).then_inc(win_lo, 1)

                    def drive_all(hf):
                        pool.wait_ge(delta_done, (b * 2 + hf) * 2 + 2)
                        pool.wait_ge(skip_done, b * GI + (hf + 1) * HALF)
                        pool.wait_ge(dbl_psum, b + 1)
                        s = slice(hf * HALF, (hf + 1) * HALF)
                        pool.tensor_tensor(du[:, s], du[:, s], delta[:, s], ALU.mult).then_inc(du_done, 1)
                    for n in range(GI + 4):
                        cut(n)
                    drive_all(0)
                    for n in range(GI + 4, NIN):
                        cut(n)
                    drive_all(1)
                    hold(pool, du_done, b * 2 + 2, passed)
                    hold(pool, bc_act, b * NS + NS, passed)
                    hold(pool, bc_dve, b * NS + NS, passed)
                    with pool.Fori(0, GI) as g:
                        base = b * (GI * UNITS) + g * UNITS

                        def drive(u):
                            hold(pool, unit_summed, base + u + 1, passed)
                            pool.tensor_tensor(hs[:, u % WR], bc_mid(du[:, g], UP), Bs[:, UP * u:UP * (u + 1)],
                                               ALU.mult).then_inc(dBu_done, 1)

                        def read_out(u):
                            pool.wait_ge(scan_done, base + u + 3)
                            pool.tensor_tensor(hs[:, u % WR], hs[:, u % WR], Cs[:, UP * u:UP * (u + 1)],
                                               ALU.mult).then_inc(hC_pool, 1)
                        drive(0)
                        for u in range(1, UNITS):
                            drive(u)
                            if u - 1 in ON_POOL:
                                read_out(u - 1)

            @block.scalar
            def _(act):
                act.wait_ge(par_loaded, 7 * 16)
                act.activation(A[:], A[:], ACT.Exp).then_inc(par_act, 1)
                with act.Fori(0, BATCH) as b:
                    act.wait_ge(y_gated, b * GI + 1)
                    for t in range(TT):
                        act.wait_ge(xT_psum, b * TT + t + 1)
                        act.copy(xT_hi[:, :, t * P:(t + 1) * P],
                                 banks[4 + t % 2][:].rearrange("p (k n) -> p k n", k=KD)).then_inc(xT_hi_done, 1)

                    def cut(n):
                        act.wait_ge(win_loaded[n % 2], (b * (NIN // 2) + n // 2 + 1) * 16)
                        act.wait_ge(in_psum, b * NIN + max(n - 1, 0) + 1)
                        act.copy(w_hi[:, n % 2], w_stage[:, n % 2]).then_inc(win_hi, 1)

                    def take(n):
                        act.wait_ge(in_psum, b * NIN + n + 2)
                        act.wait_ge(silu_done, b * NIN + max(n - 2, 0) + 1)
                        if n == 0:
                            act.wait_ge(par_done, 3)
                            act.wait_ge(pads, b + 1)
                        if n < GI:
                            act.copy(raw[:, n % 3, 3:SEQ + 3], banks[n % 4][:]).then_inc(raw_done, 1)
                            act.activation(pre[:, n % 3], banks[n % 4][:], ACT.Identity, bias=conv_b[:, n:n + 1],
                                           scale=conv_w[:, n, 3:4]).then_inc(pre_done, 1)
                        else:
                            act.activation(pre[:, n % 3], banks[n % 4][:], ACT.Identity, scale=0.5).then_inc(pre_done, 1)

                    def tanh(n):
                        if n < GI:
                            act.wait_ge(tap_done, b * GI * 3 + 3 * (n + 1))
                        else:
                            act.wait_ge(pre_done, b * NIN + n + 1)
                        act.activation(th[:, n % 3], pre[:, n % 3], ACT.Tanh).then_inc(tanh_done, 1)
                    def softplus(hf):
                        act.wait_ge(absx_done, b * GI + (hf + 1) * HALF)
                        act.activation(e_t[:], e_t[:], ACT.Exp, scale=-1.0).then_inc(expx_done, 1)

                    def logarithm(hf):
                        act.wait_ge(fix_done, b * 2 + hf + 1)
                        act.activation(w_t[:], w_t[:], ACT.Ln).then_inc(ln_done, 1)

                    def abs_x(g):
                        act.wait_ge(dt_psum, b * GI + g + 1)
                        if g >= HALF:
                            act.wait_ge(delta_done, b * 4 + 2)
                        act.activation(e_t[:, g % HALF], banks[5 + g % 2][:], ACT.Abs,
                                       bias=b_dt[:, g:g + 1]).then_inc(absx_done, 1)
                    cut(0)
                    cut(1)
                    for n in range(GI):
                        take(n)
                        cut(n + 2)
                        if n >= 1:
                            tanh(n - 1)
                    tanh(GI - 1)
                    act.wait_ge(dbl_psum, b + 1)
                    act.copy(dbl[:], banks[4][0:RB, :]).then_inc(dbl_act, 1)
                    act.copy(dbl_hi[:], banks[4][0:RB, :]).then_inc(dbl_act, 1)
                    for g in range(HALF):
                        abs_x(g)
                    softplus(0)
                    take(GI)
                    cut(GI + 2)
                    logarithm(0)
                    for g in range(HALF, GI):
                        abs_x(g)
                    softplus(1)
                    take(GI + 1)
                    cut(GI + 3)
                    tanh(GI)
                    logarithm(1)
                    for n in range(GI + 2, NIN):
                        take(n)
                        if n + 2 < NIN:
                            cut(n + 2)
                        tanh(n - 1)
                    tanh(NIN - 1)
                    act.wait_ge(delta_done, b * 4 + 4)
                    act.wait_ge(silu_done, b * NIN + NIN + 1)
                    for i in range(0, 2 * NS, 2):
                        act.wait_ge(bc_psum, b * 2 * NS + i + 1)
                        act.copy((Bs if i < NS else Cs)[:, i % NS], banks[i % 4][:]).then_inc(bc_act, 1)
                    with act.Fori(0, GI) as g:
                        base = b * (GI * UNITS) + g * UNITS
                        for u in range(UNITS):
                            act.wait_ge(scan_done, base + u + 1)
                            for n in range(UP):
                                act.activation(dA[:, u % 2, n, 1:SEQ], delta[:, g, 1:SEQ], ACT.Exp,
                                               scale=A[:, g, UP * u + n:UP * u + n + 1]).then_inc(dA_done, 1)

            @block.vector
            def _(dve):
                dve.sem_inc(y_gated, 1)
                dve.sem_inc(silu_done, 1)
                dve.wait_ge(par_act, 1)
                dve.tensor_scalar(A[:], A[:], -1.0, None, ALU.mult).then_inc(par_done, 1)
                dve.tensor_scalar(conv_w[:], conv_w[:], 0.5, None, ALU.mult).then_inc(par_done, 1)
                dve.tensor_scalar(conv_b[:], conv_b[:], 0.5, None, ALU.mult).then_inc(par_done, 1)
                dve.wait_ge(par_done, 3)
                with dve.Fori(0, BATCH) as b:
                    for t in range(TT):
                        dve.bn_stats(stats[:, t, :], xres[:, b * TT + t, :]).then_inc(stats_done, 1)
                    for t in range(TT):
                        hold(dve, stats_done, b * TT + t + 1, passed)
                        dve.bn_aggr(mv[:, t, :], stats[:, t, :]).then_inc(mv_done, 1)
                    dve.wait_ge(rstd_done, b * 2 + 2)
                    dve.tensor_copy(ln_mv[:, bass.ds(b * TT, TT), :], mv[:]).then_inc(kept, 1)
                    dve.tensor_copy(ln_rstd[:, bass.ds(b * TT, TT)], rstd[:]).then_inc(kept, 1)
                    for t in range(TT):
                        dve.tensor_scalar(xm[:, t, :], xres[:, b * TT + t, :], mv[:, t, 0:1],
                                          rstd[:, t:t + 1], ALU.subtract, ALU.mult).then_inc(xm_done, 1)
                    for t in range(TT):
                        dve.wait_ge(xT_hi_done, b * TT + t + 1)
                        s = slice(t * P, (t + 1) * P)
                        dve.tensor_tensor(xT_lo[:, :, s], banks[4 + t % 2][:].rearrange("p (k n) -> p k n", k=KD),
                                          xT_hi[:, :, s].bitcast(F32), ALU.subtract).then_inc(xT_lo_done, 1)

                    def taps(n):
                        dve.wait_ge(raw_done, b * GI + n + 1)
                        for j in range(3):
                            if j == 0:
                                dve.wait_ge(pre_done, b * NIN + n + 1)
                            else:
                                dve.wait_ge(tap_done, b * GI * 3 + 3 * n + j)
                            dve.scalar_tensor_tensor(pre[:, n % 3], raw[:, n % 3, j:j + SEQ], conv_w[:, n, j:j + 1],
                                                     pre[:, n % 3], ALU.mult, ALU.add).then_inc(tap_done, 1)

                    def silu(n):
                        dve.wait_ge(tanh_done, b * NIN + n + 1)
                        dst = du[:, n] if n < GI else gate[:, n - GI]
                        dve.scalar_tensor_tensor(dst, th[:, n % 3], 1.0, pre[:, n % 3], ALU.add,
                                                 ALU.mult).then_inc(silu_done, 1)
                    for n in range(GI):
                        taps(n)
                        if n >= 1:
                            silu(n - 1)
                    silu(GI - 1)
                    dve.wait_ge(dbl_act, b * 2 + 2)
                    dve.tensor_tensor(dbl_lo[:], banks[4][0:RB, :], dbl_hi[:].bitcast(F32), ALU.subtract).then_inc(dbl_lo_done, 1)
                    for hf in range(2):
                        s = slice(hf * HALF, (hf + 1) * HALF)
                        for g in range(hf * HALF, (hf + 1) * HALF):
                            dve.wait_ge(absx_done, b * GI + g + 1)
                            dve.tensor_scalar(delta[:, g], banks[5 + g % 2][:], b_dt[:, g:g + 1], 0.0,
                                              ALU.add, ALU.max).then_inc(relu_done, 1)
                        for g in range(hf * HALF, (hf + 1) * HALF):
                            dve.tensor_scalar(yT[:, g, bass.ds(b * SEQ, SEQ)], du[:, g], Dp[:, g:g + 1], None,
                                              ALU.mult).then_inc(skip_done, 1)
                        dve.wait_ge(expx_done, b * 2 + hf + 1)
                        dve.tensor_scalar(w_t[:], e_t[:], 1.0, None, ALU.add).then_inc(onep_done, 1)
                        dve.wait_ge(onep_done, b * 2 + hf + 1)
                        dve.scalar_tensor_tensor(e_t[:].rearrange("p g s -> p (g s)"), w_t[:].rearrange("p g s -> p (g s)"),
                                                 -1.0, e_t[:].rearrange("p g s -> p (g s)"), ALU.add,
                                                 ALU.subtract).then_inc(fix_done, 1)
                        dve.wait_ge(relu_done, b * GI + (hf + 1) * HALF)
                        dve.wait_ge(fix_done, b * 2 + hf + 1)
                        dve.tensor_tensor(delta[:, s], delta[:, s], e_t[:], ALU.subtract).then_inc(delta_done, 1)
                        dve.wait_ge(ln_done, b * 2 + hf + 1)
                        dve.wait_ge(delta_done, b * 4 + 2 * hf + 1)
                        dve.tensor_tensor(delta[:, s], delta[:, s], w_t[:], ALU.add).then_inc(delta_done, 1)
                    for n in range(GI, NIN):
                        silu(n)
                    dve.wait_ge(delta_done, b * 4 + 4)
                    for i in range(1, 2 * NS, 2):
                        dve.wait_ge(bc_psum, b * 2 * NS + i + 1)
                        dve.tensor_copy((Bs if i < NS else Cs)[:, i % NS], banks[i % 4][:]).then_inc(bc_dve, 1)
                    dve.wait_ge(bc_act, b * NS + NS)
                    dve.wait_ge(bc_dve, b * NS + NS)

                    def unit_loop(g, first):
                        base = b * (GI * UNITS) + g * UNITS

                        def scan(u):
                            dve.wait_ge(dA_done, (base + u + 1) * UP)
                            dve.wait_ge(dBu_done, base + u + 1)
                            w = hs[:, u % WR].rearrange("p n s -> p (n s)")
                            dve.tensor_tensor_scan(w, dA[:, u % 2].rearrange("p n s -> p (n s)"), w, 0.0,
                                                   ALU.mult, ALU.add).then_inc(scan_done, 1)

                        def read_out(u):
                            if u not in ON_POOL:
                                dve.wait_ge(scan_done, base + u + 3)
                                dve.tensor_tensor(hs[:, u % WR], hs[:, u % WR], Cs[:, UP * u:UP * (u + 1)],
                                                  ALU.mult).then_inc(hC_dve, 1)
                        scan(0)
                        scan(1)
                        if not first:
                            gated(g - 1)
                        read_out(0)
                        for u in range(2, UNITS):
                            scan(u)
                            read_out(u - 1)
                        read_out(UNITS - 1)

                    def gated(g):
                        dve.wait_ge(unit_summed, b * (GI * UNITS) + (g + 1) * UNITS + WR)
                        dve.tensor_tensor(yT[:, g, bass.ds(b * SEQ, SEQ)], banks[7][:], gate[:, g], ALU.mult).then_inc(y_gated, 1)
                    unit_loop(0, True)
                    with dve.Fori(1, GI) as g:
                        unit_loop(g, False)
                    gated(GI - 1)
                    dve.wait_ge(y_gated, b * GI + GI + 1)

            @block.tensor
            def _(pe):
                pe.sem_inc(in_psum, 1)
                with pe.Fori(0, BATCH) as b:
                    for t in range(TT):
                        pe.wait_ge(xm_done, b * TT + t + 1)
                        if t >= 2:
                            pe.wait_ge(xT_lo_done, b * TT + t - 1)
                        for k in range(KD):
                            last = pe.transpose(banks[4 + t % 2][:, k * P:(k + 1) * P], xm[:, t, k * P:(k + 1) * P],
                                                c["ident"][:])
                        last.then_inc(xT_psum, 1)
                    pe.wait_ge(xT_lo_done, b * TT + TT)
                    def project_in(n):
                        pe.wait_ge(win_lo, b * NIN + n + 2)
                        if n >= 4:
                            pe.wait_ge(pre_done, b * NIN + n - 3)
                        for k in range(KD):
                            last = mm3(pe, banks[n % 4][:], w_hi[:, n % 2, k], w_lo[:, n % 2, k], xT_hi[:, k], xT_lo[:, k],
                                       k == 0, k == KD - 1)
                        last.then_inc(in_psum, 1)
                    def project_u(k):
                        pe.wait_ge(silu_done, b * NIN + k + 2)
                        last = pe.matmul(banks[4][0:RB, :], w_xproj[:, k], du[:, k], start=(k == 0), stop=(k == GI - 1))
                        if k == GI - 1:
                            last.then_inc(dbl_psum, 1)
                    for n in range(GI):
                        project_in(n)
                        if n >= 3:
                            project_u(n - 3)
                    for k in range(GI - 3, GI):
                        project_u(k)
                    pe.wait_ge(dbl_act, b * 2 + 1)
                    for g in range(GI):
                        if g >= 2:
                            pe.wait_ge(relu_done, b * GI + g - 1)
                        pe.matmul(banks[5 + g % 2][:], w_dt[:, g * P:(g + 1) * P], dbl[0:DR, :],
                                  start=True, stop=True).then_inc(dt_psum, 1)
                        if g == HALF + 1:
                            project_in(GI)
                    for n in range(GI + 1, NIN):
                        project_in(n)
                    pe.wait_ge(dbl_lo_done, b + 1)
                    for i in range(2 * NS):
                        if i == 0:
                            pe.wait_ge(pre_done, b * NIN + NIN)
                        if i >= 4:
                            pe.wait_ge(bc_dve if i % 2 else bc_act, b * NS + (i - 4) // 2 + 1)
                        pick = c["ident_r"][0:RB, DR + i:DR + i + 1].to_broadcast([RB, P])
                        pe.matmul(banks[i % 4][:], pick, dbl_hi[:], start=True, stop=False)
                        pe.matmul(banks[i % 4][:], pick, dbl_lo[:], start=False, stop=True).then_inc(bc_psum, 1)
                    hold(pe, bc_act, b * NS + NS, passed)
                    hold(pe, bc_dve, b * NS + NS, passed)
                    hold(pe, skip_done, b * GI + GI, passed)
                    with pe.Fori(0, GI) as g:
                        pe.wait_ge(y_gated, b * GI + g + 1)
                        pe.matmul(banks[7][:], c["ident"][:], yT[:, g, bass.ds(b * SEQ, SEQ)], start=True, stop=False)
                        nd = UNITS - len(ON_POOL)
                        for u in range(UNITS):
                            if u in ON_POOL:
                                pe.wait_ge(hC_pool, b * (GI * len(ON_POOL)) + g * len(ON_POOL) + ON_POOL.index(u) + 1)
                            else:
                                k = len([x for x in range(u) if x not in ON_POOL])
                                pe.wait_ge(hC_dve, b * (GI * nd) + g * nd + k + 1)
                            for n in range(UP):
                                last = pe.matmul(banks[7][:], c["ident"][:], hs[:, u % WR, n], start=False,
                                                 stop=(u == UNITS - 1 and n == UP - 1))
                            last.then_inc(unit_summed, 1)


def feed_forward(nc, sem, c, xres, banks, a, ln_mv, ln_rstd, yT):
    KF = FF // P
    outer = ExitStack()
    with outer:
        def sb(name, shape, dt, ctx=outer):
            return ctx.enter_context(nc.sbuf_tensor(name, shape, dt))
        wo_hi = sb("wo_hi", [P, GI, D], F32R)
        wo_lo = sb("wo_lo", [P, GI, D], F32R)
        w1q = sb("w1q", [P, KD, FF], BF16)
        w2q = sb("w2q", [P, KF, D], BF16)
        n1 = sb("n1", [P, D], F32)
        n2 = sb("n2", [P, D], F32)
        b1 = sb("b1", [P, FF], F32)
        b2 = sb("b2", [P, D], F32)
        part = sb("part", [P, 8], F32)
        round_c = sb("round_c", [P, 2], F32)
        g = sb("g", [P, 2], F32)
        g_inv = sb("g_inv", [P, 2], F32)
        g_127 = sb("g_127", [P, 2], F32)

        stage = ExitStack()
        with stage:
            w1 = sb("w1_stage", [P, KD, FF], F32, stage)
            w2 = sb("w2_stage", [P, KF, D], F32, stage)
            wo = sb("wo_stage", [P, GI // 2, D], F32, stage)
            w_loaded = [sem(f"w_chunk{n}_loaded") for n in range(8)]
            wo_loaded, rows_loaded = sem("wo_loaded"), sem("rows_loaded")
            sum_dve, sum_act, total_psum, g_done, wo_cut = sem("sum_dve"), sem("sum_act"), sem("total_psum"), sem("g_done"), sem("wo_cut")
            round_set, w_shifted, w_top, w_quantised = sem("round_set"), sem("w_shifted"), sem("w_top"), sem("w_quantised")
            CHUNK = 2048
            w1_flat, w2_flat = w1[:].rearrange("p k n -> p (k n)"), w2[:].rearrange("p k n -> p (k n)")
            w1q_flat, w2q_flat = w1q[:].rearrange("p k n -> p (k n)"), w2q[:].rearrange("p k n -> p (k n)")
            CHUNKS = KD * FF // CHUNK
            assert len(w_loaded) == 2 * CHUNKS
            ACT_SUMS = (4, 6)
            pieces = [(w[:, n * CHUNK:(n + 1) * CHUNK], q[:, n * CHUNK:(n + 1) * CHUNK], m)
                      for m, (w, q) in enumerate(((w1_flat, w1q_flat), (w2_flat, w2q_flat))) for n in range(CHUNKS)]
            with nc.Block() as block:
                @block.sync
                def _(sp):
                    for m, (w, name) in enumerate(((w1, "w1"), (w2, "w2"))):
                        k = w.shape[1] // CHUNKS
                        for n in range(CHUNKS):
                            sp.dma_start(w[:, n * k:(n + 1) * k], a[name][:, n * k:(n + 1) * k]).then_inc(w_loaded[m * CHUNKS + n], 16)
                        if m == 0:
                            sp.dma_start(wo[:], a["w_out"][:, 0:GI // 2]).then_inc(wo_loaded, 16)
                    for dst, name in ((n1, "n1"), (n2, "n2"), (b1, "b1"), (b2, "b2")):
                        sp.dma_start(dst[:], a[name].to_broadcast([P, a[name].shape[1]])).then_inc(rows_loaded, 16)
                    sp.wait_ge(wo_cut, 2)
                    sp.dma_start(wo[:], a["w_out"][:, GI // 2:GI]).then_inc(wo_loaded, 16)
                    sp.wait_ge(rows_loaded, 64)

                @block.scalar
                def _(act):
                    def cut_out(hf):
                        act.wait_ge(wo_loaded, 16 * (hf + 1))
                        act.copy(wo_hi[:, hf * (GI // 2):(hf + 1) * (GI // 2)], wo[:]).then_inc(wo_cut, 1)

                    def add_up(n):
                        act.wait_ge(w_loaded[n], 16)
                        act.activation(pieces[n][1], pieces[n][0], ACT.Abs, accum_out=part[:, n:n + 1]).then_inc(sum_act, 1)

                    def shift(n):
                        w, _, m = pieces[n]
                        act.wait_ge(g_done, 3 * (m + 1))
                        act.activation(w, w, ACT.Identity, bias=round_c[:, 0:1], scale=g_inv[:, m:m + 1]).then_inc(w_shifted, 1)
                    act.wait_ge(round_set, 2)
                    shift(0)
                    shift(1)
                    cut_out(0)
                    shift(2)
                    add_up(4)
                    shift(3)
                    add_up(6)
                    shift(4)
                    shift(5)
                    cut_out(1)
                    shift(6)
                    shift(7)

                @block.vector
                def _(dve):
                    def add_up(n):
                        dve.wait_ge(w_loaded[n], 16)
                        dve.tensor_reduce(part[:, n:n + 1], pieces[n][0], AX.X, ALU.add,
                                          apply_absolute_value=True).then_inc(sum_dve, 1)

                    def mean(m):
                        at = slice(m, m + 1)
                        dve.wait_ge(total_psum, m + 1)
                        dve.tensor_scalar(g[:, at], banks[m][:, 0:1], 1.0 / (FF * D), 1e-5, ALU.mult, ALU.max).then_inc(g_done, 1)
                        dve.wait_ge(g_done, 3 * m + 1)
                        dve.reciprocal(g_inv[:, at], g[:, at]).then_inc(g_done, 1)
                        dve.tensor_scalar(g_127[:, at], g[:, at], 1.0 / 127.0, None, ALU.mult).then_inc(g_done, 1)
                    def top(n):
                        dve.wait_ge(w_shifted, n + 1)
                        dve.tensor_scalar(pieces[n][1], pieces[n][0], -ROUND, 1.0, ALU.add, ALU.min).then_inc(w_top, 1)

                    def bottom(n):
                        dve.wait_ge(w_top, n + 1)
                        dve.tensor_scalar(pieces[n][1], pieces[n][1], -1.0, None, ALU.max).then_inc(w_quantised, 1)
                    for n in range(CHUNKS):
                        add_up(n)
                    mean(0)
                    for n in range(len(pieces)):
                        top(n)
                        if n >= 1:
                            bottom(n - 1)
                        if n in (1, 3):
                            add_up(CHUNKS + n)
                        if n == 3:
                            mean(1)
                    bottom(len(pieces) - 1)

                @block.gpsimd
                def _(pool):
                    pool.memset(round_c[:, 0:1], ROUND).then_inc(round_set, 1)
                    pool.memset(round_c[:, 1:2], -ROUND).then_inc(round_set, 1)
                    for hf in range(2):
                        s = slice(hf * (GI // 2), (hf + 1) * (GI // 2))
                        pool.wait_ge(wo_cut, 2 * hf + 1)
                        pool.tensor_tensor(wo_lo[:, s], wo[:], wo_hi[:, s].bitcast(F32), ALU.subtract).then_inc(wo_cut, 1)

                @block.tensor
                def _(pe):
                    for n in range(len(pieces)):
                        m, k = divmod(n, CHUNKS)
                        if n in ACT_SUMS:
                            pe.wait_ge(sum_act, ACT_SUMS.index(n) + 1)
                        else:
                            pe.wait_ge(sum_dve, n + 1 - len([x for x in ACT_SUMS if x < n]))
                        last = pe.matmul(banks[m][:, 0:1], c["ones"][:], part[:, n:n + 1], start=(k == 0), stop=(k == CHUNKS - 1))
                        if k == CHUNKS - 1:
                            last.then_inc(total_psum, 1)

        y_hi = sb("y_hi", [P, GI, P], F32R)
        y_lo = sb("y_lo", [P, GI, P], F32R)
        xm = sb("p_xm", [P, D], F32)
        xr = sb("xr", [P, D], F32)
        sq = sb("sq", [P, D], F32)
        x1 = sb("x1", [P, NT, D], F32)
        qt = sb("qt", [P, D], F32)
        qx = sb("qx", [P, D], BF16)
        qxT = sb("qxT", [P, KD, P], BF16)
        f1 = sb("f1", [P, FF], F32)
        fq = sb("fq", [P, FF], BF16)
        fqT = sb("fqT", [P, KF, P], BF16)
        f2 = sb("f2", [P, D], F32)
        x1b = sb("x1b", [P, D], F32)
        sq2 = sb("sq2", [P, D], F32)
        o2 = sb("o2", [P, D], F32)
        ss = sb("ss", [P, 2], F32)
        rs = sb("rs", [P, 2], F32)
        am = sb("am", [P, 2], F32)
        quant = sb("quant", [P, 2], F32)
        unscale = sb("unscale", [P, NT, 2], F32)

        passed = sem("p_passed")
        y_hi_done, y_lo_done, out_psum = sem("y_hi_done"), sem("y_lo_done"), sem("out_psum")
        xm_done, xr_done, ss1, rs1, x1_done = sem("p_xm_done"), sem("xr_done"), sem("ss1"), sem("rs1"), sem("x1_done")
        am1, qt1, qx_done, qxT_psum, qxT_done = sem("am1"), sem("qt1"), sem("qx_done"), sem("qxT_psum"), sem("qxT_done")
        ff1_psum, f1_done, gelu_done, am2, fq_tmp, fq_done = (sem("ff1_psum"), sem("f1_done"), sem("gelu_done"), sem("am2"),
                                                              sem("fq_tmp"), sem("fq_done"))
        fqT_psum, fqT_done, ff2_psum, f2_done, ss2, rs2, o2_done, res_done, x1b_done = (
            sem("fqT_psum"), sem("fqT_done"), sem("ff2_psum"), sem("f2_done"), sem("ss2"), sem("rs2"), sem("o2_done"), sem("res_done"),
            sem("x1b_done"))
        tq = banks[1][:, 0:KD * P // 2].bitcast(BF16)
        tf = banks[6][:].bitcast(BF16)

        LAG = 3
        STEPS = NT + LAG

        def steps(eng, step):
            for s in range(LAG):
                step(s, s)
            with eng.Fori(LAG, NT) as s:
                step(s, None)
            for s in range(NT, STEPS):
                step(s, s)

        def tile(s, at, lag):
            return s - lag if at is None or 0 <= at - lag < NT else None

        def after(eng, semaphore, value, at):
            if at is None or value > 0:
                eng.wait_ge(semaphore, value)

        with nc.Block() as block:
            @block.gpsimd
            def _(pool):
                def rms(i, k, sums, done):
                    hold(pool, sums, i + 1, passed)
                    pool.tensor_scalar(rs[:, k:k + 1], ss[:, k:k + 1], 1.0 / D, RMS_EPS, ALU.mult, ALU.add).then_inc(done, 1)
                    pool.wait_ge(done, 2 * i + 1)
                    pool.tensor_tensor(rs[:, k:k + 1], rs[:, k:k + 1], c["minus_half"][:, 0:1], ALU.pow).then_inc(done, 1)

                def step(s, at):
                    i, o = tile(s, at, 0), tile(s, at, 3)
                    if i is not None:
                        hold(pool, y_hi_done, i + 1, passed)
                        pool.tensor_tensor(y_lo[:], yT[:, :, bass.ds(i * P, P)], y_hi[:].bitcast(F32),
                                           ALU.subtract).then_inc(y_lo_done, 1)
                    if o is not None:
                        after(pool, f2_done, o, at)
                        pool.tensor_tensor(x1b[:], x1[:, o, :], b2[:], ALU.add).then_inc(x1b_done, 1)
                        rms(o, 1, ss2, rs2)
                        hold(pool, o2_done, o + 1, passed)
                        pool.tensor_tensor(xres[:, o, :], xres[:, o, :], o2[:], ALU.add).then_inc(res_done, 1)
                    if i is not None:
                        rms(i, 0, ss1, rs1)
                steps(pool, step)

            @block.scalar
            def _(act):
                def step(s, at):
                    i, q, f, o = (tile(s, at, lag) for lag in range(4))
                    if i is not None:
                        after(act, out_psum, i, at)
                        act.copy(y_hi[:], yT[:, :, bass.ds(i * P, P)]).then_inc(y_hi_done, 1)
                    for hf in range(2):
                        if f is not None:
                            h = slice(hf * (FF // 2), (hf + 1) * (FF // 2))
                            act.wait_ge(f1_done, 4 * f + 2 * hf + 2)
                            act.activation(f1[:, h], f1[:, h], ACT.Gelu_apprx_tanh).then_inc(gelu_done, 1)
                        if o is not None:
                            act.wait_ge(fqT_psum, 2 * o + hf + 1)
                            act.copy(fqT[:, hf * (KF // 2):(hf + 1) * (KF // 2)].rearrange("p k n -> p (k n)"),
                                     tf).then_inc(fqT_done, 1)
                    if q is not None:
                        act.wait_ge(qxT_psum, q + 1)
                        act.copy(qxT[:].rearrange("p k n -> p (k n)"), tq).then_inc(qxT_done, 1)
                    if o is not None:
                        act.wait_ge(f2_done, o + 1)
                        act.activation(sq2[:], f2[:], ACT.Square, accum_out=ss[:, 1:2]).then_inc(ss2, 1)
                    if f is not None:
                        act.wait_ge(fq_tmp, 2 * f + 2)
                        act.activation(fq[:], f1[:], ACT.Identity, bias=round_c[:, 1:2]).then_inc(fq_done, 1)
                    if i is not None:
                        act.wait_ge(xr_done, i + 1)
                        act.activation(sq[:], xr[:], ACT.Square, accum_out=ss[:, 0:1]).then_inc(ss1, 1)
                steps(act, step)

            @block.vector
            def _(dve):
                def quantise_x(q):
                    dve.wait_ge(rs1, 2 * q + 2)
                    dve.scalar_tensor_tensor(x1[:, q, :], xr[:], rs[:, 0:1], n1[:], ALU.mult, ALU.mult).then_inc(x1_done, 1)
                    hold(dve, x1_done, q + 1, passed)
                    dve.tensor_reduce(am[:, 0:1], x1[:, q, :], AX.X, ALU.max, apply_absolute_value=True).then_inc(am1, 1)
                    dve.wait_ge(am1, 4 * q + 1)
                    dve.tensor_scalar(am[:, 0:1], am[:, 0:1], 1e-5, None, ALU.max).then_inc(am1, 1)
                    dve.wait_ge(am1, 4 * q + 2)
                    dve.reciprocal(quant[:, 0:1], am[:, 0:1]).then_inc(am1, 1)
                    dve.tensor_scalar(unscale[:, q, 0:1], am[:, 0:1], g_127[:, 0:1], None, ALU.mult).then_inc(am1, 1)
                    dve.wait_ge(am1, 4 * q + 4)
                    dve.tensor_scalar(quant[:, 0:1], quant[:, 0:1], 127.0, None, ALU.mult).then_inc(qt1, 1)
                    dve.wait_ge(qt1, 2 * q + 1)
                    dve.tensor_scalar(qt[:], x1[:, q, :], quant[:, 0:1], ROUND, ALU.mult, ALU.add).then_inc(qt1, 1)
                    dve.wait_ge(qt1, 2 * q + 2)
                    dve.tensor_scalar(qx[:], qt[:], -ROUND, None, ALU.add).then_inc(qx_done, 1)

                def first_half(f):
                    for n in range(4):
                        dve.wait_ge(ff1_psum, 4 * f + n + 1)
                        s = slice(n * 512, (n + 1) * 512)
                        dve.scalar_tensor_tensor(f1[:, s], banks[2 + n][:], unscale[:, f, 0:1], b1[:, s], ALU.mult,
                                                 ALU.add).then_inc(f1_done, 1)

                def scales_f(f):
                    dve.wait_ge(gelu_done, 2 * f + 2)
                    dve.tensor_reduce(am[:, 1:2], f1[:], AX.X, ALU.max, apply_absolute_value=True).then_inc(am2, 1)
                    dve.wait_ge(am2, 4 * f + 1)
                    dve.tensor_scalar(am[:, 1:2], am[:, 1:2], 1e-5, None, ALU.max).then_inc(am2, 1)
                    dve.wait_ge(am2, 4 * f + 2)
                    dve.reciprocal(quant[:, 1:2], am[:, 1:2]).then_inc(am2, 1)
                    dve.tensor_scalar(unscale[:, f, 1:2], am[:, 1:2], g_127[:, 1:2], None, ALU.mult).then_inc(am2, 1)
                    dve.wait_ge(am2, 4 * f + 4)
                    dve.tensor_scalar(quant[:, 1:2], quant[:, 1:2], 127.0, None, ALU.mult).then_inc(fq_tmp, 1)

                def quantise_f(f):
                    dve.wait_ge(fq_tmp, 2 * f + 1)
                    dve.tensor_scalar(f1[:], f1[:], quant[:, 1:2], ROUND, ALU.mult, ALU.add).then_inc(fq_tmp, 1)

                def second_half(o):
                    dve.wait_ge(ff2_psum, o + 1)
                    dve.wait_ge(x1b_done, o + 1)
                    dve.scalar_tensor_tensor(f2[:], banks[7][:], unscale[:, o, 1:2], x1b[:], ALU.mult, ALU.add).then_inc(f2_done, 1)

                def result(o, at):
                    dve.wait_ge(rs2, 2 * o + 2)
                    after(dve, res_done, o, at)
                    dve.scalar_tensor_tensor(o2[:], f2[:], rs[:, 1:2], n2[:], ALU.mult, ALU.mult).then_inc(o2_done, 1)

                def step(s, at):
                    i, q, f, o = (tile(s, at, lag) for lag in range(4))
                    if f is not None:
                        after(dve, fq_done, f, at)
                        first_half(f)
                    if q is not None:
                        quantise_x(q)
                    if i is not None:
                        dve.tensor_scalar(xm[:], xres[:, i, :], ln_mv[:, i, 0:1], ln_rstd[:, bass.ds(i, 1)], ALU.subtract,
                                          ALU.mult).then_inc(xm_done, 1)
                    if f is not None:
                        scales_f(f)
                    if o is not None:
                        second_half(o)
                    if f is not None:
                        quantise_f(f)
                    if o is not None:
                        result(o, at)
                    if i is not None:
                        dve.wait_ge(xm_done, i + 1)
                        dve.wait_ge(out_psum, i + 1)
                        dve.tensor_tensor(xr[:], xm[:], banks[0][:], ALU.add).then_inc(xr_done, 1)
                steps(dve, step)

            @block.tensor
            def _(pe):
                def step(s, at):
                    i, q, f, o = (tile(s, at, lag) for lag in range(4))
                    if f is not None:
                        pe.wait_ge(qxT_done, f + 1)
                        after(pe, f1_done, 4 * f, at)
                        for n in range(4):
                            for k in range(KD):
                                last = pe.matmul(banks[2 + n][:], qxT[:, k], w1q[:, k, n * 512:(n + 1) * 512],
                                                 start=(k == 0), stop=(k == KD - 1))
                            last.then_inc(ff1_psum, 1)
                    if o is not None:
                        pe.wait_ge(fq_done, o + 1)
                        for hf in range(2):
                            after(pe, fqT_done, 2 * o + hf, at)
                            for k in range(KF // 2):
                                kk = hf * (KF // 2) + k
                                last = pe.transpose(tf[:, k * P:(k + 1) * P], fq[:, kk * P:(kk + 1) * P], c["ident_b"][:])
                            last.then_inc(fqT_psum, 1)
                        after(pe, f2_done, o, at)
                        for k in range(KF):
                            if k % (KF // 2) == 0:
                                pe.wait_ge(fqT_done, 2 * o + k // (KF // 2) + 1)
                            last = pe.matmul(banks[7][:], fqT[:, k], w2q[:, k], start=(k == 0), stop=(k == KF - 1))
                        last.then_inc(ff2_psum, 1)
                    if q is not None:
                        pe.wait_ge(qx_done, q + 1)
                        after(pe, qxT_done, q, at)
                        for k in range(KD):
                            last = pe.transpose(tq[:, k * P:(k + 1) * P], qx[:, k * P:(k + 1) * P], c["ident_b"][:])
                        last.then_inc(qxT_psum, 1)
                    if i is not None:
                        pe.wait_ge(y_lo_done, i + 1)
                        after(pe, xr_done, i, at)
                        for k in range(GI):
                            last = mm3(pe, banks[0][:], y_hi[:, k], y_lo[:, k], wo_hi[:, k], wo_lo[:, k], k == 0, k == GI - 1)
                        last.then_inc(out_psum, 1)
                steps(pe, step)


def experts(nc, sem, c, xres, banks, a, out):
    KI = EI // P
    PAIRS = EALL // 2
    UNITS = EALL * BATCH
    outer = ExitStack()
    with outer:
        def sb(name, shape, dt):
            return outer.enter_context(nc.sbuf_tensor(name, shape, dt))
        gate_w = sb("gate_w", [P, KD, E], F32)
        gate_hi = sb("gate_hi", [P, KD, E], F32R)
        gate_lo = sb("gate_lo", [P, KD, E], F32R)
        gate_b = sb("gate_b", [P, E], F32)
        before4 = sb("before4", [P, 4, 4], F32)
        before16 = sb("before16", [P, E, E], F32)
        stats = sb("e_stats", [P, NT, 6], F32)
        mv = sb("e_mv", [P, NT, 2], F32)
        rstd = sb("e_rstd", [P, NT], F32)
        xf = sb("xf", [P, NT, D], F32)
        xT_hi = sb("e_xT_hi", [P, KD, BATCH * SEQ], F32R)
        xT_lo = sb("e_xT_lo", [P, KD, BATCH * SEQ], F32R)
        up_stage = sb("up_stage", [P, 2, KD, 2 * EI], F32)
        up_hi = sb("up_hi", [P, 2, KD, 2 * EI], F32R)
        up_lo = sb("up_lo", [P, 2, KD, 2 * EI], F32R)
        dn_stage = sb("dn_stage", [P, 2, KI, D], F32)
        dn_hi = sb("dn_hi", [P, 2, KI, D], F32R)
        dn_lo = sb("dn_lo", [P, 2, KI, D], F32R)
        th = sb("e_th", [P, KI, SEQ], F32)
        ga = sb("ga", [P, KI, SEQ], F32)
        ac = sb("ac", [P, BATCH, KI, SEQ], F32)
        ac_hi = sb("ac_hi", [P, BATCH, KI, SEQ], F32R)
        ac_lo = sb("ac_lo", [P, BATCH, KI, SEQ], F32R)
        lgT = sb("lgT", [E, BATCH * SEQ], F32)
        prob = sb("prob", [P, NT, E], F32)
        sfc = sb("sfc", [P, NT, E], F32)
        pairs = sb("pairs", [P, 4, NT * 4], F32)
        grp = sb("grp", [P, NT, 4], F32)
        cmp = sb("cmp", [P, NT * E, E], F32)
        eqs = sb("eqs", [P, NT * E, E], F32)
        rank = sb("rank", [P, NT * E], F32)
        cw = sb("cw", [P, NT, EALL], F32)
        tot = sb("tot", [P, NT], F32)

        gate_loaded, gate_cut, masks = sem("gate_loaded"), sem("gate_cut"), sem("masks")
        up_loaded = [sem("up_loaded0"), sem("up_loaded1")]
        dn_loaded = [sem("dn_loaded0"), sem("dn_loaded1")]
        up_hi_done, up_lo_done, dn_hi_done, dn_lo_done = sem("up_hi_done"), sem("up_lo_done"), sem("dn_hi_done"), sem("dn_lo_done")
        stats_done, mv_done, rstd_done, xf_done, xres_done = (sem("e_stats_done"), sem("e_mv_done"), sem("e_rstd_done"),
                                                              sem("xf_done"), sem("xres_done"))
        xT_psum, xT_hi_done, xT_lo_done = sem("e_xT_psum"), sem("e_xT_hi_done"), sem("e_xT_lo_done")
        logit_psum, lgT_done, lg_psum, elogit, route, cw_shared = (
            sem("logit_psum"), sem("lgT_done"), sem("lg_psum"), sem("elogit"), sem("route"), sem("cw_shared"))
        up_psum, tanh_done, ga_done, gated = sem("up_psum"), sem("e_tanh_done"), sem("ga_done"), sem("gated")
        ac_hi_done, ac_lo_done, dn_psum, stored = sem("ac_hi_done"), sem("ac_lo_done"), sem("dn_psum"), sem("stored")
        y_added = sem("e_y_added")
        ROUTE = 28

        with nc.Block() as block:
            @block.sync
            def _(sp):
                def load(e, r, first):
                    if not first:
                        sp.wait_ge(up_lo_done, e - 1)
                    sp.dma_start(up_stage[:, r], a["up"][e]).then_inc(up_loaded[r], 16)
                    if not first:
                        sp.wait_ge(dn_lo_done, e - 1)
                    sp.dma_start(dn_stage[:, r], a["down"][e]).then_inc(dn_loaded[r], 16)
                sp.dma_start(gate_w[:], a["gate"]).then_inc(gate_loaded, 16)
                sp.dma_start(gate_b[:], a["gate_b"].to_broadcast([P, E])).then_inc(gate_loaded, 16)
                load(0, 0, True)
                load(1, 1, True)
                with sp.Fori(1, PAIRS) as j:
                    for r in range(2):
                        load(2 * j + r, r, False)
                for b in range(BATCH):
                    sp.wait_ge(y_added, (UNITS - BATCH + b + 1) * TT + 1)
                    sp.dma_start(out[b].rearrange("(t p) d -> p t d", p=P), xres[:, b * TT:(b + 1) * TT]).then_inc(stored, 16)
                sp.wait_ge(stored, 16 * BATCH)

            @block.gpsimd
            def _(pool):
                pool.memset(before4[:], 1.0).then_inc(masks, 1)
                pool.memset(before16[:], 1.0).then_inc(masks, 1)
                pool.memset(cw[:, :, E:EALL], 0.5).then_inc(cw_shared, 1)
                pool.wait_ge(mv_done, NT)
                pool.tensor_scalar(rstd[:], mv[:, :, 1], LN_EPS, None, ALU.add).then_inc(rstd_done, 1)
                pool.wait_ge(rstd_done, 1)
                pool.tensor_tensor(rstd[:], rstd[:], c["minus_half"][:, 0:NT], ALU.pow).then_inc(rstd_done, 1)

                def cut_up(e, r):
                    pool.wait_ge(up_hi_done, e + 1)
                    pool.tensor_tensor(up_lo[:, r], up_stage[:, r], up_hi[:, r].bitcast(F32), ALU.subtract).then_inc(up_lo_done, 1)

                def cut_down(e, r):
                    pool.wait_ge(dn_hi_done, e + 1)
                    pool.tensor_tensor(dn_lo[:, r], dn_stage[:, r], dn_hi[:, r].bitcast(F32), ALU.subtract).then_inc(dn_lo_done, 1)

                def cut_ac(m, b):
                    for i in range(KI):
                        pool.wait_ge(ac_hi_done, m * KI + i + 1)
                        pool.tensor_tensor(ac_lo[:, b, i], ac[:, b, i], ac_hi[:, b, i].bitcast(F32), ALU.subtract).then_inc(ac_lo_done, 1)
                pool.wait_ge(gate_cut, 1)
                pool.tensor_tensor(gate_lo[:], gate_w[:], gate_hi[:].bitcast(F32), ALU.subtract).then_inc(gate_cut, 1)
                cut_up(0, 0)
                pool.wait_ge(masks, 2)
                pool.affine_select(out=before4[:], in_=before4[:], compare_op=ALU.is_gt, fill=0.0, base=0,
                                   pattern=[[1, 4], [-1, 4]], channel_multiplier=0).then_inc(masks, 1)
                pool.affine_select(out=before16[:], in_=before16[:], compare_op=ALU.is_gt, fill=0.0, base=0,
                                   pattern=[[1, E], [-1, E]], channel_multiplier=0).then_inc(masks, 1)
                cut_down(0, 0)
                cut_ac(0, 0)
                cut_up(1, 1)
                cut_down(1, 1)

                def pair(j, more):
                    cut_ac(4 * j + 1, 1)
                    cut_ac(4 * j + 2, 0)
                    if more:
                        cut_up(2 * j + 2, 0)
                    cut_ac(4 * j + 3, 1)
                    if more:
                        cut_down(2 * j + 2, 0)
                        cut_up(2 * j + 3, 1)
                        cut_ac(4 * j + 4, 0)
                        cut_down(2 * j + 3, 1)
                with pool.Fori(0, PAIRS - 1) as j:
                    pair(j, True)
                pair(PAIRS - 1, False)

            @block.scalar
            def _(act):
                def cut_up(e, r, use, first):
                    act.wait_ge(up_loaded[r], (use + 1) * 16)
                    if not first:
                        act.wait_ge(up_psum, (2 * e - 2) * KI)
                    act.copy(up_hi[:, r], up_stage[:, r]).then_inc(up_hi_done, 1)

                def cut_down(e, r, use, first):
                    act.wait_ge(dn_loaded[r], (use + 1) * 16)
                    if not first:
                        act.wait_ge(dn_psum, 2 * e - 2)
                    act.copy(dn_hi[:, r], dn_stage[:, r]).then_inc(dn_hi_done, 1)

                def unit(m, b):
                    for i in range(KI):
                        act.wait_ge(up_psum, m * KI + i + 1)
                        act.activation(th[:, i], banks[2 * i][:], ACT.Tanh, scale=0.5).then_inc(tanh_done, 1)
                    for i in range(KI):
                        act.wait_ge(gated, m * KI + i + 1)
                        act.copy(ac_hi[:, b, i], ac[:, b, i]).then_inc(ac_hi_done, 1)
                act.wait_ge(gate_loaded, 32)
                act.copy(gate_hi[:], gate_w[:]).then_inc(gate_cut, 1)
                cut_up(0, 0, 0, True)
                for t in range(NT):
                    act.wait_ge(xT_psum, t + 1)
                    act.copy(xT_hi[:, :, t * P:(t + 1) * P],
                             banks[4 + t % 4][:].rearrange("p (k n) -> p k n", k=KD)).then_inc(xT_hi_done, 1)
                for b in range(BATCH):
                    act.wait_ge(logit_psum, b + 1)
                    act.copy(lgT[:, b * SEQ:(b + 1) * SEQ], banks[4 + b][0:E, :]).then_inc(lgT_done, 1)
                act.wait_ge(lg_psum, 1)
                act.activation(prob[:].rearrange("p t e -> p (t e)"), banks[6][:, 0:NT * E], ACT.Exp, scale=-1.0).then_inc(elogit, 1)
                cut_down(0, 0, 0, True)
                unit(0, 0)
                cut_up(1, 1, 0, True)
                cut_down(1, 1, 0, True)

                def pair(j, more):
                    unit(4 * j + 1, 1)
                    unit(4 * j + 2, 0)
                    if more:
                        cut_up(2 * j + 2, 0, j + 1, False)
                    unit(4 * j + 3, 1)
                    if more:
                        cut_down(2 * j + 2, 0, j + 1, False)
                        cut_up(2 * j + 3, 1, j + 1, False)
                        unit(4 * j + 4, 0)
                        cut_down(2 * j + 3, 1, j + 1, False)
                with act.Fori(0, PAIRS - 1) as j:
                    pair(j, True)
                pair(PAIRS - 1, False)

            @block.vector
            def _(dve):
                dve.sem_inc(y_added, 1)
                for t in range(NT):
                    dve.bn_stats(stats[:, t, :], xres[:, t, :]).then_inc(stats_done, 1)
                for t in range(NT):
                    dve.wait_ge(stats_done, t + 1)
                    dve.bn_aggr(mv[:, t, :], stats[:, t, :]).then_inc(mv_done, 1)
                dve.wait_ge(rstd_done, 2)
                for t in range(NT):
                    dve.tensor_scalar(xf[:, t, :], xres[:, t, :], mv[:, t, 0:1], rstd[:, t:t + 1],
                                      ALU.subtract, ALU.mult).then_inc(xf_done, 1)
                for t in range(NT):
                    dve.wait_ge(xT_hi_done, t + 1)
                    s = slice(t * P, (t + 1) * P)
                    dve.tensor_tensor(xT_lo[:, :, s], banks[4 + t % 4][:].rearrange("p (k n) -> p k n", k=KD),
                                      xT_hi[:, :, s].bitcast(F32), ALU.subtract).then_inc(xT_lo_done, 1)

                def unit(m, b):
                    for i in range(KI):
                        dve.wait_ge(tanh_done, m * KI + i + 1)
                        dve.scalar_tensor_tensor(ga[:, i], th[:, i], 1.0, banks[2 * i][:], ALU.add,
                                                 ALU.mult).then_inc(ga_done, 1)
                    for i in range(KI):
                        dve.wait_ge(ga_done, m * KI + i + 1)
                        dve.tensor_tensor(ac[:, b, i], ga[:, i], banks[2 * i + 1][:], ALU.mult).then_inc(gated, 1)

                def add_y(m, e, b):
                    dve.wait_ge(dn_psum, m + 1)
                    for t in range(TT):
                        x = xres[:, b * TT + t, :]
                        dve.scalar_tensor_tensor(x, banks[4 + t][:], cw[:, b * TT + t, bass.ds(e, 1)], x, ALU.mult,
                                                 ALU.add).then_inc(y_added, 1)
                steps = [0]

                def step(instruction):
                    steps[0] += 1
                    instruction.then_inc(route, 1)
                    dve.wait_ge(route, steps[0])

                f = sfc[:].rearrange("p t (g e) -> p (t g) e", e=4)

                def ranks(v, n, before):
                    full = [P, NT, n, n]
                    other = v.unsqueeze(2).to_broadcast(full)
                    own = v.unsqueeze(3).to_broadcast(full)
                    gt = cmp[:, 0:NT * n, 0:n].rearrange("p (t x) y -> p t x y", t=NT)
                    eq = eqs[:, 0:NT * n, 0:n].rearrange("p (t x) y -> p t x y", t=NT)
                    step(dve.tensor_tensor(gt, other, own, ALU.is_gt))
                    step(dve.tensor_tensor(eq, other, own, ALU.is_equal))
                    step(dve.tensor_tensor(eq, eq, before.unsqueeze(1).to_broadcast(full), ALU.mult))
                    step(dve.tensor_tensor(gt, gt, eq, ALU.add))
                    step(dve.tensor_reduce(rank[:, 0:NT * n], cmp[:, 0:NT * n, 0:n], AX.X, ALU.add))

                def choose_groups():
                    dve.wait_ge(elogit, 1)
                    dve.wait_ge(masks, 4)
                    step(dve.tensor_scalar(prob[:], prob[:], 1.0, None, ALU.add))
                    step(dve.reciprocal(prob[:], prob[:]))
                    step(dve.tensor_tensor(sfc[:], prob[:], bc_mid(gate_b[:], NT), ALU.add))
                    step(dve.tensor_tensor(pairs[:, 0], f[:, :, 0], f[:, :, 1], ALU.max))
                    step(dve.tensor_tensor(pairs[:, 1], f[:, :, 2], f[:, :, 3], ALU.max))
                    step(dve.tensor_tensor(pairs[:, 2], f[:, :, 0], f[:, :, 1], ALU.add))
                    step(dve.tensor_tensor(pairs[:, 3], f[:, :, 2], f[:, :, 3], ALU.add))
                    step(dve.tensor_tensor(pairs[:, 0], pairs[:, 0], pairs[:, 1], ALU.add))
                    step(dve.tensor_tensor(pairs[:, 2], pairs[:, 2], pairs[:, 3], ALU.max))
                    step(dve.tensor_tensor(grp[:].rearrange("p t g -> p (t g)"), pairs[:, 0], pairs[:, 2], ALU.max))
                    ranks(grp[:], 4, before4[:])
                    step(dve.tensor_scalar(rank[:, 0:NT * 4], rank[:, 0:NT * 4], 2.0, BIG, ALU.is_lt, ALU.mult))
                    step(dve.tensor_scalar(rank[:, 0:NT * 4], rank[:, 0:NT * 4], -BIG, None, ALU.add))
                    step(dve.tensor_tensor(f, f, bc_free(rank[:, 0:NT * 4], 4), ALU.add))

                def choose_experts():
                    ranks(sfc[:], E, before16[:])
                    r = rank[:].rearrange("p (t e) -> p t e", t=NT)
                    w = cw[:, :, 0:E]
                    step(dve.scalar_tensor_tensor(w, r, 4.0, prob[:], ALU.is_lt, ALU.mult))
                    step(dve.reduce_sum(tot[:], w, AX.X))
                    step(dve.tensor_scalar(tot[:], tot[:], 1e-20, None, ALU.add))
                    step(dve.reciprocal(tot[:], tot[:]))
                    step(dve.scalar_tensor_tensor(w, w, 1.25, bc_free(tot[:], E), ALU.mult, ALU.mult))
                    assert steps[0] == ROUTE, steps[0]
                    dve.wait_ge(cw_shared, 1)
                    dve.wait_ge(xf_done, NT)

                def pair(j, more):
                    unit(4 * j + 1, 1)
                    add_y(4 * j, 2 * j, 0)
                    unit(4 * j + 2, 0)
                    add_y(4 * j + 1, 2 * j, 1)
                    unit(4 * j + 3, 1)
                    add_y(4 * j + 2, 2 * j + 1, 0)
                    if more:
                        unit(4 * j + 4, 0)
                    add_y(4 * j + 3, 2 * j + 1, 1)
                choose_groups()
                unit(0, 0)
                choose_experts()
                for t in range(NT):
                    dve.tensor_tensor(xres[:, t, :], xres[:, t, :], xf[:, t, :], ALU.add).then_inc(xres_done, 1)
                dve.wait_ge(xres_done, NT)
                pair(0, True)
                with dve.Fori(1, PAIRS - 1) as j:
                    pair(j, True)
                pair(PAIRS - 1, False)

            @block.tensor
            def _(pe):
                for t in range(NT):
                    pe.wait_ge(xf_done, t + 1)
                    if t >= 4:
                        pe.wait_ge(xT_lo_done, t - 3)
                    for k in range(KD):
                        last = pe.transpose(banks[4 + t % 4][:, k * P:(k + 1) * P], xf[:, t, k * P:(k + 1) * P], c["ident"][:])
                    last.then_inc(xT_psum, 1)

                def up(m, b, r, e):
                    pe.wait_ge(up_lo_done, e + 1)
                    x = slice(b * SEQ, (b + 1) * SEQ)
                    for i in range(KI):
                        if not (isinstance(m, int) and m == 0):
                            pe.wait_ge(gated, (m - 1) * KI + i + 1)
                        for half in range(2):
                            s = slice(half * EI + i * P, half * EI + (i + 1) * P)
                            for k in range(KD):
                                last = mm3(pe, banks[2 * i + half][:], up_hi[:, r, k, s], up_lo[:, r, k, s], xT_hi[:, k, x],
                                           xT_lo[:, k, x], k == 0, k == KD - 1)
                        last.then_inc(up_psum, 1)

                def down(m, b, r, e):
                    pe.wait_ge(ac_lo_done, (m + 1) * KI)
                    pe.wait_ge(dn_lo_done, e + 1)
                    pe.wait_ge(y_added, m * TT + 1)
                    for t in range(TT):
                        s = slice(t * P, (t + 1) * P)
                        for i in range(KI):
                            last = mm3(pe, banks[4 + t][:], ac_hi[:, b, i, s], ac_lo[:, b, i, s], dn_hi[:, r, i],
                                       dn_lo[:, r, i], i == 0, i == KI - 1)
                    last.then_inc(dn_psum, 1)
                pe.wait_ge(xT_lo_done, NT)
                pe.wait_ge(gate_cut, 2)
                for b in range(BATCH):
                    x = slice(b * SEQ, (b + 1) * SEQ)
                    for k in range(KD):
                        last = mm3(pe, banks[4 + b][0:E, :], gate_hi[:, k], gate_lo[:, k], xT_hi[:, k, x], xT_lo[:, k, x],
                                   k == 0, k == KD - 1)
                    last.then_inc(logit_psum, 1)
                for t in range(NT):
                    pe.wait_ge(lgT_done, t // TT + 1)
                    last = pe.transpose(banks[6][:, t * E:(t + 1) * E], lgT[:, t * P:(t + 1) * P], c["ident"][0:E, 0:E])
                last.then_inc(lg_psum, 1)
                up(0, 0, 0, 0)

                def pair(j, more):
                    up(4 * j + 1, 1, 0, 2 * j)
                    down(4 * j, 0, 0, 2 * j)
                    up(4 * j + 2, 0, 1, 2 * j + 1)
                    down(4 * j + 1, 1, 0, 2 * j)
                    up(4 * j + 3, 1, 1, 2 * j + 1)
                    down(4 * j + 2, 0, 1, 2 * j + 1)
                    if more:
                        up(4 * j + 4, 0, 0, 2 * j + 2)
                    down(4 * j + 3, 1, 1, 2 * j + 1)
                pe.wait_ge(elogit, 1)
                with pe.Fori(0, PAIRS - 1) as j:
                    pair(j, True)
                pair(PAIRS - 1, False)


def store(nc, sem, xres, out):
    stored = sem("stored")
    with nc.Block() as block:
        @block.sync
        def _(sp):
            sp.dma_start(out.rearrange("b (t p) d -> p (b t) d", p=P), xres[:]).then_inc(stored, 16)
            sp.wait_ge(stored, 16)


def load_only(nc, sem, xres, a):
    loaded = sem("x_only")
    with nc.Block() as block:
        @block.sync
        def _(sp):
            sp.dma_start(xres[:], a["x"].rearrange("b (t p) d -> p (b t) d", p=P)).then_inc(loaded, 16)
            sp.wait_ge(loaded, 16)


def dump(nc, sem, yT, out):
    d = nc.dram_tensor("dump", (P, GI, BATCH * SEQ), F32, kind="ExternalOutput").ap()
    dumped = sem("dumped")
    with nc.Block() as block:
        @block.sync
        def _(sp):
            sp.dma_start(d, yT[:]).then_inc(dumped, 16)
            sp.wait_ge(dumped, 16)


def stage_semaphores(nc, stage):
    taken = []

    def sem(name):
        taken.append(nc.alloc_semaphore(name=name))
        return taken[-1]
    stage(sem)
    nc.clear_and_free_semaphores(taken)
    nc.all_engine_barrier()


def build(nc, a, out, stages=("attention", "mamba", "moe")):
    ctx = ExitStack()
    with ctx:
        def sb(name, shape, dt):
            return ctx.enter_context(nc.sbuf_tensor(name, shape, dt))
        xres = sb("xres", [P, NT, D], F32)
        banks = [ctx.enter_context(nc.psum_tensor(f"bank{i}", [P, 512], F32)) for i in range(8)]
        c = {}
        stage_semaphores(nc, lambda sem: constants(nc, sb, sem, c))
        if "attention" in stages:
            stage_semaphores(nc, lambda sem: attention(nc, sem, c, xres, banks, a, True))
        else:
            stage_semaphores(nc, lambda sem: load_only(nc, sem, xres, a))
        if "mamba" in stages:
            with ExitStack() as mid:
                ln_mv = mid.enter_context(nc.sbuf_tensor("ln_mv", [P, NT, 2], F32))
                ln_rstd = mid.enter_context(nc.sbuf_tensor("ln_rstd", [P, NT], F32))
                yT = mid.enter_context(nc.sbuf_tensor("yT", [P, GI, BATCH * SEQ], F32))
                stage_semaphores(nc, lambda sem: mamba_scan(nc, sem, c, xres, banks, a, ln_mv, ln_rstd, yT))
                stage_semaphores(nc, lambda sem: feed_forward(nc, sem, c, xres, banks, a, ln_mv, ln_rstd, yT))
        if "moe" in stages:
            stage_semaphores(nc, lambda sem: experts(nc, sem, c, xres, banks, a, out))
        else:
            stage_semaphores(nc, lambda sem: store(nc, sem, xres, out))


def layout(np, i):
    T = np.transpose
    wg = np.concatenate([i["L0_ffn_Wg"], np.reshape(i["L0_ffn_Ws_g"], (2, EI, D))])
    wu = np.concatenate([i["L0_ffn_Wu"], np.reshape(i["L0_ffn_Ws_u"], (2, EI, D))])
    wd = np.concatenate([T(i["L0_ffn_Wd"], (0, 2, 1)), np.reshape(T(i["L0_ffn_Ws_d"]), (2, EI, D))])
    up = np.concatenate([wg, wu], axis=1)
    return {
        "x": i["x"],
        "ctxT": T(i["ctx_1024"][:, :SEQ], (0, 2, 1)),
        "wq": T(i["L0_xattn_Wq"]), "wk": T(i["L0_xattn_Wk"]), "wv": T(i["L0_xattn_Wv"]), "wo": T(i["L0_xattn_Wo"]),
        "w_in": T(np.reshape(i["L0_attn_w_in"], (2 * GI, P, KD, P)), (0, 3, 2, 1)),
        "conv_w": T(np.reshape(i["L0_attn_conv_w"], (GI, P, 4)), (1, 0, 2)),
        "conv_b": T(np.reshape(i["L0_attn_conv_b"], (GI, P))),
        "w_xproj": T(np.reshape(i["L0_attn_w_xproj"], (DR + 2 * NS, GI, P)), (2, 1, 0)),
        "w_dt": T(i["L0_attn_w_dt"]),
        "b_dt": T(np.reshape(i["L0_attn_b_dt"], (GI, P))),
        "A_log": T(np.reshape(i["L0_attn_A_log"], (GI, P, NS)), (1, 0, 2)),
        "Dp": T(np.reshape(i["L0_attn_Dp"], (GI, P))),
        "w_out": T(np.reshape(i["L0_attn_w_out"], (D, GI, P)), (2, 1, 0)),
        "n1": np.reshape(i["L0_attn_norm1_w"], (1, D)), "n2": np.reshape(i["L0_attn_norm2_w"], (1, D)),
        "w1": T(np.reshape(i["L0_attn_ffn_w1"], (FF, KD, P)), (2, 1, 0)),
        "b1": np.reshape(i["L0_attn_ffn_b1"], (1, FF)),
        "w2": T(np.reshape(i["L0_attn_ffn_w2"], (D, FF // P, P)), (2, 1, 0)),
        "b2": np.reshape(i["L0_attn_ffn_b2"], (1, D)),
        "gate": T(np.reshape(i["L0_ffn_gate_w"], (E, KD, P)), (2, 1, 0)),
        "gate_b": np.reshape(i["L0_ffn_gate_bias"], (1, E)),
        "up": T(np.reshape(up, (EALL, 2 * EI, KD, P)), (0, 3, 2, 1)),
        "down": T(np.reshape(wd, (EALL, EI // P, P, D)), (0, 2, 1, 3)),
    }


def kernel(**inputs):
    import numpy as np
    import concourse.bacc as bacc
    from concourse.bass_utils import run_bass_kernel_spmd

    nc = bacc.Bacc("TRN2", target_bir_lowering=False, num_devices=1)
    arrays, aps = {}, {}
    for name, array in layout(np, inputs).items():
        array = np.ascontiguousarray(array)
        arrays[f"in_{name}"] = array
        aps[name] = nc.dram_tensor(f"in_{name}", array.shape, F32, kind="ExternalInput").ap()
    out = nc.dram_tensor("out_x", (BATCH, SEQ, D), F32, kind="ExternalOutput").ap()
    build(nc, aps, out)
    result = run_bass_kernel_spmd(nc, [arrays], core_ids=[0])
    return result.results[0]["out_x"]
```

```python
import concourse.bass as bass
from concourse import mybir
from contextlib import ExitStack

F32 = mybir.dt.float32
F32R = mybir.dt.float32r
BF16 = mybir.dt.bfloat16
ALU = mybir.AluOpType
ACT = mybir.ActivationFunctionType
AX = mybir.AxisListType

P = 128
BATCH, SEQ, D = 2, 512, 512
TT = SEQ // P
NT = BATCH * TT
KD = D // P
HEADS, HD = 16, 32
DI, NS, DR = 1024, 16, 64
GI = DI // P
FF = 2048
E, EI = 16, 256
EALL = E + 2
LN_EPS, RMS_EPS = 1e-5, 1e-6
ROUND = 12582912.0
BIG = 1e30


def mm3(pe, out, lhs_hi, lhs_lo, rhs_hi, rhs_lo, start, stop):
    pe.matmul(out, lhs_hi, rhs_hi, start=start, stop=False)
    pe.matmul(out, lhs_hi, rhs_lo, start=False, stop=False)
    return pe.matmul(out, lhs_lo, rhs_hi, start=False, stop=stop)


def bc_free(ap, n):
    return ap.unsqueeze(2).to_broadcast([ap.shape[0], ap.shape[1], n])


def bc_mid(ap, n):
    return ap.unsqueeze(1).to_broadcast([ap.shape[0], n, ap.shape[1]])


def hold(eng, sem, value, passed):
    eng.wait_ge(sem, value)
    eng.sem_inc(passed, 1)


def constants(nc, sb, sem, c):
    c["ident"] = sb("ident", [P, P], F32)
    c["ident_r"] = sb("ident_r", [P, P], F32R)
    c["ident_b"] = sb("ident_b", [P, P], BF16)
    c["mask"] = sb("mask", [P, P], F32)
    c["minus_half"] = sb("minus_half", [P, 8], F32)
    c["ones"] = sb("ones", [P, P], F32)
    set_done = sem("constants_set")
    made = sem("constants_made")
    with nc.Block() as block:
        @block.gpsimd
        def _(pool):
            pool.memset(c["ident"][:], 0.0).then_inc(set_done, 1)
            pool.memset(c["mask"][:], 0.0).then_inc(set_done, 1)
            pool.memset(c["minus_half"][:], -0.5).then_inc(made, 1)
            pool.memset(c["ones"][:], 1.0).then_inc(made, 1)
            pool.wait_ge(set_done, 2)
            pool.affine_select(out=c["ident"][:], in_=c["ident"][:], compare_op=ALU.not_equal, fill=1.0,
                               base=0, pattern=[[-1, P]], channel_multiplier=1).then_inc(set_done, 1)
            pool.affine_select(out=c["mask"][:], in_=c["mask"][:], compare_op=ALU.is_ge, fill=-BIG,
                               base=0, pattern=[[-1, P]], channel_multiplier=1).then_inc(made, 1)
            pool.wait_ge(set_done, 3)
            pool.tensor_copy(c["ident_r"][:], c["ident"][:]).then_inc(made, 1)
            pool.tensor_copy(c["ident_b"][:], c["ident"][:]).then_inc(made, 1)
            pool.wait_ge(made, 5)


def attention(nc, sem, c, xres, banks, a):
    scale = float(HD) ** -0.5
    U = TT * HEADS
    STEPS = U + 8
    AHEAD = 2
    ctx = ExitStack()
    with ctx:
        def sb(name, shape, dt):
            return ctx.enter_context(nc.sbuf_tensor(name, shape, dt))
        stage = sb("a_stage", [P, 2, KD, D], F32)
        w_hi = sb("w_hi", [P, 4, KD, D], F32R)
        w_lo = sb("w_lo", [P, 4, KD, D], F32R)
        c_hi = sb("c_hi", [P, KD, SEQ], F32R)
        c_lo = sb("c_lo", [P, KD, SEQ], F32R)
        stats = sb("stats", [P, TT, 6], F32)
        mv = sb("mv", [P, TT, 2], F32)
        rstd = sb("rstd", [P, TT], F32)
        rows = sb("rows", [P, TT, D], F32)
        xT_hi = sb("xT_hi", [P, KD, SEQ], F32R)
        xT_lo = sb("xT_lo", [P, KD, SEQ], F32R)
        q_pad = sb("q_pad", [P, HEADS, SEQ], F32)
        kT = sb("kT", [P, KD, SEQ], F32)
        v = sb("v", [P, TT, D], F32)
        probs = sb("probs", [P, 4, SEQ], F32)
        probsT = sb("probsT", [P, 2, TT, P], F32)
        mask = sb("a_mask", [P, SEQ], F32)
        neg_max = sb("neg_max", [P, 4], F32)
        row_sum = sb("row_sum", [P, 4], F32)
        inv_sum = sb("inv_sum", [P, 4], F32)
        oT_hi = sb("oT_hi", [P, KD, P], F32R)
        oT_lo = sb("oT_lo", [P, KD, P], F32R)

        passed = sem("passed")
        x_loaded = sem("x_loaded")
        staged = [sem("staged0"), sem("staged1")]
        hi_done = sem("a_hi_done")
        cut = sem("a_cut")
        mask_done = sem("a_mask_done")
        zeroed = sem("q_zeroed")
        stats_done = sem("a_stats")
        mv_done = sem("a_mv")
        rstd_done = sem("a_rstd")
        xn_done = sem("a_xn")
        xT_psum = sem("a_xT_psum")
        xT_hi_done = sem("a_xT_hi")
        xT_lo_done = sem("a_xT_lo")
        proj_psum = sem("proj_psum")
        proj_act = sem("proj_act")
        proj_dve = sem("proj_dve")
        scores = sem("scores")
        max_done = sem("max_done")
        exp_done = sem("exp_done")
        inv_done = sem("inv_done")
        norm_done = sem("norm_done")
        pT_psum = sem("pT_psum")
        pT_act = sem("pT_act")
        pT_dve = sem("pT_dve")
        pv_done = sem("pv_done")
        oT_hi_done = sem("oT_hi_done")
        oT_lo_done = sem("oT_lo_done")
        y_psum = sem("y_psum")
        y_added = sem("y_added")

        ITEMS = ("ctx0", "wk", "wv", "wq", "wo", "ctx1")
        ON_ACT = 4
        ON_DVE = (1,)
        WEIGHTS = {"wq": 0, "wk": 1, "wv": 2, "wo": 3}
        PIECES = KD * 2 + 4

        def width(u):
            return (u // HEADS + 1) * P

        def on_act(u):
            return u % 5 in (1, 3)

        def taken(u):
            mine = [x for x in range(U) if on_act(x) == on_act(u)]
            return (pT_act if on_act(u) else pT_dve), len(mine), mine.index(u) + 1

        def take_pT(eng, copy, u, b):
            sem_, per, _ = taken(u)
            eng.wait_ge(pT_psum, b * U + u + 1)
            if u >= 2:
                eng.wait_ge(pv_done, b * U + u - 1)
            n = width(u)
            copy(probsT[:, u % 2].rearrange("p k n -> p (k n)")[:, 0:n], banks[3 + u % 2][:, 0:n]).then_inc(sem_, 1)

        with nc.Block() as block:
            @block.sync
            def _(sp):
                for i, name in enumerate(ITEMS):
                    if i == 2:
                        sp.dma_start(xres[:, 0:TT], a["x"][0].rearrange("(t p) d -> p t d", p=P)).then_inc(x_loaded, 16)
                    if i == 3:
                        sp.wait_ge(x_loaded, 16)
                        sp.dma_start(xres[:, TT:NT], a["x"][1].rearrange("(t p) d -> p t d", p=P)).then_inc(x_loaded, 16)
                    if i >= 2:
                        sp.wait_ge(cut, i - 1)
                    src = a[name] if name in WEIGHTS else a["ctxT"][int(name[3:])]
                    sp.dma_start(stage[:, i % 2], src.rearrange("(k p) n -> p k n", p=P)).then_inc(staged[i % 2], 16)

            @block.gpsimd
            def _(pool):
                pool.memset(mask[:, 0:SEQ - P], 0.0).then_inc(mask_done, 1)
                pool.tensor_copy(mask[:, SEQ - P:SEQ], c["mask"][:]).then_inc(mask_done, 1)

                def rms(b):
                    pool.wait_ge(mv_done, (b + 1) * TT)
                    pool.tensor_scalar(rstd[:], mv[:, :, 1], LN_EPS, None, ALU.add).then_inc(rstd_done, 1)
                    pool.wait_ge(rstd_done, b * 2 + 1)
                    pool.tensor_tensor(rstd[:], rstd[:], c["minus_half"][:, 0:TT], ALU.pow).then_inc(rstd_done, 1)

                def cut_item(i):
                    name = ITEMS[i]
                    hi, lo = (w_hi[:, WEIGHTS[name]], w_lo[:, WEIGHTS[name]]) if name in WEIGHTS else (c_hi[:], c_lo[:])
                    pool.wait_ge(staged[i % 2], 16 * (i // 2 + 1))
                    if name == "ctx1":
                        pool.wait_ge(proj_psum, 8)
                    if i >= ON_ACT:
                        pool.tensor_copy(hi, stage[:, i % 2]).then_inc(hi_done, 1)
                    pool.wait_ge(hi_done, i + 1)
                    if i - 1 in ON_DVE:
                        pool.wait_ge(cut, i)
                    pool.tensor_tensor(lo, stage[:, i % 2], hi.bitcast(F32), ALU.subtract).then_inc(cut, 1)
                cut_item(0)
                cut_item(2)
                rms(0)
                for i in range(3, 6):
                    cut_item(i)
                for b in range(1, BATCH):
                    rms(b)

            @block.scalar
            def _(act):
                for i in range(ON_ACT):
                    hi = w_hi[:, WEIGHTS[ITEMS[i]]] if ITEMS[i] in WEIGHTS else c_hi[:]
                    act.wait_ge(staged[i % 2], 16 * (i // 2 + 1))
                    act.copy(hi, stage[:, i % 2]).then_inc(hi_done, 1)
                with act.Fori(0, BATCH) as b:
                    for j in range(12):
                        what, n = divmod(j, 4)
                        for t in range(TT if j == 8 else 0):
                            act.wait_ge(xT_psum, b * TT + t + 1)
                            act.copy(xT_hi[:, :, t * P:(t + 1) * P],
                                     banks[4 + t][:].rearrange("p (k n) -> p k n", k=KD)).then_inc(xT_hi_done, 1)
                        if what == 2 or j % 2 == 0:
                            act.wait_ge(proj_psum, b * 12 + j + 1)
                        if what == 2:
                            if j == 8:
                                act.wait_ge(zeroed, 1)
                            for h in range(2):
                                r = slice(HD * h, HD * (h + 1))
                                act.copy(q_pad[r, 4 * n + h], banks[j % 4][r, :]).then_inc(proj_act, 1)
                        elif j % 2 == 0:
                            act.copy((kT, v)[what][:, n], banks[j % 4][:]).then_inc(proj_act, 1)
                    for i in range(STEPS):
                        if i < U:
                            act.wait_ge(max_done, b * U + i + 1)
                            if i >= 4:
                                act.wait_ge(pT_psum, b * U + i - 3)
                            act.activation(probs[:, i % 4, 0:width(i)], rows[:, i % 4, 0:width(i)], ACT.Exp,
                                           bias=neg_max[:, i % 4:i % 4 + 1], scale=-1.0,
                                           accum_out=row_sum[:, i % 4:i % 4 + 1]).then_inc(exp_done, 1)
                        u = i - 3
                        if 0 <= u < U and on_act(u):
                            take_pT(act, act.copy, u, b)
                        if i >= 20 and (i - 20) % HEADS == 0:
                            qt = (i - 20) // HEADS
                            act.wait_ge(pv_done, b * U + (qt + 1) * HEADS)
                            if qt > 0:
                                act.wait_ge(y_psum, b * TT + qt)
                            act.copy(oT_hi[:], banks[5 + qt % 2][:].rearrange("p (k n) -> p k n", k=KD)).then_inc(oT_hi_done, 1)

            @block.vector
            def _(dve):
                dve.memset(q_pad[:], 0.0).then_inc(zeroed, 1)
                dve.wait_ge(mask_done, 2)
                for i in ON_DVE:
                    dve.wait_ge(hi_done, i + 1)
                    dve.wait_ge(cut, i)
                    dve.tensor_tensor(w_lo[:, WEIGHTS[ITEMS[i]]], stage[:, i % 2], w_hi[:, WEIGHTS[ITEMS[i]]].bitcast(F32),
                                      ALU.subtract).then_inc(cut, 1)
                with dve.Fori(0, BATCH) as b:
                    hold(dve, x_loaded, b * 16 + 16, passed)
                    for t in range(TT):
                        dve.bn_stats(stats[:, t, :], xres[:, b * TT + t, :]).then_inc(stats_done, 1)
                    for t in range(TT):
                        hold(dve, stats_done, b * TT + t + 1, passed)
                        dve.bn_aggr(mv[:, t, :], stats[:, t, :]).then_inc(mv_done, 1)
                    dve.wait_ge(rstd_done, b * 2 + 2)
                    for t in range(TT):
                        dve.tensor_scalar(rows[:, t, :], xres[:, b * TT + t, :], mv[:, t, 0:1], rstd[:, t:t + 1],
                                          ALU.subtract, ALU.mult).then_inc(xn_done, 1)
                    dve.wait_ge(zeroed, 1)
                    for j in range(12):
                        what, n = divmod(j, 4)
                        for t in range(TT if j == 8 else 0):
                            dve.wait_ge(xT_hi_done, b * TT + t + 1)
                            s = slice(t * P, (t + 1) * P)
                            dve.tensor_tensor(xT_lo[:, :, s], banks[4 + t][:].rearrange("p (k n) -> p k n", k=KD),
                                              xT_hi[:, :, s].bitcast(F32), ALU.subtract).then_inc(xT_lo_done, 1)
                        if what == 2 or j % 2:
                            dve.wait_ge(proj_psum, b * 12 + j + 1)
                        if what == 2:
                            for h in range(2, 4):
                                r = slice(HD * h, HD * (h + 1))
                                dve.tensor_copy(q_pad[r, 4 * n + h], banks[j % 4][r, :]).then_inc(proj_dve, 1)
                        elif j % 2:
                            dve.tensor_copy((kT, v)[what][:, n], banks[j % 4][:]).then_inc(proj_dve, 1)
                    for i in range(STEPS):
                        if 0 <= i - 2 < U:
                            u = i - 2
                            dve.wait_ge(exp_done, b * U + u + 1)
                            dve.reciprocal(inv_sum[:, u % 4:u % 4 + 1], row_sum[:, u % 4:u % 4 + 1]).then_inc(inv_done, 1)
                        if i < U:
                            hold(dve, scores, b * U + i + 1, passed)
                            dve.tensor_tensor_reduce(out=rows[:, i % 4, 0:width(i)], in0=banks[i % 3][:, 0:width(i)],
                                                     in1=mask[:, SEQ - width(i):SEQ], scale=-scale, scalar=3e38,
                                                     op0=ALU.add, op1=ALU.min,
                                                     accum_out=neg_max[:, i % 4:i % 4 + 1]).then_inc(max_done, 1)
                        if 0 <= i - 2 < U:
                            u = i - 2
                            dve.wait_ge(inv_done, b * U + u + 1)
                            dve.tensor_scalar(probs[:, u % 4, 0:width(u)], probs[:, u % 4, 0:width(u)],
                                              inv_sum[:, u % 4:u % 4 + 1], None, ALU.mult).then_inc(norm_done, 1)
                        u = i - 3
                        if 0 <= u < U and not on_act(u):
                            take_pT(dve, dve.tensor_copy, u, b)
                        if i >= 20 and (i - 20) % HEADS == 0:
                            qt = (i - 20) // HEADS
                            dve.wait_ge(oT_hi_done, b * TT + qt + 1)
                            dve.tensor_tensor(oT_lo[:], banks[5 + qt % 2][:].rearrange("p (k n) -> p k n", k=KD),
                                              oT_hi[:].bitcast(F32), ALU.subtract).then_inc(oT_lo_done, 1)
                        if i >= 23 and (i - 23) % HEADS == 0:
                            qt = (i - 23) // HEADS
                            dve.wait_ge(y_psum, b * TT + qt + 1)
                            dve.tensor_tensor(xres[:, b * TT + qt, :], xres[:, b * TT + qt, :], banks[7][:],
                                              ALU.add).then_inc(y_added, 1)

            @block.tensor
            def _(pe):
                with pe.Fori(0, BATCH) as b:
                    def turn_rows():
                        for t in range(TT):
                            pe.wait_ge(xn_done, b * TT + t + 1)
                            for k in range(KD):
                                last = pe.transpose(banks[4 + t][:, k * P:(k + 1) * P], rows[:, t, k * P:(k + 1) * P],
                                                    c["ident"][:])
                            last.then_inc(xT_psum, 1)
                    for j in range(12):
                        what, n = divmod(j, 4)
                        if j >= 4:
                            pe.wait_ge(proj_dve if j % 2 else proj_act, b * PIECES + (j - 4) // 2 + 1)
                        if j == 0:
                            pe.wait_ge(cut, b * 4 + 2)
                        if j == 4:
                            pe.wait_ge(cut, 3)
                        if j == 8:
                            turn_rows()
                            pe.wait_ge(cut, 4)
                            pe.wait_ge(xT_lo_done, b * TT + TT)
                        s = slice(n * P, (n + 1) * P)
                        for k in range(KD):
                            if what == 2:
                                ops = (w_hi[:, 0, k, s], w_lo[:, 0, k, s], xT_hi[:, k], xT_lo[:, k])
                            elif what == 0:
                                ops = (w_hi[:, 1, k, s], w_lo[:, 1, k, s], c_hi[:, k], c_lo[:, k])
                            else:
                                ops = (c_hi[:, k, s], c_lo[:, k, s], w_hi[:, 2, k], w_lo[:, 2, k])
                            last = mm3(pe, banks[j % 4][:], *ops, k == 0, k == KD - 1)
                        last.then_inc(proj_psum, 1)
                    pe.wait_ge(proj_act, b * PIECES + PIECES)
                    pe.wait_ge(proj_dve, b * PIECES + PIECES)

                    def score(u):
                        qt, head = divmod(u, HEADS)
                        if u >= 3:
                            pe.wait_ge(max_done, b * U + u - 2)
                        pe.matmul(banks[u % 3][:, 0:width(u)], q_pad[:, head, qt * P:(qt + 1) * P],
                                  kT[:, head // 4, 0:width(u)], start=True, stop=True).then_inc(scores, 1)
                    for u in range(AHEAD):
                        score(u)
                    for i in range(STEPS):
                        if 0 <= i - 3 < U:
                            u = i - 3
                            pe.wait_ge(norm_done, b * U + u + 1)
                            if u >= 2:
                                sem_, per, n = taken(u - 2)
                                pe.wait_ge(sem_, b * per + n)
                            for kt in range(u // HEADS + 1):
                                last = pe.transpose(banks[3 + u % 2][:, kt * P:(kt + 1) * P],
                                                    probs[:, u % 4, kt * P:(kt + 1) * P], c["ident"][:])
                            last.then_inc(pT_psum, 1)
                        if i + AHEAD < U:
                            score(i + AHEAD)
                        if 0 <= i - 4 < U:
                            u = i - 4
                            qt, head = divmod(u, HEADS)
                            sem_, per, n = taken(u)
                            pe.wait_ge(sem_, b * per + n)
                            if head == 0 and qt >= 2:
                                pe.wait_ge(oT_lo_done, b * TT + qt - 1)
                            r = slice(HD * (head % 4), HD * (head % 4 + 1))
                            q = slice((head // 4) * P, (head // 4 + 1) * P)
                            for kt in range(qt + 1):
                                last = pe.matmul(banks[5 + qt % 2][r, q], v[:, kt, head * HD:(head + 1) * HD],
                                                 probsT[:, u % 2, kt], start=(kt == 0), stop=(kt == qt))
                            last.then_inc(pv_done, 1)
                        if i >= 22 and (i - 22) % HEADS == 0:
                            qt = (i - 22) // HEADS
                            pe.wait_ge(oT_lo_done, b * TT + qt + 1)
                            pe.wait_ge(cut, 5)
                            if qt > 0:
                                pe.wait_ge(y_added, b * TT + qt)
                            for k in range(KD):
                                last = mm3(pe, banks[7][:], oT_hi[:, k], oT_lo[:, k], w_hi[:, 3, k], w_lo[:, 3, k],
                                           k == 0, k == KD - 1)
                            last.then_inc(y_psum, 1)


def mamba_scan(nc, sem, c, xres, banks, a, ln_mv, ln_rstd, yT):
    UP = 2
    UNITS = NS // UP
    WR = 4
    HALF = GI // 2
    NIN = 2 * GI
    RB = DR + 2 * NS
    assert RB + 2 * NS == P
    outer = ExitStack()
    with outer:
        def sb(name, shape, dt, ctx=outer):
            return ctx.enter_context(nc.sbuf_tensor(name, shape, dt))
        conv_w = sb("conv_w", [P, GI, 4], F32)
        conv_b = sb("conv_b", [P, GI], F32)
        w_xproj = sb("w_xproj", [P, GI, RB], F32)
        w_dt = sb("w_dt", [DR, DI], F32)
        b_dt = sb("b_dt", [P, GI], F32)
        A = sb("A", [P, GI, NS], F32)
        Dp = sb("Dp", [P, GI], F32)
        stats = sb("m_stats", [P, TT, 6], F32)
        mv = sb("m_mv", [P, TT, 2], F32)
        rstd = sb("m_rstd", [P, TT], F32)
        gate = sb("gate", [P, GI, SEQ], F32)
        delta = sb("delta", [P, GI, SEQ], F32)
        du = sb("du", [P, GI, SEQ], F32)
        dA = sb("dA", [P, 2, UP, SEQ], F32)
        hs = sb("hs", [P, WR, UP, SEQ], F32)
        dbl = sb("dbl", [DR, SEQ], F32)
        bc_parts = sb("bc_parts", [P, SEQ], F32R)
        pick_bc = sb("pick_bc", [P, 2 * NS], F32R)
        early = ExitStack()
        with early:
            xm = sb("xm", [P, TT, D], F32, early)
            xT_hi = sb("m_xT_hi", [P, KD, SEQ], F32R, early)
            xT_lo = sb("m_xT_lo", [P, KD, SEQ], F32R, early)
            w_stage = sb("w_in_stage", [P, 2, KD, P], F32, early)
            w_hi = sb("w_in_hi", [P, 2, KD, P], F32R, early)
            w_lo = sb("w_in_lo", [P, 2, KD, P], F32R, early)
            raw = sb("raw", [P, 3, SEQ + 3], F32, early)
            pre = sb("pre", [P, 3, SEQ], F32, early)
            th = sb("th", [P, 3, SEQ], F32, early)
            e_t = sb("e_t", [P, HALF, SEQ], F32, early)
            assert TT == HALF and D == SEQ
            e_half = (e_t, xm)
            w_t = sb("w_t", [P, HALF, SEQ], F32, early)
        Bs = sb("Bs", [P, NS, SEQ], F32)
        Cs = sb("Cs", [P, NS, SEQ], F32)

        passed = sem("m_passed")
        par_loaded = sem("par_loaded")
        par_act = sem("par_act")
        par_done = sem("par_done")
        pads = sem("pads")
        kept = sem("kept")
        win_loaded = [sem("win_loaded0"), sem("win_loaded1")]
        win_hi = sem("win_hi")
        win_lo = sem("win_lo")
        stats_done = sem("m_stats_done")
        mv_done = sem("m_mv_done")
        rstd_done = sem("m_rstd_done")
        xm_done = sem("xm_done")
        xT_psum = sem("m_xT_psum")
        xT_hi_done = sem("m_xT_hi_done")
        xT_lo_done = sem("m_xT_lo_done")
        in_psum = sem("in_psum")
        raw_done = sem("raw_done")
        pre_done = sem("pre_done")
        tap_done = sem("tap_done")
        tanh_done = sem("tanh_done")
        silu_done = sem("silu_done")
        dbl_psum = sem("dbl_psum")
        dbl_act = sem("dbl_act")
        dbl_lo_done = sem("dbl_lo_done")
        pick_set = sem("pick_set")
        dt_psum = sem("dt_psum")
        absx_done = sem("absx_done")
        relu_done = sem("relu_done")
        expx_done = sem("expx_done")
        onep_done = sem("onep_done")
        fix_done = sem("fix_done")
        ln_done = sem("ln_done")
        delta_done = sem("delta_done")
        skip_done = sem("skip_done")
        du_done = sem("du_done")
        bc_psum = sem("bc_psum")
        bc_act = sem("bc_act")
        bc_dve = sem("bc_dve")
        dA_done = sem("dA_done")
        dBu_done = sem("dBu_done")
        scan_done = sem("scan_done")
        hC_done = sem("hC_done")
        unit_summed = sem("unit_summed")
        y_gated = sem("y_gated")

        with nc.Block() as block:
            @block.sync
            def _(sp):
                for dst, name in ((conv_w, "conv_w"), (conv_b, "conv_b"), (w_xproj, "w_xproj"), (w_dt, "w_dt"),
                                  (b_dt, "b_dt"), (A, "A_log"), (Dp, "Dp")):
                    sp.dma_start(dst[:], a[name]).then_inc(par_loaded, 16)
                with sp.Fori(0, BATCH) as b:
                    hold(sp, y_gated, b * GI + 1, passed)
                    sp.wait_ge(win_lo, b * NIN + 1)
                    for n in range(NIN):
                        if n >= 2:
                            sp.wait_ge(win_lo, b * NIN + n)
                        sp.dma_start(w_stage[:, n % 2], a["w_in"][n]).then_inc(win_loaded[n % 2], 16)

            @block.gpsimd
            def _(pool):
                pool.sem_inc(win_lo, 1)
                pool.tensor_tensor(pick_bc[:], c["ident"][:, DR:RB], c["ident"][:, RB:P], ALU.add).then_inc(pick_set, 1)
                pool.memset(bc_parts[0:DR].bitcast(F32), 0.0).then_inc(pick_set, 1)
                for r in range(2):
                    pool.memset(dA[:, r, :, 0:1], 0.0).then_inc(scan_done, 1)
                for r in range(WR):
                    pool.memset(hs[:, r], 0.0).then_inc(unit_summed, 1)
                with pool.Fori(0, BATCH) as b:
                    hold(pool, y_gated, b * GI + 1, passed)
                    pool.memset(raw[:, :, 0:3], 0.0).then_inc(pads, 1)
                    hold(pool, mv_done, (b + 1) * TT, passed)
                    r = rstd[:]
                    pool.tensor_scalar(r, mv[:, :, 1], LN_EPS, None, ALU.add).then_inc(rstd_done, 1)
                    pool.wait_ge(rstd_done, b * 2 + 1)
                    pool.tensor_tensor(r, r, c["minus_half"][:, 0:TT], ALU.pow).then_inc(rstd_done, 1)
                    def cut(n):
                        pool.wait_ge(win_hi, b * NIN + n + 1)
                        pool.tensor_tensor(w_lo[:, n % 2], w_stage[:, n % 2], w_hi[:, n % 2].bitcast(F32),
                                           ALU.subtract).then_inc(win_lo, 1)

                    def drive_all(hf):
                        pool.wait_ge(delta_done, (b * 2 + hf) * 2 + 2)
                        pool.wait_ge(skip_done, b * 2 + hf + 1)
                        pool.wait_ge(dbl_psum, b + 1)
                        s = slice(hf * HALF, (hf + 1) * HALF)
                        pool.tensor_tensor(du[:, s], du[:, s], delta[:, s], ALU.mult).then_inc(du_done, 1)
                    for n in range(GI + 2):
                        cut(n)
                    for hf in range(2):
                        s = slice(hf * HALF, (hf + 1) * HALF)
                        hold(pool, silu_done, b * NIN + (hf + 1) * HALF + 1, passed)
                        pool.tensor_tensor(yT[:, s, bass.ds(b * SEQ, SEQ)], du[:, s], bc_free(Dp[:, s], SEQ),
                                           ALU.mult).then_inc(skip_done, 1)
                    for n in range(GI + 2, GI + 4):
                        cut(n)
                    drive_all(0)
                    for n in range(GI + 4, NIN):
                        cut(n)
                    drive_all(1)
                    hold(pool, du_done, b * 2 + 2, passed)
                    hold(pool, bc_act, b * NS + NS // 2, passed)
                    hold(pool, bc_dve, b * NS + NS // 2, passed)
                    with pool.Fori(0, GI) as g:
                        base = b * (GI * UNITS) + g * UNITS

                        def drive(u):
                            hold(pool, unit_summed, base + u + 1, passed)
                            pool.tensor_tensor(hs[:, u % WR], bc_mid(du[:, g], UP), Bs[:, UP * u:UP * (u + 1)],
                                               ALU.mult).then_inc(dBu_done, 1)
                        for u in range(UNITS):
                            drive(u)

            @block.scalar
            def _(act):
                act.wait_ge(par_loaded, 7 * 16)
                act.activation(A[:], A[:], ACT.Exp).then_inc(par_act, 1)
                act.activation(conv_w[:], conv_w[:], ACT.Identity, scale=0.5).then_inc(par_done, 1)
                act.activation(conv_b[:], conv_b[:], ACT.Identity, scale=0.5).then_inc(par_done, 1)
                act.wait_ge(par_act, 1)
                act.activation(A[:], A[:], ACT.Identity, scale=-1.0).then_inc(par_done, 1)
                with act.Fori(0, BATCH) as b:
                    act.wait_ge(y_gated, b * GI + 1)
                    for t in range(TT):
                        act.wait_ge(xT_psum, b * TT + t + 1)
                        act.copy(xT_hi[:, :, t * P:(t + 1) * P],
                                 banks[4 + t][:].rearrange("p (k n) -> p k n", k=KD)).then_inc(xT_hi_done, 1)

                    def cut(n):
                        act.wait_ge(win_loaded[n % 2], (b * (NIN // 2) + n // 2 + 1) * 16)
                        act.wait_ge(in_psum, b * NIN + max(n - 1, 0) + 1)
                        act.copy(w_hi[:, n % 2], w_stage[:, n % 2]).then_inc(win_hi, 1)

                    def take(n):
                        act.wait_ge(in_psum, b * NIN + n + 2)
                        act.wait_ge(silu_done, b * NIN + max(n - 2, 0) + 1)
                        if n == 0:
                            act.wait_ge(par_done, 3)
                            act.wait_ge(pads, b + 1)
                        if n < GI:
                            act.copy(raw[:, n % 3, 3:SEQ + 3], banks[n % 4][:]).then_inc(raw_done, 1)
                            act.activation(pre[:, n % 3], banks[n % 4][:], ACT.Identity, bias=conv_b[:, n:n + 1],
                                           scale=conv_w[:, n, 3:4]).then_inc(pre_done, 1)
                        else:
                            act.activation(pre[:, n % 3], banks[n % 4][:], ACT.Identity, scale=0.5).then_inc(pre_done, 1)

                    def tanh(n):
                        if n < GI:
                            act.wait_ge(tap_done, b * GI * 3 + 3 * (n + 1))
                        else:
                            act.wait_ge(pre_done, b * NIN + n + 1)
                        act.activation(th[:, n % 3], pre[:, n % 3], ACT.Tanh).then_inc(tanh_done, 1)
                    def softplus(hf):
                        act.wait_ge(absx_done, b * GI + (hf + 1) * HALF)
                        act.activation(e_half[hf][:], e_half[hf][:], ACT.Exp, scale=-1.0).then_inc(expx_done, 1)

                    def logarithm(hf):
                        act.wait_ge(fix_done, b * 2 + hf + 1)
                        act.activation(w_t[:], w_t[:], ACT.Ln).then_inc(ln_done, 1)

                    def abs_x(g):
                        act.wait_ge(dt_psum, b * GI + g + 1)
                        act.activation(e_half[g // HALF][:, g % HALF], banks[5 + g % 3][:], ACT.Abs,
                                       bias=b_dt[:, g:g + 1]).then_inc(absx_done, 1)
                    cut(0)
                    cut(1)
                    for n in range(GI):
                        take(n)
                        cut(n + 2)
                        if n >= 1:
                            tanh(n - 1)
                    tanh(GI - 1)
                    act.wait_ge(dbl_psum, b + 1)
                    act.copy(dbl[:], banks[4][0:DR, :]).then_inc(dbl_act, 1)
                    act.copy(bc_parts[DR:RB], banks[4][DR:RB, :]).then_inc(dbl_act, 1)
                    for g in range(GI):
                        abs_x(g)
                    softplus(0)
                    softplus(1)
                    take(GI)
                    cut(GI + 2)
                    logarithm(0)
                    take(GI + 1)
                    cut(GI + 3)
                    tanh(GI)
                    logarithm(1)
                    for n in range(GI + 2, NIN):
                        take(n)
                        if n + 2 < NIN:
                            cut(n + 2)
                        tanh(n - 1)
                    tanh(NIN - 1)
                    act.wait_ge(delta_done, b * 4 + 4)
                    act.wait_ge(silu_done, b * NIN + NIN + 1)
                    for i in range(0, 2 * NS, 2):
                        act.wait_ge(bc_psum, b * 2 * NS + i + 1)
                        act.copy((Bs if i < NS else Cs)[:, i % NS], banks[i % 4][:]).then_inc(bc_act, 1)
                    with act.Fori(0, GI) as g:
                        base = b * (GI * UNITS) + g * UNITS
                        for u in range(UNITS):
                            act.wait_ge(scan_done, base + u + 1)
                            for n in range(UP):
                                act.activation(dA[:, u % 2, n, 1:SEQ], delta[:, g, 1:SEQ], ACT.Exp,
                                               scale=A[:, g, UP * u + n:UP * u + n + 1]).then_inc(dA_done, 1)

            @block.vector
            def _(dve):
                dve.sem_inc(y_gated, 1)
                dve.sem_inc(silu_done, 1)
                with dve.Fori(0, BATCH) as b:
                    for t in range(TT):
                        dve.bn_stats(stats[:, t, :], xres[:, b * TT + t, :]).then_inc(stats_done, 1)
                    for t in range(TT):
                        hold(dve, stats_done, b * TT + t + 1, passed)
                        dve.bn_aggr(mv[:, t, :], stats[:, t, :]).then_inc(mv_done, 1)
                    dve.wait_ge(rstd_done, b * 2 + 2)
                    dve.tensor_copy(ln_mv[:, bass.ds(b * TT, TT), :], mv[:]).then_inc(kept, 1)
                    dve.tensor_copy(ln_rstd[:, bass.ds(b * TT, TT)], rstd[:]).then_inc(kept, 1)
                    for t in range(TT):
                        dve.tensor_scalar(xm[:, t, :], xres[:, b * TT + t, :], mv[:, t, 0:1],
                                          rstd[:, t:t + 1], ALU.subtract, ALU.mult).then_inc(xm_done, 1)
                    for t in range(TT):
                        dve.wait_ge(xT_hi_done, b * TT + t + 1)
                        s = slice(t * P, (t + 1) * P)
                        dve.tensor_tensor(xT_lo[:, :, s], banks[4 + t][:].rearrange("p (k n) -> p k n", k=KD),
                                          xT_hi[:, :, s].bitcast(F32), ALU.subtract).then_inc(xT_lo_done, 1)

                    def taps(n):
                        dve.wait_ge(raw_done, b * GI + n + 1)
                        for j in range(3):
                            if j == 0:
                                dve.wait_ge(pre_done, b * NIN + n + 1)
                            else:
                                dve.wait_ge(tap_done, b * GI * 3 + 3 * n + j)
                            dve.scalar_tensor_tensor(pre[:, n % 3], raw[:, n % 3, j:j + SEQ], conv_w[:, n, j:j + 1],
                                                     pre[:, n % 3], ALU.mult, ALU.add).then_inc(tap_done, 1)

                    def silu(n):
                        dve.wait_ge(tanh_done, b * NIN + n + 1)
                        dst = du[:, n] if n < GI else gate[:, n - GI]
                        dve.scalar_tensor_tensor(dst, th[:, n % 3], 1.0, pre[:, n % 3], ALU.add,
                                                 ALU.mult).then_inc(silu_done, 1)
                    for n in range(GI):
                        taps(n)
                        if n >= 1:
                            silu(n - 1)
                    silu(GI - 1)
                    dve.wait_ge(dbl_act, b * 2 + 2)
                    dve.tensor_tensor(bc_parts[RB:P], banks[4][DR:RB, :], bc_parts[DR:RB].bitcast(F32),
                                      ALU.subtract).then_inc(dbl_lo_done, 1)
                    for g in range(GI):
                        dve.wait_ge(absx_done, b * GI + g + 1)
                        dve.tensor_scalar(delta[:, g], banks[5 + g % 3][:], b_dt[:, g:g + 1], 0.0,
                                          ALU.add, ALU.max).then_inc(relu_done, 1)
                    for hf in range(2):
                        s = slice(hf * HALF, (hf + 1) * HALF)
                        e = e_half[hf][:].rearrange("p g s -> p (g s)")
                        dve.wait_ge(expx_done, b * 2 + hf + 1)
                        if hf == 1:
                            dve.wait_ge(delta_done, b * 4 + 2)
                        dve.tensor_scalar(w_t[:], e_half[hf][:], 1.0, None, ALU.add).then_inc(onep_done, 1)
                        dve.wait_ge(onep_done, b * 2 + hf + 1)
                        dve.scalar_tensor_tensor(e, w_t[:].rearrange("p g s -> p (g s)"), -1.0, e, ALU.add,
                                                 ALU.subtract).then_inc(fix_done, 1)
                        dve.wait_ge(relu_done, b * GI + (hf + 1) * HALF)
                        dve.wait_ge(fix_done, b * 2 + hf + 1)
                        dve.tensor_tensor(delta[:, s], delta[:, s], e_half[hf][:], ALU.subtract).then_inc(delta_done, 1)
                        dve.wait_ge(ln_done, b * 2 + hf + 1)
                        dve.wait_ge(delta_done, b * 4 + 2 * hf + 1)
                        dve.tensor_tensor(delta[:, s], delta[:, s], w_t[:], ALU.add).then_inc(delta_done, 1)
                    for n in range(GI, NIN):
                        silu(n)
                    dve.wait_ge(delta_done, b * 4 + 4)
                    for i in range(1, 2 * NS, 2):
                        dve.wait_ge(bc_psum, b * 2 * NS + i + 1)
                        dve.tensor_copy((Bs if i < NS else Cs)[:, i % NS], banks[i % 4][:]).then_inc(bc_dve, 1)
                    dve.wait_ge(bc_act, b * NS + NS)
                    dve.wait_ge(bc_dve, b * NS + NS)

                    def unit_loop(g, first):
                        base = b * (GI * UNITS) + g * UNITS

                        def scan(u):
                            dve.wait_ge(dA_done, (base + u + 1) * UP)
                            dve.wait_ge(dBu_done, base + u + 1)
                            w = hs[:, u % WR].rearrange("p n s -> p (n s)")
                            dve.tensor_tensor_scan(w, dA[:, u % 2].rearrange("p n s -> p (n s)"), w, 0.0,
                                                   ALU.mult, ALU.add).then_inc(scan_done, 1)

                        def read_out(u):
                            dve.wait_ge(scan_done, base + u + 3)
                            dve.tensor_tensor(hs[:, u % WR], hs[:, u % WR], Cs[:, UP * u:UP * (u + 1)],
                                              ALU.mult).then_inc(hC_done, 1)
                        scan(0)
                        scan(1)
                        if not first:
                            gated(g - 1)
                        read_out(0)
                        for u in range(2, UNITS):
                            scan(u)
                            read_out(u - 1)
                        read_out(UNITS - 1)

                    def gated(g):
                        dve.wait_ge(unit_summed, b * (GI * UNITS) + (g + 1) * UNITS + WR)
                        dve.tensor_tensor(yT[:, g, bass.ds(b * SEQ, SEQ)], banks[7][:], gate[:, g], ALU.mult).then_inc(y_gated, 1)
                    unit_loop(0, True)
                    with dve.Fori(1, GI) as g:
                        unit_loop(g, False)
                    gated(GI - 1)
                    dve.wait_ge(y_gated, b * GI + GI + 1)

            @block.tensor
            def _(pe):
                pe.sem_inc(in_psum, 1)
                with pe.Fori(0, BATCH) as b:
                    for t in range(TT):
                        pe.wait_ge(xm_done, b * TT + t + 1)
                        for k in range(KD):
                            last = pe.transpose(banks[4 + t][:, k * P:(k + 1) * P], xm[:, t, k * P:(k + 1) * P],
                                                c["ident"][:])
                        last.then_inc(xT_psum, 1)
                    pe.wait_ge(xT_lo_done, b * TT + TT)
                    def project_in(n):
                        pe.wait_ge(win_lo, b * NIN + n + 2)
                        if n >= 4:
                            pe.wait_ge(pre_done, b * NIN + n - 3)
                        for k in range(KD):
                            last = mm3(pe, banks[n % 4][:], w_hi[:, n % 2, k], w_lo[:, n % 2, k], xT_hi[:, k], xT_lo[:, k],
                                       k == 0, k == KD - 1)
                        last.then_inc(in_psum, 1)
                    def project_u(k):
                        pe.wait_ge(silu_done, b * NIN + k + 2)
                        last = pe.matmul(banks[4][0:RB, :], w_xproj[:, k], du[:, k], start=(k == 0), stop=(k == GI - 1))
                        if k == GI - 1:
                            last.then_inc(dbl_psum, 1)
                    for n in range(GI):
                        project_in(n)
                        if n >= 3:
                            project_u(n - 3)
                    for k in range(GI - 3, GI):
                        project_u(k)
                    pe.wait_ge(dbl_act, b * 2 + 1)
                    for g in range(GI):
                        if g >= 3:
                            pe.wait_ge(relu_done, b * GI + g - 2)
                        pe.matmul(banks[5 + g % 3][:], w_dt[:, g * P:(g + 1) * P], dbl[0:DR, :],
                                  start=True, stop=True).then_inc(dt_psum, 1)
                    for n in range(GI, NIN):
                        project_in(n)
                    pe.wait_ge(dbl_lo_done, b + 1)
                    pe.wait_ge(pick_set, 2)
                    for i in range(2 * NS):
                        if i == 0:
                            pe.wait_ge(pre_done, b * NIN + NIN)
                        if i >= 4:
                            pe.wait_ge(bc_dve if i % 2 else bc_act, b * NS + (i - 4) // 2 + 1)
                        pick = pick_bc[:, i:i + 1].to_broadcast([P, P])
                        pe.matmul(banks[i % 4][:], pick, bc_parts[:], start=True, stop=True).then_inc(bc_psum, 1)
                    hold(pe, bc_act, b * NS + NS, passed)
                    hold(pe, bc_dve, b * NS + NS, passed)
                    hold(pe, skip_done, b * 2 + 2, passed)
                    with pe.Fori(0, GI) as g:
                        pe.wait_ge(y_gated, b * GI + g + 1)
                        pe.matmul(banks[7][:], c["ident"][:], yT[:, g, bass.ds(b * SEQ, SEQ)], start=True, stop=False)
                        for u in range(UNITS):
                            pe.wait_ge(hC_done, b * (GI * UNITS) + g * UNITS + u + 1)
                            for n in range(UP):
                                last = pe.matmul(banks[7][:], c["ident"][:], hs[:, u % WR, n], start=False,
                                                 stop=(u == UNITS - 1 and n == UP - 1))
                            last.then_inc(unit_summed, 1)


def feed_forward(nc, sem, c, xres, banks, a, ln_mv, ln_rstd, yT):
    KF = FF // P
    outer = ExitStack()
    with outer:
        def sb(name, shape, dt, ctx=outer):
            return ctx.enter_context(nc.sbuf_tensor(name, shape, dt))
        wo_hi = sb("wo_hi", [P, GI, D], F32R)
        wo_lo = sb("wo_lo", [P, GI, D], F32R)
        w1q = sb("w1q", [P, KD, FF], BF16)
        w2q = sb("w2q", [P, KF, D], BF16)
        n1 = sb("n1", [P, D], F32)
        n2 = sb("n2", [P, D], F32)
        b1 = sb("b1", [P, FF], F32)
        b2 = sb("b2", [P, D], F32)
        part = sb("part", [P, 8], F32)
        round_c = sb("round_c", [P, 2], F32)
        g = sb("g", [P, 2], F32)
        g_inv = sb("g_inv", [P, 2], F32)
        g_127 = sb("g_127", [P, 2], F32)

        y_hi = sb("y_hi", [P, GI, P], F32R)
        y_lo = sb("y_lo", [P, GI, P], F32R)
        xm = sb("p_xm", [P, D], F32)
        xr = sb("xr", [P, D], F32)
        sq = sb("sq", [P, D], F32)
        x1 = sb("x1", [P, NT, D], F32)
        qt = sb("qt", [P, D], F32)
        qx = sb("qx", [P, D], BF16)
        qxT = sb("qxT", [P, KD, P], BF16)
        fq = sb("fq", [P, FF], BF16)
        ss = sb("ss", [P, 2], F32)
        rs = sb("rs", [P, 2], F32)
        am = sb("am", [P, 2], F32)
        quant = sb("quant", [P, 2], F32)
        unscale = sb("unscale", [P, NT, 2], F32)

        with ExitStack() as early:
            wo = sb("wo_stage", [P, GI // 2, D], F32, early)
            stage = sb("w_stage", [P, KD * FF], F32, early)
            wo_half = (wo[:], stage[:, KD * FF - GI // 2 * D:].rearrange("p (k n) -> p k n", n=D))
        f1 = sb("f1", [P, FF], F32)
        fqT = sb("fqT", [P, KF, P], BF16)
        f2 = sb("f2", [P, D], F32)
        x1b = sb("x1b", [P, D], F32)
        o2 = sb("o2", [P, D], F32)
        scale2 = sb("scale2", [P, 1], F32)
        scale2_done = sem("scale2_done")

        CHUNK = 2048
        CHUNKS = KD * FF // CHUNK
        pieces = [(stage[:, n * CHUNK:(n + 1) * CHUNK], q[:].rearrange("p k n -> p (k n)")[:, n * CHUNK:(n + 1) * CHUNK], m)
                  for m, q in enumerate((w1q, w2q)) for n in range(CHUNKS)]
        ACT_SUMS = (4, 6)
        w_loaded = [sem(f"w_chunk{n}_loaded") for n in range(2 * CHUNKS)]
        wo_loaded, rows_loaded = [sem("wo_loaded0"), sem("wo_loaded1")], sem("rows_loaded")
        assert CHUNK == GI // 2 * D
        sum_dve, sum_act, total_psum, g_done, wo_cut = sem("sum_dve"), sem("sum_act"), sem("total_psum"), sem("g_done"), sem("wo_cut")
        round_set, w_shifted, w_top, w_quantised = sem("round_set"), sem("w_shifted"), sem("w_top"), sem("w_quantised")
        passed = sem("p_passed")
        y_hi_done, y_lo_done, out_psum = sem("y_hi_done"), sem("y_lo_done"), sem("out_psum")
        xm_done, xr_done, ss1, rs1, x1_done = sem("p_xm_done"), sem("xr_done"), sem("ss1"), sem("rs1"), sem("x1_done")
        am1, qt1, qx_done, qxT_psum, qxT_done = sem("am1"), sem("qt1"), sem("qx_done"), sem("qxT_psum"), sem("qxT_done")
        ff1_psum, f1_done, gelu_done, am2, fq_tmp, fq_done = (sem("ff1_psum"), sem("f1_done"), sem("gelu_done"), sem("am2"),
                                                              sem("fq_tmp"), sem("fq_done"))
        fqT_psum, fqT_done, ff2_psum, f2_done, ss2, rs2, o2_done, res_done, x1b_done = (
            sem("fqT_psum"), sem("fqT_done"), sem("ff2_psum"), sem("f2_done"), sem("ss2"), sem("rs2"), sem("o2_done"), sem("res_done"),
            sem("x1b_done"))
        tq = banks[1][:, 0:KD * P // 2].bitcast(BF16)
        tf = banks[6][:].bitcast(BF16)

        LAG = 3
        STEPS = NT + LAG

        def steps(eng, step):
            with eng.Fori(LAG, NT) as s:
                step(s, None)
            for s in range(NT, STEPS):
                step(s, s)

        def tile(s, at, lag):
            return s - lag if at is None or 0 <= at - lag < NT else None

        def after(eng, semaphore, value, at):
            if at is None or value > 0:
                eng.wait_ge(semaphore, value)

        with nc.Block() as block:
            @block.sync
            def _(sp):
                def load(n, name):
                    k = a[name].shape[1] // CHUNKS
                    c0 = n % CHUNKS
                    sp.dma_start(pieces[n][0].rearrange("p (k n) -> p k n", k=k), a[name][:, c0 * k:(c0 + 1) * k]).then_inc(w_loaded[n], 16)
                for hf in range(2):
                    sp.dma_start(wo_half[hf], a["w_out"][:, hf * (GI // 2):(hf + 1) * (GI // 2)]).then_inc(wo_loaded[hf], 16)
                for n in range(CHUNKS):
                    if n == CHUNKS - 1:
                        sp.wait_ge(wo_cut, 4)
                    load(n, "w1")
                def spread(dst, name):
                    sp.dma_start(dst[:], a[name].to_broadcast([P, a[name].shape[1]])).then_inc(rows_loaded, 16)
                spread(n1, "n1")
                spread(b1, "b1")
                for n in range(CHUNKS):
                    sp.wait_ge(w_top, n + 1)
                    load(CHUNKS + n, "w2")
                sp.wait_ge(rows_loaded, 32)
                spread(b2, "b2")
                spread(n2, "n2")
                sp.wait_ge(rows_loaded, 64)

            @block.gpsimd
            def _(pool):
                pool.memset(round_c[:, 0:1], ROUND).then_inc(round_set, 1)
                pool.memset(round_c[:, 1:2], -ROUND).then_inc(round_set, 1)

                def rms(i, k, sums, done):
                    hold(pool, sums, i + 1, passed)
                    pool.tensor_scalar(rs[:, k:k + 1], ss[:, k:k + 1], 1.0 / D, RMS_EPS, ALU.mult, ALU.add).then_inc(done, 1)
                    pool.wait_ge(done, 2 * i + 1)
                    pool.tensor_tensor(rs[:, k:k + 1], rs[:, k:k + 1], c["minus_half"][:, 0:1], ALU.pow).then_inc(done, 1)

                def step(s, at):
                    i, o = tile(s, at, 0), tile(s, at, 3)
                    if i is not None:
                        hold(pool, y_hi_done, i + 1, passed)
                        pool.tensor_tensor(y_lo[:], yT[:, :, bass.ds(i * P, P)], y_hi[:].bitcast(F32),
                                           ALU.subtract).then_inc(y_lo_done, 1)
                    if o is not None:
                        after(pool, f2_done, o, at)
                        pool.tensor_tensor(x1b[:], x1[:, o, :], b2[:], ALU.add).then_inc(x1b_done, 1)
                        rms(o, 1, ss2, rs2)
                        hold(pool, o2_done, o + 1, passed)
                        pool.tensor_tensor(xres[:, o, :], xres[:, o, :], o2[:], ALU.add).then_inc(res_done, 1)
                    if i is not None:
                        rms(i, 0, ss1, rs1)
                for s in range(LAG):
                    step(s, s)
                pool.wait_ge(w_top, 2 * CHUNKS)
                pool.wait_ge(rows_loaded, 64)
                steps(pool, step)

            @block.scalar
            def _(act):
                def cut_out(hf):
                    act.wait_ge(wo_loaded[hf], 16)
                    act.copy(wo_hi[:, hf * (GI // 2):(hf + 1) * (GI // 2)], wo_half[hf]).then_inc(wo_cut, 1)

                def add_up(n):
                    act.wait_ge(w_loaded[n], 16)
                    act.activation(pieces[n][1], pieces[n][0], ACT.Abs, accum_out=part[:, n:n + 1]).then_inc(sum_act, 1)

                def shift(n):
                    w, _, m = pieces[n]
                    act.wait_ge(g_done, 3 * (m + 1))
                    act.activation(w, w, ACT.Identity, bias=round_c[:, 0:1], scale=g_inv[:, m:m + 1]).then_inc(w_shifted, 1)

                def cut_y(i, at):
                    after(act, out_psum, i, at)
                    act.copy(y_hi[:], yT[:, :, bass.ds(i * P, P)]).then_inc(y_hi_done, 1)

                def step(s, at):
                    i, q, f, o = (tile(s, at, lag) for lag in range(4))
                    if i is not None and at not in (0, 1):
                        cut_y(i, at)
                    for hf in range(2):
                        if f is not None:
                            h = slice(hf * (FF // 2), (hf + 1) * (FF // 2))
                            act.wait_ge(f1_done, 4 * f + 2 * hf + 2)
                            act.activation(f1[:, h], f1[:, h], ACT.Gelu_apprx_tanh).then_inc(gelu_done, 1)
                        if o is not None:
                            act.wait_ge(fqT_psum, 2 * o + hf + 1)
                            act.copy(fqT[:, hf * (KF // 2):(hf + 1) * (KF // 2)].rearrange("p k n -> p (k n)"),
                                     tf).then_inc(fqT_done, 1)
                    if at == 2:
                        add_up(ACT_SUMS[0])
                        add_up(ACT_SUMS[1])
                    if q is not None:
                        act.wait_ge(qxT_psum, q + 1)
                        act.copy(qxT[:].rearrange("p k n -> p (k n)"), tq).then_inc(qxT_done, 1)
                    if o is not None:
                        act.wait_ge(f2_done, o + 1)
                        act.activation(sq[:], f2[:], ACT.Square, accum_out=ss[:, 1:2]).then_inc(ss2, 1)
                    if f is not None:
                        act.wait_ge(fq_tmp, 2 * f + 2)
                        act.activation(fq[:], f1[:], ACT.Identity, bias=round_c[:, 1:2]).then_inc(fq_done, 1)
                    if i is not None:
                        act.wait_ge(xr_done, i + 1)
                        act.activation(sq[:], xr[:], ACT.Square, accum_out=ss[:, 0:1]).then_inc(ss1, 1)
                cut_y(0, 0)
                cut_out(0)
                cut_out(1)
                step(0, 0)
                cut_y(1, 1)
                act.wait_ge(round_set, 2)
                for n in range(CHUNKS):
                    shift(n)
                step(1, 1)
                step(2, 2)
                for n in range(CHUNKS, 2 * CHUNKS):
                    shift(n)
                act.wait_ge(w_top, 2 * CHUNKS)
                steps(act, step)

            @block.vector
            def _(dve):
                def cut_out(hf):
                    s = slice(hf * (GI // 2), (hf + 1) * (GI // 2))
                    dve.wait_ge(wo_cut, 2 * hf + 1)
                    dve.tensor_tensor(wo_lo[:, s], wo_half[hf], wo_hi[:, s].bitcast(F32), ALU.subtract).then_inc(wo_cut, 1)

                def add_up(n):
                    dve.wait_ge(w_loaded[n], 16)
                    dve.tensor_reduce(part[:, n:n + 1], pieces[n][0], AX.X, ALU.add,
                                      apply_absolute_value=True).then_inc(sum_dve, 1)

                def mean(m):
                    at = slice(m, m + 1)
                    dve.wait_ge(total_psum, m + 1)
                    dve.tensor_scalar(g[:, at], banks[7][:, at], 1.0 / (FF * D), 1e-5, ALU.mult, ALU.max).then_inc(g_done, 1)
                    dve.wait_ge(g_done, 3 * m + 1)
                    dve.reciprocal(g_inv[:, at], g[:, at]).then_inc(g_done, 1)
                    dve.tensor_scalar(g_127[:, at], g[:, at], 1.0 / 127.0, None, ALU.mult).then_inc(g_done, 1)

                def quantise_w(m):
                    def bottom(n):
                        dve.wait_ge(w_top, n + 1)
                        dve.tensor_scalar(pieces[n][1], pieces[n][1], -1.0, None, ALU.max).then_inc(w_quantised, 1)
                    for n in range(m * CHUNKS, (m + 1) * CHUNKS):
                        dve.wait_ge(w_shifted, n + 1)
                        dve.tensor_scalar(pieces[n][1], pieces[n][0], -ROUND, 1.0, ALU.add, ALU.min).then_inc(w_top, 1)
                        if n > m * CHUNKS:
                            bottom(n - 1)
                    bottom((m + 1) * CHUNKS - 1)

                def quantise_x(q):
                    dve.wait_ge(rs1, 2 * q + 2)
                    dve.scalar_tensor_tensor(x1[:, q, :], xr[:], rs[:, 0:1], n1[:], ALU.mult, ALU.mult).then_inc(x1_done, 1)
                    hold(dve, x1_done, q + 1, passed)
                    dve.tensor_reduce(am[:, 0:1], x1[:, q, :], AX.X, ALU.max, apply_absolute_value=True).then_inc(am1, 1)
                    dve.wait_ge(am1, 4 * q + 1)
                    dve.tensor_scalar(am[:, 0:1], am[:, 0:1], 1e-5, None, ALU.max).then_inc(am1, 1)
                    dve.wait_ge(am1, 4 * q + 2)
                    dve.reciprocal(quant[:, 0:1], am[:, 0:1]).then_inc(am1, 1)
                    dve.tensor_scalar(unscale[:, q, 0:1], am[:, 0:1], g_127[:, 0:1], None, ALU.mult).then_inc(am1, 1)
                    dve.wait_ge(am1, 4 * q + 4)
                    dve.tensor_scalar(quant[:, 0:1], quant[:, 0:1], 127.0, None, ALU.mult).then_inc(qt1, 1)
                    dve.wait_ge(qt1, 2 * q + 1)
                    dve.tensor_scalar(qt[:], x1[:, q, :], quant[:, 0:1], ROUND, ALU.mult, ALU.add).then_inc(qt1, 1)
                    dve.wait_ge(qt1, 2 * q + 2)
                    dve.tensor_scalar(qx[:], qt[:], -ROUND, None, ALU.add).then_inc(qx_done, 1)

                def first_half(f):
                    for n in range(4):
                        dve.wait_ge(ff1_psum, 4 * f + n + 1)
                        s = slice(n * 512, (n + 1) * 512)
                        dve.scalar_tensor_tensor(f1[:, s], banks[2 + n][:], unscale[:, f, 0:1], b1[:, s], ALU.mult,
                                                 ALU.add).then_inc(f1_done, 1)

                def scales_f(f):
                    dve.wait_ge(gelu_done, 2 * f + 2)
                    dve.tensor_reduce(am[:, 1:2], f1[:], AX.X, ALU.max, apply_absolute_value=True).then_inc(am2, 1)
                    dve.wait_ge(am2, 3 * f + 1)
                    dve.tensor_scalar(unscale[:, f, 1:2], am[:, 1:2], 1e-5, None, ALU.max).then_inc(am2, 1)
                    hold(dve, am2, 3 * f + 2, passed)
                    dve.reciprocal(quant[:, 1:2], unscale[:, f, 1:2]).then_inc(am2, 1)
                    dve.wait_ge(am2, 3 * f + 3)
                    dve.tensor_scalar(quant[:, 1:2], quant[:, 1:2], 127.0, None, ALU.mult).then_inc(fq_tmp, 1)

                def quantise_f(f):
                    dve.wait_ge(fq_tmp, 2 * f + 1)
                    dve.tensor_scalar(f1[:], f1[:], quant[:, 1:2], ROUND, ALU.mult, ALU.add).then_inc(fq_tmp, 1)

                def second_half(o):
                    dve.tensor_scalar(scale2[:], unscale[:, o, 1:2], g_127[:, 1:2], None, ALU.mult).then_inc(scale2_done, 1)
                    dve.wait_ge(scale2_done, o + 1)
                    dve.wait_ge(ff2_psum, o + 1)
                    dve.wait_ge(x1b_done, o + 1)
                    dve.scalar_tensor_tensor(f2[:], banks[7][:], scale2[:], x1b[:], ALU.mult, ALU.add).then_inc(f2_done, 1)

                def result(o, at):
                    dve.wait_ge(rs2, 2 * o + 2)
                    after(dve, res_done, o, at)
                    dve.scalar_tensor_tensor(o2[:], f2[:], rs[:, 1:2], n2[:], ALU.mult, ALU.mult).then_inc(o2_done, 1)

                def step(s, at):
                    i, q, f, o = (tile(s, at, lag) for lag in range(4))
                    if f is not None:
                        after(dve, fq_done, f, at)
                        first_half(f)
                    if q is not None and at != 1:
                        quantise_x(q)
                    if i is not None:
                        dve.tensor_scalar(xm[:], xres[:, i, :], ln_mv[:, i, 0:1], ln_rstd[:, bass.ds(i, 1)], ALU.subtract,
                                          ALU.mult).then_inc(xm_done, 1)
                    if at == 2:
                        add_up(5)
                        add_up(7)
                    if f is not None:
                        scales_f(f)
                    if o is not None:
                        second_half(o)
                    if f is not None:
                        quantise_f(f)
                    if o is not None:
                        result(o, at)
                    if i is not None:
                        dve.wait_ge(xm_done, i + 1)
                        dve.wait_ge(out_psum, i + 1)
                        dve.tensor_tensor(xr[:], xm[:], banks[0][:], ALU.add).then_inc(xr_done, 1)
                cut_out(0)
                cut_out(1)
                add_up(0)
                add_up(1)
                add_up(2)
                step(0, 0)
                add_up(3)
                mean(0)
                dve.wait_ge(g_done, 3)
                dve.wait_ge(rows_loaded, 32)
                quantise_x(0)
                quantise_w(0)
                step(1, 1)
                step(2, 2)
                mean(1)
                dve.wait_ge(g_done, 6)
                quantise_w(1)
                dve.wait_ge(rows_loaded, 64)
                steps(dve, step)

            @block.tensor
            def _(pe):
                def total(m):
                    for n in range(m * CHUNKS, (m + 1) * CHUNKS):
                        if n in ACT_SUMS:
                            pe.wait_ge(sum_act, ACT_SUMS.index(n) + 1)
                        else:
                            pe.wait_ge(sum_dve, n + 1 - len([x for x in ACT_SUMS if x < n]))
                        last = pe.matmul(banks[7][:, m:m + 1], c["ones"][:], part[:, n:n + 1], start=(n % CHUNKS == 0),
                                         stop=(n % CHUNKS == CHUNKS - 1))
                    last.then_inc(total_psum, 1)

                def step(s, at):
                    i, q, f, o = (tile(s, at, lag) for lag in range(4))
                    if f is not None:
                        pe.wait_ge(qxT_done, f + 1)
                        after(pe, f1_done, 4 * f, at)
                        for n in range(4):
                            for k in range(KD):
                                last = pe.matmul(banks[2 + n][:], qxT[:, k], w1q[:, k, n * 512:(n + 1) * 512],
                                                 start=(k == 0), stop=(k == KD - 1))
                            last.then_inc(ff1_psum, 1)
                    if o is not None:
                        pe.wait_ge(fq_done, o + 1)
                        for hf in range(2):
                            after(pe, fqT_done, 2 * o + hf, at)
                            for k in range(KF // 2):
                                kk = hf * (KF // 2) + k
                                last = pe.transpose(tf[:, k * P:(k + 1) * P], fq[:, kk * P:(kk + 1) * P], c["ident_b"][:])
                            last.then_inc(fqT_psum, 1)
                        after(pe, f2_done, o, at)
                        for k in range(KF):
                            if k % (KF // 2) == 0:
                                pe.wait_ge(fqT_done, 2 * o + k // (KF // 2) + 1)
                            last = pe.matmul(banks[7][:], fqT[:, k], w2q[:, k], start=(k == 0), stop=(k == KF - 1))
                        last.then_inc(ff2_psum, 1)
                    if q is not None:
                        pe.wait_ge(qx_done, q + 1)
                        after(pe, qxT_done, q, at)
                        for k in range(KD):
                            last = pe.transpose(tq[:, k * P:(k + 1) * P], qx[:, k * P:(k + 1) * P], c["ident_b"][:])
                        last.then_inc(qxT_psum, 1)
                    if i is not None:
                        pe.wait_ge(y_lo_done, i + 1)
                        after(pe, xr_done, i, at)
                        for k in range(GI):
                            last = mm3(pe, banks[0][:], y_hi[:, k], y_lo[:, k], wo_hi[:, k], wo_lo[:, k], k == 0, k == GI - 1)
                        last.then_inc(out_psum, 1)
                pe.wait_ge(wo_cut, 4)
                step(0, 0)
                total(0)
                step(1, 1)
                pe.wait_ge(w_quantised, CHUNKS)
                step(2, 2)
                total(1)
                pe.wait_ge(w_quantised, 2 * CHUNKS)
                steps(pe, step)


def experts(nc, sem, c, xres, banks, a, out):
    KI = EI // P
    PAIRS = EALL // 2
    UNITS = EALL * BATCH
    outer = ExitStack()
    with outer:
        def sb(name, shape, dt):
            return outer.enter_context(nc.sbuf_tensor(name, shape, dt))
        gate_w = sb("gate_w", [P, KD, E], F32)
        gate_hi = sb("gate_hi", [P, KD, E], F32R)
        gate_lo = sb("gate_lo", [P, KD, E], F32R)
        gate_b = sb("gate_b", [P, E], F32)
        before4 = sb("before4", [P, 4, 4], F32)
        before16 = sb("before16", [P, E, E], F32)
        stats = sb("e_stats", [P, NT, 6], F32)
        mv = sb("e_mv", [P, NT, 2], F32)
        rstd = sb("e_rstd", [P, NT], F32)
        xf = sb("xf", [P, NT, D], F32)
        xT_hi = sb("e_xT_hi", [P, KD, BATCH * SEQ], F32R)
        xT_lo = sb("e_xT_lo", [P, KD, BATCH * SEQ], F32R)
        up_stage = sb("up_stage", [P, 2, KD, 2 * EI], F32)
        up_hi = sb("up_hi", [P, 2, KD, 2 * EI], F32R)
        up_lo = sb("up_lo", [P, 2, KD, 2 * EI], F32R)
        dn_stage = sb("dn_stage", [P, 2, KI, D], F32)
        dn_hi = sb("dn_hi", [P, 2, KI, D], F32R)
        dn_lo = sb("dn_lo", [P, 2, KI, D], F32R)
        th = sb("e_th", [P, KI, SEQ], F32)
        ga = sb("ga", [P, KI, SEQ], F32)
        ac = sb("ac", [P, BATCH, KI, SEQ], F32)
        ac_hi = sb("ac_hi", [P, BATCH, KI, SEQ], F32R)
        ac_lo = sb("ac_lo", [P, BATCH, KI, SEQ], F32R)
        lgT = sb("lgT", [E, BATCH * SEQ], F32)
        prob = sb("prob", [P, NT, E], F32)
        sfc = sb("sfc", [P, NT, E], F32)
        pairs = sb("pairs", [P, 4, NT * 4], F32)
        grp = sb("grp", [P, NT, 4], F32)
        cmp = sb("cmp", [P, NT * E, E], F32)
        eqs = sb("eqs", [P, NT * E, E], F32)
        rank = sb("rank", [P, NT * E], F32)
        cw = sb("cw", [P, NT, EALL], F32)
        tot = sb("tot", [P, NT], F32)

        gate_loaded, gate_cut, masks = sem("gate_loaded"), sem("gate_cut"), sem("masks")
        up_loaded = [sem("up_loaded0"), sem("up_loaded1")]
        dn_loaded = [sem("dn_loaded0"), sem("dn_loaded1")]
        up_hi_done, up_lo_done, dn_hi_done, dn_lo_done = sem("up_hi_done"), sem("up_lo_done"), sem("dn_hi_done"), sem("dn_lo_done")
        stats_done, mv_done, rstd_done, xf_done, xres_done = (sem("e_stats_done"), sem("e_mv_done"), sem("e_rstd_done"),
                                                              sem("xf_done"), sem("xres_done"))
        xT_psum, xT_hi_done, xT_lo_done = sem("e_xT_psum"), sem("e_xT_hi_done"), sem("e_xT_lo_done")
        logit_psum, lgT_done, lg_psum, elogit, route, cw_shared = (
            sem("logit_psum"), sem("lgT_done"), sem("lg_psum"), sem("elogit"), sem("route"), sem("cw_shared"))
        up_psum, tanh_done, ga_done, gated = sem("up_psum"), sem("e_tanh_done"), sem("ga_done"), sem("gated")
        ac_hi_done, ac_lo_done, dn_psum, stored = sem("ac_hi_done"), sem("ac_lo_done"), sem("dn_psum"), sem("stored")
        dn_last = sem("dn_last")
        y_added = sem("e_y_added")
        ROUTE = 28

        with nc.Block() as block:
            @block.sync
            def _(sp):
                def load(e, r, first):
                    if not first:
                        sp.wait_ge(up_lo_done, e - 1)
                    sp.dma_start(up_stage[:, r], a["up"][e]).then_inc(up_loaded[r], 16)
                    if not first:
                        sp.wait_ge(dn_lo_done, e - 1)
                    sp.dma_start(dn_stage[:, r], a["down"][e]).then_inc(dn_loaded[r], 16)
                sp.dma_start(gate_w[:], a["gate"]).then_inc(gate_loaded, 16)
                sp.dma_start(gate_b[:], a["gate_b"].to_broadcast([P, E])).then_inc(gate_loaded, 16)
                load(0, 0, True)
                load(1, 1, True)
                with sp.Fori(1, PAIRS) as j:
                    for r in range(2):
                        load(2 * j + r, r, False)
                for b in range(BATCH):
                    rows = out[b].rearrange("(t p) d -> p t d", p=P)
                    for t in range(0, TT, 2):
                        sp.wait_ge(y_added, (UNITS - BATCH + b) * TT + t + 3)
                        sp.dma_start(rows[:, t:t + 2], xres[:, b * TT + t:b * TT + t + 2]).then_inc(stored, 16)
                sp.wait_ge(stored, 16 * NT // 2)

            @block.gpsimd
            def _(pool):
                pool.memset(before4[:], 1.0).then_inc(masks, 1)
                pool.memset(before16[:], 1.0).then_inc(masks, 1)
                pool.memset(cw[:, :, E:EALL], 0.5).then_inc(cw_shared, 1)
                for b in range(BATCH):
                    s = slice(b * TT, (b + 1) * TT)
                    pool.wait_ge(mv_done, (b + 1) * TT)
                    pool.tensor_scalar(rstd[:, s], mv[:, s, 1], LN_EPS, None, ALU.add).then_inc(rstd_done, 1)
                    pool.wait_ge(rstd_done, 2 * b + 1)
                    pool.tensor_tensor(rstd[:, s], rstd[:, s], c["minus_half"][:, 0:TT], ALU.pow).then_inc(rstd_done, 1)

                def cut_up(e, r):
                    pool.wait_ge(up_hi_done, e + 1)
                    pool.tensor_tensor(up_lo[:, r], up_stage[:, r], up_hi[:, r].bitcast(F32), ALU.subtract).then_inc(up_lo_done, 1)

                def cut_down(e, r):
                    pool.wait_ge(dn_hi_done, e + 1)
                    pool.tensor_tensor(dn_lo[:, r], dn_stage[:, r], dn_hi[:, r].bitcast(F32), ALU.subtract).then_inc(dn_lo_done, 1)

                def cut_ac(m, b):
                    for i in range(KI):
                        pool.wait_ge(ac_hi_done, m * KI + i + 1)
                        pool.tensor_tensor(ac_lo[:, b, i], ac[:, b, i], ac_hi[:, b, i].bitcast(F32), ALU.subtract).then_inc(ac_lo_done, 1)
                pool.wait_ge(gate_cut, 1)
                pool.tensor_tensor(gate_lo[:], gate_w[:], gate_hi[:].bitcast(F32), ALU.subtract).then_inc(gate_cut, 1)
                cut_up(0, 0)
                pool.wait_ge(masks, 2)
                pool.affine_select(out=before4[:], in_=before4[:], compare_op=ALU.is_gt, fill=0.0, base=0,
                                   pattern=[[1, 4], [-1, 4]], channel_multiplier=0).then_inc(masks, 1)
                pool.affine_select(out=before16[:], in_=before16[:], compare_op=ALU.is_gt, fill=0.0, base=0,
                                   pattern=[[1, E], [-1, E]], channel_multiplier=0).then_inc(masks, 1)
                cut_down(0, 0)
                cut_ac(0, 0)
                cut_up(1, 1)
                cut_down(1, 1)

                def pair(j, more):
                    cut_ac(4 * j + 1, 1)
                    cut_ac(4 * j + 2, 0)
                    if more:
                        cut_up(2 * j + 2, 0)
                    cut_ac(4 * j + 3, 1)
                    if more:
                        cut_down(2 * j + 2, 0)
                        cut_up(2 * j + 3, 1)
                        cut_ac(4 * j + 4, 0)
                        cut_down(2 * j + 3, 1)
                with pool.Fori(0, PAIRS - 1) as j:
                    pair(j, True)
                pair(PAIRS - 1, False)

            @block.scalar
            def _(act):
                def cut_up(e, r, use, first):
                    act.wait_ge(up_loaded[r], (use + 1) * 16)
                    if not first:
                        act.wait_ge(up_psum, (2 * e - 2) * KI)
                    act.copy(up_hi[:, r], up_stage[:, r]).then_inc(up_hi_done, 1)

                def cut_down(e, r, use, first):
                    act.wait_ge(dn_loaded[r], (use + 1) * 16)
                    if not first:
                        act.wait_ge(dn_psum, 2 * e - 2)
                    act.copy(dn_hi[:, r], dn_stage[:, r]).then_inc(dn_hi_done, 1)

                def unit(m, b):
                    for i in range(KI):
                        act.wait_ge(up_psum, m * KI + i + 1)
                        act.activation(th[:, i], banks[2 * i][:], ACT.Tanh, scale=0.5).then_inc(tanh_done, 1)
                    for i in range(KI):
                        act.wait_ge(gated, m * KI + i + 1)
                        act.copy(ac_hi[:, b, i], ac[:, b, i]).then_inc(ac_hi_done, 1)
                act.wait_ge(gate_loaded, 32)
                act.copy(gate_hi[:], gate_w[:]).then_inc(gate_cut, 1)
                cut_up(0, 0, 0, True)
                for t in range(NT):
                    act.wait_ge(xT_psum, t + 1)
                    act.copy(xT_hi[:, :, t * P:(t + 1) * P],
                             banks[4 + t % 4][:].rearrange("p (k n) -> p k n", k=KD)).then_inc(xT_hi_done, 1)
                for b in range(BATCH):
                    act.wait_ge(logit_psum, b + 1)
                    act.copy(lgT[:, b * SEQ:(b + 1) * SEQ], banks[4 + b][0:E, :]).then_inc(lgT_done, 1)
                act.wait_ge(lg_psum, 1)
                act.activation(prob[:].rearrange("p t e -> p (t e)"), banks[6][:, 0:NT * E], ACT.Exp, scale=-1.0).then_inc(elogit, 1)
                cut_down(0, 0, 0, True)
                unit(0, 0)
                cut_up(1, 1, 0, True)
                cut_down(1, 1, 0, True)

                def pair(j, more):
                    unit(4 * j + 1, 1)
                    unit(4 * j + 2, 0)
                    if more:
                        cut_up(2 * j + 2, 0, j + 1, False)
                    unit(4 * j + 3, 1)
                    if more:
                        cut_down(2 * j + 2, 0, j + 1, False)
                        cut_up(2 * j + 3, 1, j + 1, False)
                        unit(4 * j + 4, 0)
                        cut_down(2 * j + 3, 1, j + 1, False)
                with act.Fori(0, PAIRS - 1) as j:
                    pair(j, True)
                pair(PAIRS - 1, False)

            @block.vector
            def _(dve):
                dve.sem_inc(y_added, 1)
                for b in range(BATCH):
                    for t in range(b * TT, (b + 1) * TT):
                        dve.bn_stats(stats[:, t, :], xres[:, t, :]).then_inc(stats_done, 1)
                    for t in range(b * TT, (b + 1) * TT):
                        dve.wait_ge(stats_done, t + 1)
                        dve.bn_aggr(mv[:, t, :], stats[:, t, :]).then_inc(mv_done, 1)
                for t in range(NT):
                    dve.wait_ge(rstd_done, 2 * (t // TT + 1))
                    dve.tensor_scalar(xf[:, t, :], xres[:, t, :], mv[:, t, 0:1], rstd[:, t:t + 1],
                                      ALU.subtract, ALU.mult).then_inc(xf_done, 1)
                for t in range(NT):
                    dve.wait_ge(xT_hi_done, t + 1)
                    s = slice(t * P, (t + 1) * P)
                    dve.tensor_tensor(xT_lo[:, :, s], banks[4 + t % 4][:].rearrange("p (k n) -> p k n", k=KD),
                                      xT_hi[:, :, s].bitcast(F32), ALU.subtract).then_inc(xT_lo_done, 1)

                def unit(m, b):
                    for i in range(KI):
                        dve.wait_ge(tanh_done, m * KI + i + 1)
                        dve.scalar_tensor_tensor(ga[:, i], th[:, i], 1.0, banks[2 * i][:], ALU.add,
                                                 ALU.mult).then_inc(ga_done, 1)
                        dve.wait_ge(ga_done, m * KI + i + 1)
                        dve.tensor_tensor(ac[:, b, i], ga[:, i], banks[2 * i + 1][:], ALU.mult).then_inc(gated, 1)

                def add_y(m, e, b, last=False):
                    if not last:
                        dve.wait_ge(dn_psum, m + 1)
                    for t in range(TT):
                        if last:
                            dve.wait_ge(dn_last, t + 1)
                        x = xres[:, b * TT + t, :]
                        dve.scalar_tensor_tensor(x, banks[t if last else 4 + t][:], cw[:, b * TT + t, bass.ds(e, 1)], x, ALU.mult,
                                                 ALU.add).then_inc(y_added, 1)
                steps = [0]

                def step(instruction):
                    steps[0] += 1
                    instruction.then_inc(route, 1)
                    dve.wait_ge(route, steps[0])

                f = sfc[:].rearrange("p t (g e) -> p (t g) e", e=4)

                def ranks(v, n, before):
                    full = [P, NT, n, n]
                    other = v.unsqueeze(2).to_broadcast(full)
                    own = v.unsqueeze(3).to_broadcast(full)
                    gt = cmp[:, 0:NT * n, 0:n].rearrange("p (t x) y -> p t x y", t=NT)
                    eq = eqs[:, 0:NT * n, 0:n].rearrange("p (t x) y -> p t x y", t=NT)
                    step(dve.tensor_tensor(gt, other, own, ALU.is_gt))
                    step(dve.tensor_tensor(eq, other, own, ALU.is_equal))
                    step(dve.tensor_tensor(eq, eq, before.unsqueeze(1).to_broadcast(full), ALU.mult))
                    step(dve.tensor_tensor(gt, gt, eq, ALU.add))
                    step(dve.tensor_reduce(rank[:, 0:NT * n], cmp[:, 0:NT * n, 0:n], AX.X, ALU.add))

                def choose_groups():
                    dve.wait_ge(elogit, 1)
                    dve.wait_ge(masks, 4)
                    step(dve.tensor_scalar(prob[:], prob[:], 1.0, None, ALU.add))
                    step(dve.reciprocal(prob[:], prob[:]))
                    step(dve.tensor_tensor(sfc[:], prob[:], bc_mid(gate_b[:], NT), ALU.add))
                    step(dve.tensor_tensor(pairs[:, 0], f[:, :, 0], f[:, :, 1], ALU.max))
                    step(dve.tensor_tensor(pairs[:, 1], f[:, :, 2], f[:, :, 3], ALU.max))
                    step(dve.tensor_tensor(pairs[:, 2], f[:, :, 0], f[:, :, 1], ALU.add))
                    step(dve.tensor_tensor(pairs[:, 3], f[:, :, 2], f[:, :, 3], ALU.add))
                    step(dve.tensor_tensor(pairs[:, 0], pairs[:, 0], pairs[:, 1], ALU.add))
                    step(dve.tensor_tensor(pairs[:, 2], pairs[:, 2], pairs[:, 3], ALU.max))
                    step(dve.tensor_tensor(grp[:].rearrange("p t g -> p (t g)"), pairs[:, 0], pairs[:, 2], ALU.max))
                    ranks(grp[:], 4, before4[:])
                    step(dve.tensor_scalar(rank[:, 0:NT * 4], rank[:, 0:NT * 4], 2.0, BIG, ALU.is_lt, ALU.mult))
                    step(dve.tensor_scalar(rank[:, 0:NT * 4], rank[:, 0:NT * 4], -BIG, None, ALU.add))
                    step(dve.tensor_tensor(f, f, bc_free(rank[:, 0:NT * 4], 4), ALU.add))

                def weigh_experts():
                    r = rank[:].rearrange("p (t e) -> p t e", t=NT)
                    w = cw[:, :, 0:E]
                    step(dve.scalar_tensor_tensor(w, r, 4.0, prob[:], ALU.is_lt, ALU.mult))
                    step(dve.reduce_sum(tot[:], w, AX.X))
                    step(dve.tensor_scalar(tot[:], tot[:], 1e-20, None, ALU.add))
                    step(dve.reciprocal(tot[:], tot[:]))
                    step(dve.scalar_tensor_tensor(w, w, 1.25, bc_free(tot[:], E), ALU.mult, ALU.mult))
                    assert steps[0] == ROUTE, steps[0]
                    dve.wait_ge(cw_shared, 1)
                    dve.wait_ge(xf_done, NT)

                def pair(j, more, first=False):
                    unit(4 * j + 1, 1)
                    if first:
                        weigh_experts()
                        for t in range(NT):
                            dve.tensor_tensor(xres[:, t, :], xres[:, t, :], xf[:, t, :], ALU.add).then_inc(xres_done, 1)
                        dve.wait_ge(xres_done, NT)
                    add_y(4 * j, 2 * j, 0)
                    unit(4 * j + 2, 0)
                    add_y(4 * j + 1, 2 * j, 1)
                    unit(4 * j + 3, 1)
                    add_y(4 * j + 2, 2 * j + 1, 0)
                    if more:
                        unit(4 * j + 4, 0)
                    add_y(4 * j + 3, 2 * j + 1, 1, not more)
                choose_groups()
                unit(0, 0)
                ranks(sfc[:], E, before16[:])
                pair(0, True, True)
                with dve.Fori(1, PAIRS - 1) as j:
                    pair(j, True)
                pair(PAIRS - 1, False)

            @block.tensor
            def _(pe):
                for t in range(NT):
                    pe.wait_ge(xf_done, t + 1)
                    if t >= 4:
                        pe.wait_ge(xT_lo_done, t - 3)
                    for k in range(KD):
                        last = pe.transpose(banks[4 + t % 4][:, k * P:(k + 1) * P], xf[:, t, k * P:(k + 1) * P], c["ident"][:])
                    last.then_inc(xT_psum, 1)

                def up(m, b, r, e):
                    pe.wait_ge(up_lo_done, e + 1)
                    x = slice(b * SEQ, (b + 1) * SEQ)
                    for i in range(KI):
                        if not (isinstance(m, int) and m == 0):
                            pe.wait_ge(gated, (m - 1) * KI + i + 1)
                        for half in range(2):
                            s = slice(half * EI + i * P, half * EI + (i + 1) * P)
                            for k in range(KD):
                                last = mm3(pe, banks[2 * i + half][:], up_hi[:, r, k, s], up_lo[:, r, k, s], xT_hi[:, k, x],
                                           xT_lo[:, k, x], k == 0, k == KD - 1)
                        last.then_inc(up_psum, 1)

                def down(m, b, r, e, last_unit=False):
                    pe.wait_ge(ac_lo_done, (m + 1) * KI)
                    pe.wait_ge(dn_lo_done, e + 1)
                    if not last_unit:
                        pe.wait_ge(y_added, m * TT + 1)
                    for t in range(TT):
                        s = slice(t * P, (t + 1) * P)
                        if last_unit and t > 0:
                            last.then_inc(dn_last, 1)
                        for i in range(KI):
                            last = mm3(pe, banks[t if last_unit else 4 + t][:], ac_hi[:, b, i, s], ac_lo[:, b, i, s], dn_hi[:, r, i],
                                       dn_lo[:, r, i], i == 0, i == KI - 1)
                    last.then_inc(dn_last if last_unit else dn_psum, 1)
                pe.wait_ge(xT_lo_done, NT)
                pe.wait_ge(gate_cut, 2)
                for b in range(BATCH):
                    x = slice(b * SEQ, (b + 1) * SEQ)
                    for k in range(KD):
                        last = mm3(pe, banks[4 + b][0:E, :], gate_hi[:, k], gate_lo[:, k], xT_hi[:, k, x], xT_lo[:, k, x],
                                   k == 0, k == KD - 1)
                    last.then_inc(logit_psum, 1)
                for t in range(NT):
                    pe.wait_ge(lgT_done, t // TT + 1)
                    last = pe.transpose(banks[6][:, t * E:(t + 1) * E], lgT[:, t * P:(t + 1) * P], c["ident"][0:E, 0:E])
                last.then_inc(lg_psum, 1)
                up(0, 0, 0, 0)

                def pair(j, more):
                    up(4 * j + 1, 1, 0, 2 * j)
                    down(4 * j, 0, 0, 2 * j)
                    up(4 * j + 2, 0, 1, 2 * j + 1)
                    down(4 * j + 1, 1, 0, 2 * j)
                    up(4 * j + 3, 1, 1, 2 * j + 1)
                    down(4 * j + 2, 0, 1, 2 * j + 1)
                    if more:
                        up(4 * j + 4, 0, 0, 2 * j + 2)
                    down(4 * j + 3, 1, 1, 2 * j + 1, not more)
                pe.wait_ge(elogit, 1)
                with pe.Fori(0, PAIRS - 1) as j:
                    pair(j, True)
                pair(PAIRS - 1, False)


def stage_semaphores(nc, stage):
    taken = []

    def sem(name):
        taken.append(nc.alloc_semaphore(name=name))
        return taken[-1]
    stage(sem)
    nc.clear_and_free_semaphores(taken)
    nc.all_engine_barrier()


def build(nc, a, out):
    with ExitStack() as ctx:
        def sb(name, shape, dt):
            return ctx.enter_context(nc.sbuf_tensor(name, shape, dt))
        xres = sb("xres", [P, NT, D], F32)
        banks = [ctx.enter_context(nc.psum_tensor(f"bank{i}", [P, 512], F32)) for i in range(8)]
        c = {}
        stage_semaphores(nc, lambda sem: constants(nc, sb, sem, c))
        stage_semaphores(nc, lambda sem: attention(nc, sem, c, xres, banks, a))
        with ExitStack() as mid:
            ln_mv = mid.enter_context(nc.sbuf_tensor("ln_mv", [P, NT, 2], F32))
            ln_rstd = mid.enter_context(nc.sbuf_tensor("ln_rstd", [P, NT], F32))
            yT = mid.enter_context(nc.sbuf_tensor("yT", [P, GI, BATCH * SEQ], F32))
            stage_semaphores(nc, lambda sem: mamba_scan(nc, sem, c, xres, banks, a, ln_mv, ln_rstd, yT))
            stage_semaphores(nc, lambda sem: feed_forward(nc, sem, c, xres, banks, a, ln_mv, ln_rstd, yT))
        stage_semaphores(nc, lambda sem: experts(nc, sem, c, xres, banks, a, out))


def layout(np, i):
    T = np.transpose
    wg = np.concatenate([i["L0_ffn_Wg"], np.reshape(i["L0_ffn_Ws_g"], (2, EI, D))])
    wu = np.concatenate([i["L0_ffn_Wu"], np.reshape(i["L0_ffn_Ws_u"], (2, EI, D))])
    wd = np.concatenate([T(i["L0_ffn_Wd"], (0, 2, 1)), np.reshape(T(i["L0_ffn_Ws_d"]), (2, EI, D))])
    up = np.concatenate([wg, wu], axis=1)
    return {
        "x": i["x"],
        "ctxT": T(i["ctx_1024"][:, :SEQ], (0, 2, 1)),
        "wq": T(i["L0_xattn_Wq"]), "wk": T(i["L0_xattn_Wk"]), "wv": T(i["L0_xattn_Wv"]), "wo": T(i["L0_xattn_Wo"]),
        "w_in": T(np.reshape(i["L0_attn_w_in"], (2 * GI, P, KD, P)), (0, 3, 2, 1)),
        "conv_w": T(np.reshape(i["L0_attn_conv_w"], (GI, P, 4)), (1, 0, 2)),
        "conv_b": T(np.reshape(i["L0_attn_conv_b"], (GI, P))),
        "w_xproj": T(np.reshape(i["L0_attn_w_xproj"], (DR + 2 * NS, GI, P)), (2, 1, 0)),
        "w_dt": T(i["L0_attn_w_dt"]),
        "b_dt": T(np.reshape(i["L0_attn_b_dt"], (GI, P))),
        "A_log": T(np.reshape(i["L0_attn_A_log"], (GI, P, NS)), (1, 0, 2)),
        "Dp": T(np.reshape(i["L0_attn_Dp"], (GI, P))),
        "w_out": T(np.reshape(i["L0_attn_w_out"], (D, GI, P)), (2, 1, 0)),
        "n1": np.reshape(i["L0_attn_norm1_w"], (1, D)), "n2": np.reshape(i["L0_attn_norm2_w"], (1, D)),
        "w1": T(np.reshape(i["L0_attn_ffn_w1"], (FF, KD, P)), (2, 1, 0)),
        "b1": np.reshape(i["L0_attn_ffn_b1"], (1, FF)),
        "w2": T(np.reshape(i["L0_attn_ffn_w2"], (D, FF // P, P)), (2, 1, 0)),
        "b2": np.reshape(i["L0_attn_ffn_b2"], (1, D)),
        "gate": T(np.reshape(i["L0_ffn_gate_w"], (E, KD, P)), (2, 1, 0)),
        "gate_b": np.reshape(i["L0_ffn_gate_bias"], (1, E)),
        "up": T(np.reshape(up, (EALL, 2 * EI, KD, P)), (0, 3, 2, 1)),
        "down": T(np.reshape(wd, (EALL, EI // P, P, D)), (0, 2, 1, 3)),
    }


def kernel(**inputs):
    import numpy as np
    import concourse.bacc as bacc
    from concourse.bass_utils import run_bass_kernel_spmd

    nc = bacc.Bacc("TRN2", target_bir_lowering=False, num_devices=1)
    arrays, aps = {}, {}
    for name, array in layout(np, inputs).items():
        array = np.ascontiguousarray(array)
        arrays[f"in_{name}"] = array
        aps[name] = nc.dram_tensor(f"in_{name}", array.shape, F32, kind="ExternalInput").ap()
    out = nc.dram_tensor("out_x", (BATCH, SEQ, D), F32, kind="ExternalOutput").ap()
    build(nc, aps, out)
    result = run_bass_kernel_spmd(nc, [arrays], core_ids=[0])
    return result.results[0]["out_x"]
```
